# Optimizing a Trainium2 kernel written in Bass

```python
import numpy as np
import jax
import jax.numpy as jnp

def _softmax(x, axis=-1):
    return jax.nn.softmax(x, axis=axis)

def _gelu(x):
    return jax.nn.gelu(x, approximate=True)

def _silu(x):
    return jax.nn.silu(x)

def _sigmoid(x):
    return jax.nn.sigmoid(x)

def _layernorm(x, axis=-1, eps=1e-05):
    m = jnp.mean(x, axis=axis, keepdims=True)
    v = jnp.var(x, axis=axis, keepdims=True)
    return (x - m) / jnp.sqrt(v + eps)

def _scatter_add(tgt, idx, src, axis=0):
    return tgt.at[idx].add(src)

def _segment_sum(src, seg, n):
    return jax.ops.segment_sum(src, seg, n)
kernel_name = 'mk_gnn_preln_d4_gnn_r64_cc0146'

def setup_inputs(seed: int=0):
    np.random.seed(seed)
    _w = jnp.asarray

    def _rec_inputs():
        import jax
        import jax.numpy as jnp
        _gk = jax.random.key(seed)
        x = -0.0001079 + 1 * jax.random.normal(jax.random.fold_in(_gk, 1), (100000, 64), jnp.float32)
        src = jax.random.randint(jax.random.fold_in(_gk, 2), (50000,), 0, 100000, jnp.int32)
        dst = jnp.minimum((100000 * jax.random.uniform(jax.random.fold_in(_gk, 3), (50000,)) ** 2.0).astype(jnp.int32), 99999)
        _o = jnp.argsort(dst, stable=True)
        src = src[_o]
        dst = dst[_o]
        edge_attr_32 = -8.62073e-06 + 0.999901 * jax.random.normal(jax.random.fold_in(_gk, 11), (50000, 32), jnp.float32)
        return (x, src, dst, edge_attr_32)
    x, src, dst, edge_attr_32 = _rec_inputs()

    def _L0_gnn_setup():
        import jax, jax.numpy as jnp
        import numpy as np
        NUM_NODES = 50000
        EMBED_DIM = 64
        NUM_EDGES = 1250000
        NUM_LAYERS = 3
        key = jax.random.key(seed)
        k1, k2 = jax.random.split(key)
        edge_index = jax.random.randint(k1, (2, NUM_EDGES), 0, NUM_NODES, dtype=jnp.int64) if jax.config.read('jax_enable_x64') else jax.random.randint(k1, (2, NUM_EDGES), 0, NUM_NODES, dtype=jnp.int32)
        embedding_weight = jax.random.normal(k2, (NUM_NODES, EMBED_DIM), dtype=jnp.float32)
        return {'edge_index': edge_index, 'embedding_weight': embedding_weight}
    _L0_gnn_all = _L0_gnn_setup()
    _L0_gnn_in = {k: v for k, v in _L0_gnn_all.items() if k in ()}
    del _L0_gnn_all

    def _L1_gnn_setup():
        import jax, jax.numpy as jnp
        import numpy as np
        N_NODES = 100000
        N_EDGES = 15625
        NODE_DIM = 64
        EDGE_DIM = 32
        EPS = 1e-05
        SLOPE = 0.1

        def _mlp2(v, W1, b1, W2, b2):
            h = jax.nn.leaky_relu(v @ W1 + b1, negative_slope=SLOPE)
            return h @ W2 + b2
        key = jax.random.key(seed)
        ks = jax.random.split(key, 8)
        s = 0.05
        return {'x': jax.random.normal(ks[0], (N_NODES, NODE_DIM), dtype=jnp.float32), 'edge_attr': jax.random.normal(ks[1], (N_EDGES, EDGE_DIM), dtype=jnp.float32), 'W1n': jax.random.normal(ks[2], (NODE_DIM, 2 * NODE_DIM), dtype=jnp.float32) * s, 'b1n': jnp.zeros((2 * NODE_DIM,), dtype=jnp.float32), 'W2n': jax.random.normal(ks[3], (2 * NODE_DIM, NODE_DIM), dtype=jnp.float32) * s, 'b2n': jnp.zeros((NODE_DIM,), dtype=jnp.float32), 'W1e': jax.random.normal(ks[4], (EDGE_DIM, NODE_DIM), dtype=jnp.float32) * s, 'b1e': jnp.zeros((NODE_DIM,), dtype=jnp.float32), 'W2e': jax.random.normal(ks[5], (NODE_DIM, NODE_DIM), dtype=jnp.float32) * s, 'b2e': jnp.zeros((NODE_DIM,), dtype=jnp.float32), 'res_w': jnp.ones((1,), dtype=jnp.float32), 'dp_scale': jnp.ones((1,), dtype=jnp.float32), 'gamma': jnp.ones((NODE_DIM,), dtype=jnp.float32), 'beta': jnp.zeros((NODE_DIM,), dtype=jnp.float32), 'edge_index': jax.random.randint(ks[6], (2, N_EDGES), 0, N_NODES, dtype=jnp.int64) if jax.config.jax_enable_x64 else jax.random.randint(ks[6], (2, N_EDGES), 0, N_NODES, dtype=jnp.int32)}
    _L1_gnn_all = _L1_gnn_setup()
    _L1_gnn_in = {k: v for k, v in _L1_gnn_all.items() if k in ('W1n', 'b1n', 'W2n', 'b2n', 'W1e', 'b1e', 'W2e', 'b2e', 'res_w', 'dp_scale', 'gamma', 'beta')}
    del _L1_gnn_all

    def _L2_gnn_setup():
        import jax, jax.numpy as jnp
        import numpy as np
        NUM_NODES = 100000
        EMBED_DIM = 64
        NUM_LAYERS = 3
        NUM_EDGES = 50000

        def _lightgcn_embedding(emb, edge_index):
            n = emb.shape[0]
            src, dst = (edge_index[0], edge_index[1])
            deg = jax.ops.segment_sum(jnp.ones(src.shape[0], dtype=emb.dtype), dst, num_segments=n)
            deg_inv_sqrt = jnp.where(deg > 0, jax.lax.rsqrt(jnp.maximum(deg, 1.0)), 0.0)
            w = deg_inv_sqrt[src] * deg_inv_sqrt[dst]
            x = emb
            out = emb
            for _ in range(NUM_LAYERS):
                x = jax.ops.segment_sum(w[:, None] * x[src], dst, num_segments=n)
                out = out + x
            return out / (NUM_LAYERS + 1)
        key = jax.random.key(seed)
        k_emb, k_edge = jax.random.split(key)
        emb = jax.random.normal(k_emb, (NUM_NODES, EMBED_DIM), dtype=jnp.float32) * 0.1
        edge_index = jax.random.randint(k_edge, (2, NUM_EDGES), 0, NUM_NODES, dtype=jnp.int64)
        return {'emb': emb, 'edge_index': edge_index}
    _L2_gnn_all = _L2_gnn_setup()
    _L2_gnn_in = {k: v for k, v in _L2_gnn_all.items() if k in ()}
    del _L2_gnn_all

    def _L3_gnn_setup():
        import jax, jax.numpy as jnp
        import numpy as np
        NUM_USERS = 100000
        NUM_MOVIES = 50000
        NUM_NODES = NUM_USERS + NUM_MOVIES
        EMB_DIM = 64
        N_LAYERS = 3
        N_EDGES = 62500
        key = jax.random.key(seed)
        k_e, k_w = jax.random.split(key)
        edge_index = jax.random.randint(k_e, (2, N_EDGES), 0, NUM_NODES, dtype=jnp.int64 if jax.config.jax_enable_x64 else jnp.int32)
        emb_weight = jax.random.normal(k_w, (NUM_NODES, EMB_DIM), dtype=jnp.float32)
        return {'edge_index': edge_index, 'emb_weight': emb_weight}
    _L3_gnn_all = _L3_gnn_setup()
    _L3_gnn_in = {k: v for k, v in _L3_gnn_all.items() if k in ()}
    del _L3_gnn_all
    return {'x': x, 'src': src, 'dst': dst, 'edge_attr_32': edge_attr_32, 'L1_gnn_W1n': _L1_gnn_in['W1n'], 'L1_gnn_b1n': _L1_gnn_in['b1n'], 'L1_gnn_W2n': _L1_gnn_in['W2n'], 'L1_gnn_b2n': _L1_gnn_in['b2n'], 'L1_gnn_W1e': _L1_gnn_in['W1e'], 'L1_gnn_b1e': _L1_gnn_in['b1e'], 'L1_gnn_W2e': _L1_gnn_in['W2e'], 'L1_gnn_b2e': _L1_gnn_in['b2e'], 'L1_gnn_res_w': _L1_gnn_in['res_w'], 'L1_gnn_dp_scale': _L1_gnn_in['dp_scale'], 'L1_gnn_gamma': _L1_gnn_in['gamma'], 'L1_gnn_beta': _L1_gnn_in['beta']}

def reference(x, src, dst, edge_attr_32, L1_gnn_W1n, L1_gnn_b1n, L1_gnn_W2n, L1_gnn_b2n, L1_gnn_W1e, L1_gnn_b1e, L1_gnn_W2e, L1_gnn_b2e, L1_gnn_res_w, L1_gnn_dp_scale, L1_gnn_gamma, L1_gnn_beta):
    import jax
    import jax.numpy as jnp

    def _L0_gnn_ref(edge_index, embedding_weight):
        import jax, jax.numpy as jnp
        import numpy as np
        NUM_NODES = 50000
        EMBED_DIM = 64
        NUM_EDGES = 1250000
        NUM_LAYERS = 3
        row, col = (edge_index[0], edge_index[1])
        n = embedding_weight.shape[0]
        deg = jax.ops.segment_sum(jnp.ones_like(row, dtype=embedding_weight.dtype), row, num_segments=n)
        deg_inv_sqrt = jnp.where(deg > 0, jax.lax.rsqrt(jnp.maximum(deg, 1.0)) * jnp.where(deg > 0, 1.0, 0.0) + jax.lax.rsqrt(jnp.maximum(deg, 1.0)) * 0.0, 0.0)
        deg_inv_sqrt = jnp.where(deg > 0, jax.lax.rsqrt(jnp.maximum(deg, 1.0)), 0.0)
        x = embedding_weight
        acc = x
        for _ in range(NUM_LAYERS):
            m = deg_inv_sqrt[row][:, None] * x[col]
            x = jax.ops.segment_sum(m, row, num_segments=n) * deg_inv_sqrt[:, None]
            acc = acc + x
        return acc / (NUM_LAYERS + 1)

    def _L1_gnn_ref(x, edge_attr, W1n, b1n, W2n, b2n, W1e, b1e, W2e, b2e, res_w, dp_scale, gamma, beta, edge_index):
        import jax, jax.numpy as jnp
        import numpy as np
        N_NODES = 100000
        N_EDGES = 15625
        NODE_DIM = 64
        EDGE_DIM = 32
        EPS = 1e-05
        SLOPE = 0.1

        def _mlp2(v, W1, b1, W2, b2):
            h = jax.nn.leaky_relu(v @ W1 + b1, negative_slope=SLOPE)
            return h @ W2 + b2
        num_nodes = x.shape[0]
        x_t = _mlp2(x, W1n, b1n, W2n, b2n)
        e_t = _mlp2(edge_attr, W1e, b1e, W2e, b2e)
        src, dst = (edge_index[0], edge_index[1])
        msgs = x_t[src] * e_t * dp_scale
        aggregated = jax.ops.segment_sum(msgs, dst, num_segments=num_nodes)
        out = x + aggregated * res_w
        mu = jnp.mean(out, axis=-1, keepdims=True)
        var = jnp.mean(jnp.square(out - mu), axis=-1, keepdims=True)
        return (out - mu) * jax.lax.rsqrt(var + EPS) * gamma + beta

    def _L2_gnn_ref(emb, edge_index):
        import jax, jax.numpy as jnp
        import numpy as np
        NUM_NODES = 100000
        EMBED_DIM = 64
        NUM_LAYERS = 3
        NUM_EDGES = 50000

        def _lightgcn_embedding(emb, edge_index):
            n = emb.shape[0]
            src, dst = (edge_index[0], edge_index[1])
            deg = jax.ops.segment_sum(jnp.ones(src.shape[0], dtype=emb.dtype), dst, num_segments=n)
            deg_inv_sqrt = jnp.where(deg > 0, jax.lax.rsqrt(jnp.maximum(deg, 1.0)), 0.0)
            w = deg_inv_sqrt[src] * deg_inv_sqrt[dst]
            x = emb
            out = emb
            for _ in range(NUM_LAYERS):
                x = jax.ops.segment_sum(w[:, None] * x[src], dst, num_segments=n)
                out = out + x
            return out / (NUM_LAYERS + 1)
        return _lightgcn_embedding(emb, edge_index)

    def _L3_gnn_ref(edge_index, emb_weight):
        import jax, jax.numpy as jnp
        import numpy as np
        NUM_USERS = 100000
        NUM_MOVIES = 50000
        NUM_NODES = NUM_USERS + NUM_MOVIES
        EMB_DIM = 64
        N_LAYERS = 3
        N_EDGES = 62500
        row, col = (edge_index[0], edge_index[1])
        num_nodes = emb_weight.shape[0]
        deg = jax.ops.segment_sum(jnp.ones_like(col, dtype=emb_weight.dtype), col, num_segments=num_nodes)
        deg_inv_sqrt = jnp.where(deg > 0, jax.lax.rsqrt(jnp.maximum(deg, 1.0)), 0.0)
        deg_inv_sqrt = jnp.where(deg > 0, deg ** (-0.5), 0.0)
        norm = deg_inv_sqrt[row] * deg_inv_sqrt[col]
        embs = emb_weight
        acc = emb_weight
        for _ in range(N_LAYERS):
            msgs = norm[:, None] * embs[row]
            embs = jax.ops.segment_sum(msgs, col, num_segments=num_nodes)
            acc = acc + embs
        return acc / (N_LAYERS + 1)
    edge_index = jnp.stack([src, dst])
    h = jnp.maximum(_layernorm(x, axis=-1), 0.0)
    x = x + _L0_gnn_ref(edge_index, h)
    h = jnp.maximum(_layernorm(x, axis=-1), 0.0)
    x = x + _L1_gnn_ref(h, edge_attr_32, L1_gnn_W1n, L1_gnn_b1n, L1_gnn_W2n, L1_gnn_b2n, L1_gnn_W1e, L1_gnn_b1e, L1_gnn_W2e, L1_gnn_b2e, L1_gnn_res_w, L1_gnn_dp_scale, L1_gnn_gamma, L1_gnn_beta, edge_index)
    h = jnp.maximum(_layernorm(x, axis=-1), 0.0)
    x = x + _L2_gnn_ref(h, edge_index)
    h = jnp.maximum(_layernorm(x, axis=-1), 0.0)
    x = x + _L3_gnn_ref(edge_index, h)
    return x

_drawn_inputs = setup_inputs


def setup_inputs(seed=0):
    import zlib

    import numpy as np

    out = dict(_drawn_inputs(seed))
    spreads = {'L1_gnn_b1n': (0.0, 0.8),
     'L1_gnn_b2n': (0.0, 0.659),
     'L1_gnn_b1e': (0.0, 2.0),
     'L1_gnn_b2e': (0.0, 2.0),
     'L1_gnn_gamma': (1.0, 0.2),
     'L1_gnn_beta': (0.0, 0.1)}
    factors = {'edge_attr_32': 8.0,
     'L1_gnn_W1n': 8.0,
     'L1_gnn_W2n': 5.483,
     'L1_gnn_W1e': 8.0,
     'L1_gnn_W2e': 7.024}
    for name, (base, spread) in spreads.items():
        noise = np.random.default_rng([zlib.crc32(name.encode()), seed]).standard_normal(out[name].shape)
        drawn = base * np.exp(spread * noise) if base else spread * noise
        out[name] = jnp.asarray(drawn.astype(out[name].dtype))
    for name, factor in factors.items():
        out[name] = (out[name] * factor).astype(out[name].dtype)
    return out
```

```python
from contextlib import ExitStack

import concourse.bass as bass
from concourse import mybir

F32 = mybir.dt.float32
I32 = mybir.dt.int32
ALU = mybir.AluOpType
ACT = mybir.ActivationFunctionType
AX_X = mybir.AxisListType.X

P = 128
C = 64
CE = 32
N = 100000
E0 = 50000
T = 392
E = T * P
NC = 782
NP = NC * P
PADKEY = NP - 1
G = 7
NG = T // G
GC = G * C
HALF = T // 2
ZROW = E
TROWS = E + P
SKIP = float(1 << 20)
EPS = 1e-5
SLOPE = 0.1
TB = 98
NTB = T // TB
DCH = 17
NDC = NC // DCH
DW = 8 + C
assert NG % 2 == 0 and NDC % 2 == 0 and NTB * TB == T and NDC * DCH == NC


class Phase:

    def __init__(self, nc, ctx):
        self.nc, self.ctx, self.sets, self.n, self.kept = nc, ctx, ({}, {}), -1, {}

    def next(self):
        self.n += 1

    def sem(self, name):
        mine = self.sets[self.n % 2]
        if name not in mine:
            mine[name] = self.ctx.enter_context(self.nc.semaphore(f"{name}_{self.n % 2}"))
        return mine[name]

    def landed(self, name, total):
        if name not in self.kept:
            self.kept[name] = Landed(self.ctx.enter_context(self.nc.semaphore(name)))
        return self.kept[name].next(total)

    def clear_previous(self, sp):
        if self.n:
            for s in self.sets[1 - self.n % 2].values():
                sp.sem_clear(s)


class Landed:

    def __init__(self, sem):
        self.sem, self.at, self.end = sem, 0, 0

    def next(self, total):
        self.at, self.end = self.end, self.end + total
        return self


def wait_apart(eng, passed, *waits):
    for sem, value in waits:
        eng.wait_ge(sem, value)
    eng.sem_inc(passed, 1)


class Chain:

    def __init__(self, eng, sem, base=0):
        self.eng, self.sem, self.base, self.n = eng, sem, base, 0

    def do(self, ins):
        ins.then_inc(self.sem, 1)
        self.n += 1

    def wait(self):
        self.eng.wait_ge(self.sem, self.base + self.n)


def turns(eng, n, body):
    body(0)
    with eng.Fori(1, n) as i:
        body(i)


def later(i):
    return not isinstance(i, int) or i > 0


def reused(i, b, n):
    return later(i) or b >= n


def bcast(ap, n):
    return ap.unsqueeze(2).to_broadcast([ap.shape[0], ap.shape[1], n])


def program(nc, x, src, dst, attr_t, w1n, b1n, w2n, b2n, w1e, b1e, w2e, b2e, res_w, dp_scale, gamma, beta, out):
    with ExitStack() as ctx:
        def sb(name, shape, dt=F32):
            return ctx.enter_context(nc.sbuf_tensor(name, shape, dt))

        def psum(name, shape):
            return ctx.enter_context(nc.psum_tensor(name, shape, F32))

        def dram(name, shape):
            return nc.dram_tensor(name, shape, F32).ap()

        ph = Phase(nc, ctx)

        keyrow = [dram(f"keyrow{a}", [E]) for a in range(2)]
        count = [dram(f"count{j}", [NP, 1]) for j in range(4)]
        node_tab = dram("node_tab", [NP, 8])
        e_feat = dram("e_feat", [E, C])
        s_rec = dram("s_rec", [E, 8])
        d_rec = dram("d_rec", [E, DW])
        skey = [dram(f"skey{a}", [E]) for a in range(2)]
        table = [dram(f"table{a}", [TROWS, C]) for a in range(2)]
        z0 = dram("z0", [NP, C])
        x1 = dram("x1", [NP, C])
        xd = dram("xd", [E, C])

        ident = sb("ident", [P, P])
        tri = sb("tri", [P, P])
        strict = sb("strict", [P, P])
        lower = sb("lower", [P, P])
        upper = sb("upper", [P, P])
        ones_row = sb("ones_row", [1, P])
        zeros = sb("zeros", [P, NC])
        res_col = sb("res_col", [P, 1])
        dp_col = sb("dp_col", [P, 1])
        gamma_b = sb("gamma_b", [P, C])
        beta_b = sb("beta_b", [P, C])

        key = sb("key", [P, 2, T])
        rank = sb("rank", [P, 2, T])
        after = sb("after", [P, 2, T])
        skey_col = sb("skey_col", [P, 2, T])
        rdeg = sb("rdeg", [P, 2, T])
        TS = T + 2 * G
        hop1_idx = sb("hop1_idx", [P, TS], I32)
        src_idx = sb("src_idx", [P, TS], I32)
        dst_idx = sb("dst_idx", [P, TS], I32)
        end_idx = sb("end_idx", [P, 2, TS], I32)
        scat_idx = sb("scat_idx", [P, 2, TS], I32)
        first_same = sb("first_same", [1, 2, T])

        acc = sb("acc", [P, T, C])
        WORK = 14600
        work = sb("work", [P, WORK])
        cursor = [0]

        def take(*shape, dt=F32, parts=P):
            n = 1
            for s in shape:
                n *= s
            a = work[0:parts, cursor[0]:cursor[0] + n]
            cursor[0] += n
            assert cursor[0] <= WORK, cursor[0]
            if dt != F32:
                a = a.bitcast(dt)
            if len(shape) == 2:
                a = a.rearrange("p (a b) -> p a b", a=shape[0])
            if len(shape) == 3:
                a = a.rearrange("p (a b c) -> p a b c", a=shape[0], b=shape[1])
            return a

        bank = [psum(f"bank{k}", [P, 512]) for k in range(8)]

        def layernorm(c, src_, xc, sq, st, n, roots, k, relu=True, dst_=None):
            s1, s2 = st[:, 0:n], st[:, n:2 * n]
            c.do(nc.vector.tensor_reduce(s1, src_, AX_X, ALU.add))
            c.wait()
            c.do(nc.vector.tensor_scalar(s1, s1, -1.0 / C, None, ALU.mult))
            c.wait()
            c.do(nc.vector.tensor_tensor(xc, src_, bcast(s1, C), ALU.add))
            c.wait()
            c.do(nc.vector.tensor_tensor(sq, xc, xc, ALU.mult))
            c.wait()
            c.do(nc.vector.tensor_reduce(s2, sq, AX_X, ALU.add))
            c.wait()
            c.do(nc.vector.tensor_scalar(s2, s2, 1.0 / C, EPS, ALU.mult, ALU.add))
            c.wait()
            nc.vector.reciprocal(s2, s2).then_inc(roots[0], 1)
            c.eng.wait_ge(roots[1], k + 1)
            if relu:
                c.do(nc.vector.scalar_tensor_tensor(dst_, xc, 0.0, bcast(s2, C), ALU.max, ALU.mult))
            else:
                c.do(nc.vector.tensor_tensor(dst_, xc, bcast(s2, C), ALU.mult))
            c.wait()

        def root(act, st, n, roots, k):
            s2 = st[:, n:2 * n]
            act.wait_ge(roots[0], k + 1)
            nc.scalar.activation(s2, s2, ACT.Sqrt).then_inc(roots[1], 1)

        def keys():
            ph.next()
            s_in, s_conv, s_turn, s_col, s_row = (ph.sem(n) for n in ("k_in", "k_conv", "k_turn", "k_col", "k_row"))
            s_zero, s_clear, s_const, s_par = (ph.sem(n) for n in ("k_zero", "k_clear", "k_const", "k_par"))
            cursor[0] = 0
            raw = take(2, NTB * P, dt=I32, parts=TB)
            rowf = take(2, NTB * P, parts=TB)
            with nc.Block() as block:
                @block.sync
                def _(sp):
                    ph.clear_previous(sp)
                    for a, arr in enumerate((src, dst)):
                        sp.dma_start(raw[:, a, :].rearrange("p (b e) -> p b e", b=NTB),
                                     arr.rearrange("(b p e) -> p b e", b=NTB, p=TB)).then_inc(s_in, 16)
                    sp.dma_start(res_col[:], res_w.unsqueeze(0).to_broadcast([P, 1])).then_inc(s_par, 16)
                    sp.dma_start(dp_col[:], dp_scale.unsqueeze(0).to_broadcast([P, 1])).then_inc(s_par, 16)
                    sp.dma_start(gamma_b[:], gamma.unsqueeze(0).to_broadcast([P, C])).then_inc(s_par, 16)
                    sp.dma_start(beta_b[:], beta.unsqueeze(0).to_broadcast([P, C])).then_inc(s_par, 16)
                    sp.wait_ge(s_zero, 1)
                    for t in count:
                        sp.dma_start(t.rearrange("(p c) o -> p (c o)", p=P), zeros[:]).then_inc(s_clear, 16)
                    for t in table:
                        sp.dma_start(t[ZROW:ZROW + P, :], zeros[:, 0:C]).then_inc(s_clear, 16)
                    sp.wait_ge(s_conv, 2)
                    for a in range(2):
                        sp.dma_start(keyrow[a].rearrange("(b p e) -> p b e", b=NTB, p=TB),
                                     rowf[:, a, :].rearrange("p (b e) -> p b e", b=NTB)).then_inc(s_row, 16)
                    sp.wait_ge(s_row, 32)
                    sp.wait_ge(s_clear, 96)
                    sp.wait_ge(s_par, 64)

                @block.gpsimd
                def _(pool):
                    nc.gpsimd.memset(zeros[:], 0.0).then_inc(s_zero, 1)
                    nc.gpsimd.memset(ident[:], 0.0).then_inc(s_const, 1)
                    for m in (tri, strict, lower, upper, ones_row):
                        nc.gpsimd.memset(m[:], 1.0).then_inc(s_const, 1)
                    pool.wait_ge(s_const, 6)
                    for m, op, fill in ((ident, ALU.not_equal, 1.0), (tri, ALU.is_ge, 0.0), (strict, ALU.is_gt, 0.0)):
                        nc.gpsimd.affine_select(out=m[:], in_=m[:], compare_op=op, fill=fill, base=0,
                                                pattern=[[1, P]], channel_multiplier=-1).then_inc(s_const, 1)
                    nc.gpsimd.affine_select(out=upper[:], in_=upper[:], compare_op=ALU.is_gt, fill=0.0, base=0,
                                            pattern=[[1, P]], channel_multiplier=-1).then_inc(s_const, 1)
                    nc.gpsimd.affine_select(out=lower[:], in_=lower[:], compare_op=ALU.is_gt, fill=0.0, base=0,
                                            pattern=[[-1, P]], channel_multiplier=1).then_inc(s_const, 1)
                    pool.wait_ge(s_const, 11)

                @block.vector
                def _(dve):
                    dve.wait_ge(s_in, 32)
                    for a in range(2):
                        nc.vector.tensor_copy(rowf[:, a, :], raw[:, a, :]).then_inc(s_conv, 1)
                    for a in range(2):
                        dve.wait_ge(s_turn, NTB * (a + 1))
                        nc.vector.tensor_copy(key[:, a, :], bank[a][:, 0:T]).then_inc(s_col, 1)
                    dve.wait_ge(s_col, 2)

                @block.tensor
                def _(pe):
                    pe.wait_ge(s_conv, 2)
                    pe.wait_ge(s_const, 11)
                    for a in range(2):
                        for b in range(NTB):
                            nc.tensor.transpose(bank[a][:, b * TB:(b + 1) * TB], rowf[:, a, b * P:(b + 1) * P],
                                                ident[0:TB, 0:TB]).then_inc(s_turn, 1)

        def ranks():
            ph.next()
            s_row = [ph.sem(f"r_row{b}") for b in range(2)]
            s_pair, s_gidx, s_last, s_sidx, s_rank, s_clear = (
                ph.sem(n) for n in ("r_pair", "r_gidx", "r_last", "r_sidx", "r_rank", "r_clear"))
            got_in = [ph.landed(f"r_got{j}", 16 * HALF) for j in range(4)]
            s_new = [ph.sem(f"r_new{j}") for j in range(4)]
            put_out = [ph.landed(f"r_put{j}", 16 * HALF) for j in range(4)]
            cursor[0] = 0
            kr = take(2, 4, P)
            junk = take(8, P)
            gidx = take(2, 4, dt=I32)
            sidx = take(2, 4, dt=I32)
            last = take(2, 4)
            got = take(2, 4)
            val = take(2, 4)
            keyc, rankc, afterc = (t.rearrange("p a (h s) -> p a h s", h=2) for t in (key, rank, after))

            def four(t):
                return t.rearrange("p (a h o) -> p a h o", a=2, h=2)

            with nc.Block() as block:
                @block.sync
                def _(sp):
                    ph.clear_previous(sp)

                    def load(i, b):
                        if later(i):
                            sp.wait_ge(s_pair, i * 16 + 8 * b - 8)
                        for a in range(2):
                            for h in range(2):
                                sp.dma_start(kr[:, b, 2 * a + h, :],
                                             keyrow[a].rearrange("(h s e) -> h s e", h=2, e=P)
                                             [h, bass.ds(i * 2 + b, 1), :].to_broadcast([P, P])
                                             ).then_inc(s_row[b], 16)

                    def both(i):
                        load(i, 0)
                        load(i, 1)
                    turns(sp, HALF // 2, both)

                @block.scalar
                def _(act):
                    z = z0.rearrange("(p c) d -> p (c d)", p=P)
                    for k in range(C):
                        act.dma_start(z[:, k * NC:(k + 1) * NC], zeros[:]).then_inc(s_clear, 16)
                    act.wait_ge(s_clear, 16 * C)

                @block.gpsimd
                def _(pool):
                    passed = ph.sem("passed_pool")

                    def step(i, b):
                        s = i * 2 + b
                        wait_apart(pool, passed, (s_gidx, s + 1))
                        for j in range(4):
                            if reused(i, b, 1):
                                wait_apart(pool, passed, (put_out[j].sem, s * 16))
                            nc.gpsimd.indirect_dma_start(
                                got[:, b, j:j + 1], None, count[j],
                                bass.IndirectOffsetOnAxis(ap=gidx[:, b, j:j + 1], axis=0)).then_inc(got_in[j].sem, 16)
                        for j in range(4):
                            wait_apart(pool, passed, (s_new[j], s + 1), (s_sidx, s + 1))
                            nc.gpsimd.indirect_dma_start(
                                count[j], bass.IndirectOffsetOnAxis(ap=sidx[:, b, j:j + 1], axis=0),
                                val[:, b, j:j + 1], None, bounds_check=NP - 1, oob_is_err=False
                            ).then_inc(put_out[j].sem, 16)

                    def both(i):
                        step(i, 0)
                        step(i, 1)
                    turns(pool, HALF // 2, both)
                    for j in range(4):
                        pool.wait_ge(put_out[j].sem, 16 * HALF)

                @block.vector
                def _(dve):
                    def pairs(s, uses, b, first):
                        dve.wait_ge(s_row[b], uses * 64)
                        col = bass.ds(s, 1)
                        for j in range(4):
                            a, h = j // 2, j % 2
                            for m, to, k in ((lower, rankc, 0), (upper, afterc, 1)):
                                nc.vector.scalar_tensor_tensor(
                                    junk[:, 2 * j + k, :], kr[:, b, j, :], keyc[:, a, h, col], m[:], ALU.is_equal, ALU.mult,
                                    accum_out=to[:, a, h, col]).then_inc(s_pair, 1)
                        dve.wait_ge(s_pair, s * 8 + 8)
                        if not first:
                            for j in range(4):
                                dve.wait_ge(put_out[j].sem, s * 16 - 16)
                        nc.vector.tensor_scalar(four(gidx[:, b, :]), keyc[:, :, :, col], 1.0, None, ALU.mult).then_inc(s_gidx, 1)
                        nc.vector.tensor_scalar(four(last[:, b, :]), afterc[:, :, :, col], 1.0, SKIP, ALU.min,
                                                ALU.mult).then_inc(s_last, 1)
                        dve.wait_ge(s_last, s + 1)
                        nc.vector.tensor_tensor(four(sidx[:, b, :]), four(last[:, b, :]), keyc[:, :, :, col],
                                                ALU.add).then_inc(s_sidx, 1)

                    def update(s, b):
                        col = bass.ds(s, 1)
                        for j in range(4):
                            dve.wait_ge(got_in[j].sem, s * 16 + 16)
                            nc.vector.scalar_tensor_tensor(
                                val[:, b, j:j + 1], got[:, b, j:j + 1], 1.0, rankc[:, j // 2, j % 2, col],
                                ALU.add, ALU.add).then_inc(s_new[j], 1)
                        dve.wait_ge(s_new[3], s + 1)
                        nc.vector.tensor_tensor(rankc[:, :, :, col], rankc[:, :, :, col], four(got[:, b, :]),
                                                ALU.add).then_inc(s_rank, 1)

                    pairs(0, 1, 0, True)
                    pairs(1, 1, 1, True)
                    update(0, 0)
                    with dve.Fori(1, HALF // 2) as i:
                        pairs(i * 2, i + 1, 0, False)
                        update(i * 2 - 1, 1)
                        pairs(i * 2 + 1, i + 1, 1, False)
                        update(i * 2, 0)
                    update(HALF - 1, 1)
                    dve.wait_ge(s_rank, HALF)

        def edge_mlp():
            ph.next()
            s_w, s_hid, s_z, s_act, s_mm, s_out = (ph.sem(n) for n in ("e_w", "e_hid", "e_z", "e_act", "e_mm", "e_out"))
            s_in = [ph.sem(f"e_in{b}") for b in range(2)]
            stored = [ph.landed(f"e_st{b}", 16 * (NG // 2)) for b in range(2)]
            cursor[0] = 0
            w1 = take(C, parts=CE)
            w2 = take(C, parts=C)
            b1 = take(1, parts=C)
            b2 = take(C, parts=1)
            at = [take(G * P, parts=CE) for _ in range(2)]
            z = [take(2, GC, parts=C) for _ in range(2)]
            hid = [take(G * P, parts=C) for _ in range(2)]
            ft = [take(G, C) for _ in range(2)]
            e_view = e_feat.rearrange("(g k p) d -> g p k d", k=G, p=P)
            with nc.Block() as block:
                @block.sync
                def _(sp):
                    ph.clear_previous(sp)
                    sp.dma_start(w1, w1e).then_inc(s_w, 16)
                    sp.dma_start(w2, w2e).then_inc(s_w, 16)
                    sp.dma_start(b1, b1e.unsqueeze(1)).then_inc(s_w, 16)
                    sp.dma_start(b2, b2e.unsqueeze(0)).then_inc(s_w, 16)

                    def load(i):
                        for b in range(2):
                            g = i * 2 + b
                            if later(i):
                                sp.wait_ge(s_z, g - 1)
                            sp.dma_start(at[b], attr_t[:, bass.ds(g * (G * P), G * P)]).then_inc(s_in[b], 16)
                    turns(sp, NG // 2, load)

                @block.tensor
                def _(pe):
                    pe.wait_ge(s_w, 64)

                    def products(i):
                        for b in range(2):
                            pe.wait_ge(s_in[b], i * 16 + 16)
                            if later(i):
                                pe.wait_ge(s_act, i * 2 + b - 1)
                            for h in range(2):
                                mm = nc.tensor.matmul(bank[2 * b + h][0:C, 0:GC], w1, at[b][:, h * GC:(h + 1) * GC],
                                                      start=True, stop=True)
                            mm.then_inc(s_z, 1)
                        for b in range(2):
                            pe.wait_ge(s_hid, i * 2 + b + 1)
                            if later(i):
                                pe.wait_ge(s_out, i * 2 + b - 1)
                            for k in range(G):
                                o = bank[4 + b][:, k * C:(k + 1) * C]
                                nc.tensor.matmul(o, hid[b][:, k * P:(k + 1) * P], w2, start=True, stop=False)
                                mm = nc.tensor.matmul(o, ones_row[:], b2, start=False, stop=True)
                            mm.then_inc(s_mm, 1)
                    turns(pe, NG // 2, products)

                @block.scalar
                def _(act):
                    act.wait_ge(s_w, 64)

                    def bias(i):
                        for b in range(2):
                            act.wait_ge(s_z, i * 2 + b + 1)
                            if later(i):
                                act.wait_ge(s_hid, i * 2 + b - 1)
                            for h in range(2):
                                ins = nc.scalar.activation(z[b][:, h, :], bank[2 * b + h][0:C, 0:GC], ACT.Identity,
                                                           bias=b1)
                            ins.then_inc(s_act, 1)
                    turns(act, NG // 2, bias)

                @block.vector
                def _(dve):
                    def both(i):
                        for b in range(2):
                            dve.wait_ge(s_act, i * 2 + b + 1)
                            if later(i):
                                dve.wait_ge(s_mm, i * 2 + b - 1)
                            zf = z[b].rearrange("p h e -> p (h e)")
                            nc.vector.scalar_tensor_tensor(hid[b], zf, SLOPE, zf, ALU.mult, ALU.max).then_inc(s_hid, 1)
                        for b in range(2):
                            dve.wait_ge(s_mm, i * 2 + b + 1)
                            if later(i):
                                dve.wait_ge(stored[b].sem, i * 16)
                            nc.vector.tensor_scalar(ft[b].rearrange("p k d -> p (k d)"), bank[4 + b][:, 0:GC],
                                                    dp_col[:], None, ALU.mult).then_inc(s_out, 1)
                    turns(dve, NG // 2, both)

                @block.gpsimd
                def _(pool):
                    with pool.Fori(0, NG // 2) as i:
                        for b in range(2):
                            pool.wait_ge(s_out, i * 2 + b + 1)
                            pool.dma_start(e_view[i * 2 + b], ft[b]).then_inc(stored[b].sem, 16)
                    for b in range(2):
                        pool.wait_ge(stored[b].sem, 16 * (NG // 2))

        def offsets():
            ph.next()
            s_in, s_dve, s_pe, s_out = (ph.sem(n) for n in ("o_in", "o_dve", "o_pe", "o_out"))
            cursor[0] = 0
            cnt = take(4, NC)
            tab = take(NC, 8)
            scan = [acc[:].rearrange("p t d -> p (t d)")[:, k * 2 * NC:(k + 1) * 2 * NC]
                    .rearrange("p (a c) -> p a c", a=2) for k in range(3)]
            with nc.Block() as block:
                @block.sync
                def _(sp):
                    ph.clear_previous(sp)
                    for j in range(4):
                        sp.dma_start(cnt[:, j, :], count[j].rearrange("(p c) o -> p (c o)", p=P)).then_inc(s_in, 16)
                    sp.wait_ge(s_dve, 18)
                    sp.dma_start(node_tab.rearrange("(p c) f -> p c f", p=P), tab).then_inc(s_out, 16)
                    sp.wait_ge(s_out, 16)

                @block.tensor
                def _(pe):
                    pe.wait_ge(s_dve, 12)
                    nc.tensor.matmul(bank[0][:, 0:2], strict[:], scan[1][:, :, NC - 1], start=True, stop=True
                                     ).then_inc(s_pe, 1)

                @block.vector
                def _(dve):
                    c = Chain(dve, s_dve)
                    dve.wait_ge(s_in, 64)
                    halves = cnt.rearrange("p (a h) c -> p a h c", a=2)
                    deg, cur, nxt = scan[0], scan[1], scan[2]
                    c.do(nc.vector.tensor_tensor(deg, halves[:, :, 0, :], halves[:, :, 1, :], ALU.add))
                    c.wait()
                    src_, k = deg, 1
                    steps = []
                    while k < NC:
                        steps.append(k)
                        k *= 2
                    assert len(steps) == 10
                    dst_ = nxt
                    for k in steps:
                        nc.vector.tensor_copy(dst_[:, :, 0:k], src_[:, :, 0:k])
                        c.do(nc.vector.tensor_tensor(dst_[:, :, k:NC], src_[:, :, k:NC], src_[:, :, 0:NC - k], ALU.add))
                        c.wait()
                        src_, dst_ = dst_, (cur if dst_ is nxt else nxt)
                    assert src_ is cur
                    c.do(nc.vector.memset(tab[:, :, 6:8], 0.0))
                    t2 = tab.rearrange("p c f -> p f c")
                    dve.wait_ge(s_pe, 1)
                    for a in range(2):
                        c.do(nc.vector.scalar_tensor_tensor(t2[:, 3 * a, :], cur[:, a, :], bank[0][:, a:a + 1],
                                                            deg[:, a, :], ALU.add, ALU.subtract))
                        c.do(nc.vector.tensor_copy(t2[:, 3 * a + 1, :], cnt[:, 2 * a, :]))
                        c.do(nc.vector.tensor_copy(t2[:, 3 * a + 2, :], deg[:, a, :]))
                    assert c.n == 18, c.n

        def records():
            ph.next()
            s_dve, s_stage, s_ready, s_fill = (ph.sem(n) for n in ("d_dve", "d_stage", "d_ready", "d_fill"))
            s_feat = [ph.sem(f"d_feat{b}") for b in range(2)]
            got_in = [ph.landed(f"d_got{b}", 16 * G * NG) for b in range(2)]
            put_out = [ph.landed(f"d_put{b}", 16 * G * NG) for b in range(2)]
            cursor[0] = 0
            gidx = [take(2, G, dt=I32) for _ in range(2)]
            pidx = [take(2, G, dt=I32) for _ in range(2)]
            got = [take(2, G, 8) for _ in range(2)]
            srec = [take(G, 8) for _ in range(2)]
            drec = [take(G, DW) for _ in range(2)]
            pos = take(G)
            lastp = take(G)
            e_view = e_feat.rearrange("(g k p) d -> g p k d", k=G, p=P)
            with nc.Block() as block:
                @block.sync
                def _(sp):
                    ph.clear_previous(sp)

                    def load(i):
                        for b in range(2):
                            if later(i):
                                sp.wait_ge(put_out[b].sem, i * (16 * 2 * G))
                            sp.dma_start(drec[b][:, :, 8:DW], e_view[i * 2 + b]).then_inc(s_feat[b], 16)
                    turns(sp, NG // 2, load)

                @block.gpsimd
                def _(pool):
                    def both(i):
                        for b in range(2):
                            wait_apart(pool, ph.sem("passed_pool"), (s_stage, i * 2 + b + 1),
                                       *([(s_ready, i * 2 + b - 1)] if later(i) else []))
                            for a in range(2):
                                for k in range(G):
                                    nc.gpsimd.indirect_dma_start(
                                        got[b][:, a, k, :], None, node_tab,
                                        bass.IndirectOffsetOnAxis(ap=gidx[b][:, a, k:k + 1], axis=0)
                                    ).then_inc(got_in[b].sem, 16)
                        for b in range(2):
                            wait_apart(pool, ph.sem("passed_pool"), (s_feat[b], i * 16 + 16), (s_ready, i * 2 + b + 1))
                            for k in range(G):
                                nc.gpsimd.indirect_dma_start(
                                    s_rec, bass.IndirectOffsetOnAxis(ap=pidx[b][:, 0, k:k + 1], axis=0),
                                    srec[b][:, k, :], None).then_inc(put_out[b].sem, 16)
                                nc.gpsimd.indirect_dma_start(
                                    d_rec, bass.IndirectOffsetOnAxis(ap=pidx[b][:, 1, k:k + 1], axis=0),
                                    drec[b][:, k, :], None).then_inc(put_out[b].sem, 16)
                    turns(pool, NG // 2, both)
                    for b in range(2):
                        pool.wait_ge(put_out[b].sem, 16 * 2 * G * (NG // 2))

                @block.vector
                def _(dve):
                    def stage(g, b):
                        nc.vector.tensor_scalar(gidx[b], key[:, :, bass.ds(g * G, G)], 1.0, None, ALU.mult).then_inc(s_stage, 1)

                    def group(i, b, half, n0, again):
                        c = Chain(dve, s_dve, n0)
                        g = i * 2 + b
                        cols = bass.ds(g * G, G)
                        dve.wait_ge(got_in[b].sem, i * (16 * 2 * G) + 16 * 2 * G)
                        if again:
                            stage(g + 2, b)
                        if later(i):
                            dve.wait_ge(put_out[b].sem, i * (16 * 2 * G))
                        for a, rec in ((0, srec[b]), (1, drec[b])):
                            own = got[b][:, a, :, 3 * a:3 * a + 3]
                            oth = got[b][:, 1 - a, :, 3 * a:3 * a + 3]
                            f = rec[:, :, 0:8]
                            c.do(nc.vector.tensor_scalar(f[:, :, 0], key[:, a, cols], 1.0, None, ALU.mult))
                            c.do(nc.vector.tensor_copy(f[:, :, 1], own[:, :, 2]))
                            c.do(nc.vector.tensor_copy(f[:, :, 2], key[:, 1 - a, cols]))
                            c.do(nc.vector.tensor_tensor(pos, own[:, :, 0], rank[:, a, cols], ALU.add))
                            c.wait()
                            if half:
                                c.do(nc.vector.tensor_tensor(pos, pos, own[:, :, 1], ALU.add))
                                c.wait()
                            c.do(nc.vector.tensor_copy(pidx[b][:, a, :], pos))
                            c.do(nc.vector.scalar_tensor_tensor(lastp, own[:, :, 0], -1.0, own[:, :, 2], ALU.add,
                                                                ALU.add))
                            c.wait()
                            c.do(nc.vector.tensor_tensor(lastp, lastp, pos, ALU.not_equal))
                            c.wait()
                            c.do(nc.vector.scalar_tensor_tensor(f[:, :, 4], lastp, SKIP, key[:, a, cols], ALU.mult,
                                                                ALU.add))
                            c.do(nc.vector.scalar_tensor_tensor(f[:, :, 3], oth[:, :, 0], -1.0 - ZROW, oth[:, :, 2],
                                                                ALU.add, ALU.add))
                            c.do(nc.vector.tensor_scalar(f[:, :, 5], oth[:, :, 2], 1.0, None, ALU.min))
                            c.wait()
                            c.do(nc.vector.tensor_tensor(f[:, :, 3], f[:, :, 3], f[:, :, 5], ALU.mult))
                            c.wait()
                            row = nc.vector.tensor_scalar(f[:, :, 3], f[:, :, 3], float(ZROW), None, ALU.add)
                            if a == 0:
                                c.do(row)
                                c.wait()
                            else:
                                row.then_inc(s_ready, 1)
                        return c.n

                    for b in range(2):
                        nc.vector.memset(srec[b][:, :, 6:8], 0.0).then_inc(s_fill, 1)
                        nc.vector.memset(drec[b][:, :, 6:8], 0.0).then_inc(s_fill, 1)
                    dve.wait_ge(s_fill, 4)
                    stage(0, 0)
                    stage(1, 1)
                    per = [23, 25]
                    mid = NG // 4

                    def both(half, i0):
                        def body(i):
                            for b in range(2):
                                n0 = (i - i0) * (2 * per[half]) + (mid * 2 * per[0] if half else 0) + b * per[half]
                                n = group(i, b, half, n0, True)
                                assert n == per[half], n
                        return body
                    both(0, 0)(0)
                    with dve.Fori(1, mid) as i:
                        both(0, 0)(i)
                    with dve.Fori(mid, NG // 2 - 1) as i:
                        both(1, mid)(i)
                    for b in range(2):
                        i = NG // 2 - 1
                        n = group(i, b, 1, (i - mid) * 2 * per[1] + mid * 2 * per[0] + b * per[1], False)
                        assert n == per[1], n

        def columns():
            ph.next()
            s_in, s_dve, s_turn, s_rows, s_put, s_ft, s_z = (
                ph.sem(n) for n in ("c_in", "c_dve", "c_turn", "c_rows", "c_put", "c_ft", "c_z"))
            cursor[0] = 0
            flat = acc[:].rearrange("p t d -> p (t d)")
            meta = [flat[:, a * T * 8:(a + 1) * T * 8].rearrange("p (t f) -> p t f", f=8) for a in range(2)]
            rows = take(2, NTB * P, parts=TB)
            ends = take(2, 2, T, parts=1)
            with nc.Block() as block:
                @block.sync
                def _(sp):
                    ph.clear_previous(sp)
                    for m, r in zip(meta, (s_rec, d_rec)):
                        sp.dma_start(m[:, :, 0:5], r[:, 0:5].rearrange("(t p) f -> p t f", p=P)).then_inc(s_in, 16)
                    sp.wait_ge(s_rows, 2 * NTB)
                    for a in range(2):
                        sp.dma_start(skey[a].rearrange("(b p e) -> p b e", b=NTB, p=TB),
                                     rows[:, a, :].rearrange("p (b e) -> p b e", b=NTB)).then_inc(s_put, 16)
                    sp.wait_ge(s_put, 32)
                    sp.wait_ge(s_z, 1)
                    for a in range(2):
                        v = skey[a].rearrange("(t e) -> e t", e=P)
                        sp.dma_start(ends[:, 0, a, :], v[0:1, :], allow_slow_non_contiguous=True).then_inc(s_ft, 16)
                        sp.dma_start(ends[:, 1, a, 1:T], v[P - 1:P, 0:T - 1], allow_slow_non_contiguous=True).then_inc(s_ft, 16)

                @block.tensor
                def _(pe):
                    pe.wait_ge(s_dve, 2)
                    for a in range(2):
                        for b in range(NTB):
                            nc.tensor.transpose(bank[4 * a + b][0:TB, 0:P], skey_col[:, a, b * TB:(b + 1) * TB],
                                                ident[:]).then_inc(s_turn, 1)

                @block.vector
                def _(dve):
                    c = Chain(dve, s_dve)
                    dve.wait_ge(s_in, 32)
                    for a in range(2):
                        c.do(nc.vector.tensor_copy(skey_col[:, a, :], meta[a][:, :, 0]))
                    nc.vector.memset(ends[:, 1, :, 0:1], -1.0).then_inc(s_z, 1)
                    for a in range(2):
                        c.do(nc.vector.reciprocal(rdeg[:, a, :], meta[a][:, :, 1]))
                        c.do(nc.vector.tensor_copy((hop1_idx, src_idx)[a][:, 0:T], meta[a][:, :, 2]))
                        c.do(nc.vector.tensor_copy(end_idx[:, a, 0:T], meta[a][:, :, 3]))
                        c.do(nc.vector.tensor_copy(scat_idx[:, a, 0:T], meta[a][:, :, 4]))
                        for t in (end_idx[:, a, :], scat_idx[:, a, :], (hop1_idx, src_idx)[a][:, :]):
                            c.do(nc.vector.memset(t[:, T:TS], 0))
                    c.do(nc.vector.tensor_copy(dst_idx[:, 0:T], meta[1][:, :, 0]))
                    c.do(nc.vector.memset(dst_idx[:, T:TS], 0))
                    for a in range(2):
                        for b in range(NTB):
                            dve.wait_ge(s_turn, a * NTB + b + 1)
                            nc.vector.tensor_copy(rows[:, a, b * P:(b + 1) * P], bank[4 * a + b][0:TB, 0:P]
                                                  ).then_inc(s_rows, 1)
                    dve.wait_ge(s_ft, 64)
                    c.do(nc.vector.tensor_tensor(first_same[:], ends[:, 0, :, :], ends[:, 1, :, :], ALU.is_equal))
                    c.wait()
        def select(c, a, g, kr, sel, s_sel):
            c.do(nc.vector.tensor_tensor(sel, kr, bcast(skey_col[:, a, bass.ds(g * G, G)], P), ALU.is_equal))
            c.wait()
            nc.vector.tensor_tensor(sel, sel, tri[:].unsqueeze(1).to_broadcast([P, G, P]), ALU.mult
                                    ).then_inc(s_sel, 1)

        def load_keys(sp, a, g, keys_all, sem):
            sp.dma_start(keys_all.rearrange("p k e -> p (k e)"),
                         skey[a].unsqueeze(0)[:, bass.ds(g * (G * P), G * P)].to_broadcast([P, G * P])
                         ).then_inc(sem, 16)

        def hop(a, source, idx, norm=False, fresh=False, to_table=None, to_nodes=None):
            ph.next()
            NB = 4
            s_kr = [ph.sem(f"h_kr{b}") for b in range(2)]
            got_in = [ph.landed(f"h_got{b}", 16 * G * (NG // NB)) for b in range(NB)]
            s_st = [ph.sem(f"h_st{b}") for b in range(2)]
            put_out = [ph.landed(f"h_put{b}", 16 * G * (NG // 2) if to_nodes is not None else 0) for b in range(2)]
            s_dve, s_stage, s_sel, s_row0, s_carry, s_sum, s_tab, s_acc, s_scat, s_zero = (
                ph.sem(n) for n in ("h_dve", "h_stage", "h_sel", "h_row0", "h_carry", "h_sum", "h_tab", "h_acc",
                                    "h_scat", "h_zero"))
            cursor[0] = 0
            got = [take(G, C) for _ in range(NB)]
            gidx = [take(G, dt=I32) for _ in range(NB)]
            kr = [take(G, P) for _ in range(2)]
            sel = [take(G, P) for _ in range(2)]
            tb = [take(G, C) for _ in range(2)]
            sidx = [take(G, dt=I32) for _ in range(2)]
            xc, sq, st = take(G, C), take(G, C), take(2 * G)
            roots = (ph.sem("h_var"), ph.sem("h_root"))
            carry = bank[2][0:1, 0:C]
            sums = [bank[b][:, 0:GC] for b in range(2)]

            def groups(eng, body):
                def turn(i):
                    for b in range(NB):
                        body(i, b, i * NB + b)
                turns(eng, NG // NB, turn)

            with nc.Block() as block:
                @block.sync
                def _(sp):
                    ph.clear_previous(sp)

                    def load(i, b, g):
                        if reused(i, b, 2):
                            sp.wait_ge(s_sel, g - 1)
                        load_keys(sp, a, g, kr[b % 2], s_kr[b % 2])
                    groups(sp, load)

                @block.scalar
                def _(act):
                    if to_table is not None:
                        view = to_table[0:E, :].rearrange("(g k p) d -> g p k d", k=G, p=P)
                        with act.Fori(0, NG // 2) as i:
                            for b in range(2):
                                if norm:
                                    root(act, st, G, roots, i * 2 + b)
                                act.wait_ge(s_tab, i * 2 + b + 1)
                                act.dma_start(view[i * 2 + b], tb[b]).then_inc(s_st[b], 16)
                        for b in range(2):
                            act.wait_ge(s_st[b], 16 * (NG // 2))

                @block.gpsimd
                def _(pool):
                    def scatter(g, b):
                        wait_apart(pool, ph.sem("passed_pool"), (s_scat, g + 1))
                        for k in range(G):
                            nc.gpsimd.indirect_dma_start(
                                to_nodes, bass.IndirectOffsetOnAxis(ap=sidx[b][:, k:k + 1], axis=0),
                                tb[b][:, k, :], None, bounds_check=NP - 1, oob_is_err=False).then_inc(put_out[b].sem, 16)

                    def gather(i, b, g):
                        wait_apart(pool, ph.sem("passed_pool"), (s_stage, g + 1), *([(s_sum, g - (NB - 1))] if later(i) else []))
                        for k in range(G):
                            nc.gpsimd.indirect_dma_start(
                                got[b][:, k, :], None, source,
                                bass.IndirectOffsetOnAxis(ap=gidx[b][:, k:k + 1], axis=0)).then_inc(got_in[b].sem, 16)
                        if to_nodes is not None and (later(i) or b):
                            scatter(g - 1, (b - 1) % 2)
                    groups(pool, gather)
                    if to_nodes is not None:
                        scatter(NG - 1, (NG - 1) % 2)
                        for b in range(2):
                            pool.wait_ge(put_out[b].sem, put_out[b].end)

                @block.tensor
                def _(pe):
                    def sum_group(i, b, g):
                        pe.wait_ge(s_sel, g + 1)
                        if reused(i, b, 2):
                            pe.wait_ge(s_acc, g - 1)
                        for k in range(G):
                            pe.wait_ge(s_row0, g * G + k + 1)
                            row = got[b][:, k, :]
                            nc.tensor.matmul(carry, sel[b % 2][:, k, P - 1:P], row, start=True, stop=True
                                             ).then_inc(s_carry, 1)
                            mm = nc.tensor.matmul(sums[b % 2][:, k * C:(k + 1) * C], sel[b % 2][:, k, :], row,
                                                  start=True, stop=True)
                        mm.then_inc(s_sum, 1)
                    groups(pe, sum_group)

                @block.vector
                def _(dve):
                    PER = 1 + (7 if norm else 0)

                    def stage(g, b):
                        nc.vector.tensor_scalar(gidx[b], idx[:, bass.ds(g * G, G)], 1.0, None, ALU.mult).then_inc(s_stage, 1)

                    def group(i, b, g):
                        b2, cols = b % 2, bass.ds(g * G, G)
                        c = Chain(dve, s_dve, g * PER)
                        dve.wait_ge(s_kr[b2], (i * 2 + b // 2) * 16 + 16)
                        if reused(i, b, 2):
                            dve.wait_ge(s_sum, g - 1)
                        select(c, a, g, kr[b2], sel[b2], s_sel)
                        dve.wait_ge(got_in[b].sem, i * (16 * G) + (got_in[b].at + 16 * G))
                        stage(g + 2, (b + 2) % NB)
                        if norm:
                            layernorm(c, got[b], xc, sq, st, G, roots, g, dst_=got[b])
                        assert c.n == PER, c.n
                        for k in range(G):
                            t = g * G + k
                            if reused(i, b, 1) or k:
                                dve.wait_ge(s_carry, t)
                            nc.vector.scalar_tensor_tensor(
                                got[b][0:1, k, :], carry, first_same[0:1, a, bass.ds(t, 1)], got[b][0:1, k, :],
                                ALU.mult, ALU.add).then_inc(s_row0, 1)
                        dve.wait_ge(s_sum, g + 1)
                        ps = sums[b2].rearrange("p (k d) -> p k d", k=G)
                        if to_table is not None:
                            if reused(i, b, 2):
                                dve.wait_ge(s_st[b2], (i * 2 + b // 2) * 16)
                            nc.vector.tensor_tensor(tb[b2], ps, bcast(rdeg[:, a, cols], C), ALU.mult
                                                    ).then_inc(s_tab, 1)
                        if fresh:
                            nc.vector.tensor_scalar(acc[:, cols, :], ps, 1.0, None, ALU.mult).then_inc(s_acc, 1)
                        else:
                            nc.vector.tensor_tensor(acc[:, cols, :], acc[:, cols, :], ps, ALU.add).then_inc(s_acc, 1)
                        if to_nodes is not None:
                            if reused(i, b, 2):
                                dve.wait_ge(put_out[b2].sem, (i * 2 + b // 2) * (16 * G) + put_out[b2].at)
                            dve.wait_ge(s_acc, g + 1)
                            nc.vector.tensor_scalar(sidx[b2], scat_idx[:, a, cols], 1.0, None, ALU.mult).then_inc(s_zero, 1)
                            nc.vector.tensor_tensor(tb[b2], acc[:, cols, :], bcast(rdeg[:, a, cols], C), ALU.mult
                                                    ).then_inc(s_scat, 1)

                    nc.vector.memset(carry, 0.0).then_inc(s_zero, 1)
                    dve.wait_ge(s_zero, 1)
                    stage(0, 0)
                    stage(1, 1)
                    groups(dve, group)
                    dve.wait_ge(s_acc, NG)

        def node_chunks():
            return [t.rearrange("(p j c) d -> j p c d", p=P, c=DCH) for t in (x, z0, x1, out)]

        def light_update(c, cur, h, extra, xc, sq, st, roots, k):
            layernorm(c, cur, xc, sq, st, DCH, roots, k, dst_=h)
            if extra is not None:
                c.do(nc.vector.tensor_tensor(h, h, extra, ALU.add))
                c.wait()
            c.do(nc.vector.scalar_tensor_tensor(cur, h, 0.25, cur, ALU.mult, ALU.add))
            c.wait()

        def nodes_after_first():
            ph.next()
            s_in = [ph.sem(f"n_in{b}") for b in range(2)]
            s_out = [ph.sem(f"n_out{b}") for b in range(2)]
            s_dve, s_done = ph.sem("n_dve"), ph.sem("n_done")
            roots = (ph.sem("n_var"), ph.sem("n_root"))
            cursor[0] = 0
            cur = [take(DCH, C) for _ in range(2)]
            zz = [take(DCH, C) for _ in range(2)]
            h, xc, sq, st = take(DCH, C), take(DCH, C), take(DCH, C), take(2 * DCH)
            vx, vz, v1, _ = node_chunks()
            PER = 9
            with nc.Block() as block:
                @block.sync
                def _(sp):
                    ph.clear_previous(sp)

                    def load(i):
                        for b in range(2):
                            if later(i):
                                sp.wait_ge(s_out[b], i * 16)
                            sp.dma_start(cur[b], vx[i * 2 + b]).then_inc(s_in[b], 16)
                            sp.dma_start(zz[b], vz[i * 2 + b]).then_inc(s_in[b], 16)
                    turns(sp, NDC // 2, load)

                @block.vector
                def _(dve):
                    with dve.Fori(0, NDC // 2) as i:
                        for b in range(2):
                            c = Chain(dve, s_dve, i * (2 * PER) + b * PER)
                            dve.wait_ge(s_in[b], i * 32 + 32)
                            light_update(c, cur[b], h, zz[b], xc, sq, st, roots, i * 2 + b)
                            assert c.n == PER
                            dve.sem_inc(s_done, 1)

                @block.scalar
                def _(act):
                    with act.Fori(0, NDC // 2) as i:
                        for b in range(2):
                            root(act, st, DCH, roots, i * 2 + b)
                            act.wait_ge(s_done, i * 2 + b + 1)
                            act.dma_start(v1[i * 2 + b], cur[b]).then_inc(s_out[b], 16)
                    for b in range(2):
                        act.wait_ge(s_out[b], 16 * (NDC // 2))

        def nodes_alone():
            ph.next()
            s_in = [ph.sem(f"a_in{b}") for b in range(2)]
            s_out = [ph.sem(f"a_out{b}") for b in range(2)]
            s_dve, s_done = ph.sem("a_dve"), ph.sem("a_done")
            roots = (ph.sem("a_var"), ph.sem("a_root"))
            cursor[0] = 0
            cur = [take(DCH, C) for _ in range(2)]
            h, xc, sq, st = take(DCH, C), take(DCH, C), take(DCH, C), take(2 * DCH)
            _, _, v1, vo = node_chunks()
            gb, bb = (t[:].unsqueeze(1).to_broadcast([P, DCH, C]) for t in (gamma_b, beta_b))
            PER = 7 + 7 + 3 + 8 + 8
            with nc.Block() as block:
                @block.sync
                def _(sp):
                    ph.clear_previous(sp)

                    def load(i):
                        for b in range(2):
                            if later(i):
                                sp.wait_ge(s_out[b], i * 16)
                            sp.dma_start(cur[b], v1[i * 2 + b]).then_inc(s_in[b], 16)
                    turns(sp, NDC // 2, load)

                @block.vector
                def _(dve):
                    with dve.Fori(0, NDC // 2) as i:
                        for b in range(2):
                            c = Chain(dve, s_dve, i * (2 * PER) + b * PER)
                            dve.wait_ge(s_in[b], i * 16 + 16)
                            k = i * 8 + b * 4
                            layernorm(c, cur[b], xc, sq, st, DCH, roots, k, dst_=h)
                            layernorm(c, h, xc, sq, st, DCH, roots, k + 1, relu=False, dst_=h)
                            c.do(nc.vector.tensor_tensor(h, h, gb, ALU.mult))
                            c.wait()
                            c.do(nc.vector.tensor_tensor(h, h, bb, ALU.add))
                            c.wait()
                            c.do(nc.vector.tensor_tensor(cur[b], cur[b], h, ALU.add))
                            c.wait()
                            light_update(c, cur[b], h, None, xc, sq, st, roots, k + 2)
                            light_update(c, cur[b], h, None, xc, sq, st, roots, k + 3)
                            assert c.n == PER
                            dve.sem_inc(s_done, 1)

                @block.scalar
                def _(act):
                    with act.Fori(0, NDC // 2) as i:
                        for b in range(2):
                            for r in range(4):
                                root(act, st, DCH, roots, i * 8 + b * 4 + r)
                            act.wait_ge(s_done, i * 2 + b + 1)
                            act.dma_start(vo[i * 2 + b], cur[b]).then_inc(s_out[b], 16)
                    for b in range(2):
                        act.wait_ge(s_out[b], 16 * (NDC // 2))

        def mlp_layer():
            ph.next()
            s_kr = [ph.sem(f"m_kr{b}") for b in range(2)]
            s_fe = [ph.sem(f"m_fe{b}") for b in range(2)]
            got_in = [ph.landed(f"m_got{b}", 16 * G * NG) for b in range(2)]
            s_st = [ph.sem(f"m_st{b}") for b in range(2)]
            (s_w, s_dve, s_stage, s_sel, s_h, s_turn, s_ht, s_z, s_zb, s_hid, s_xt, s_msg, s_row0, s_carry, s_sum,
             s_out, s_zero) = (ph.sem("m_" + n) for n in (
                 "w", "dve", "stage", "sel", "h", "turn", "ht", "z", "zb", "hid", "xt", "msg", "row0", "carry", "sum",
                 "out", "zero"))
            roots = (ph.sem("m_var"), ph.sem("m_root"))
            cursor[0] = 0
            w1, w2, b1, b2 = take(P, parts=C), take(C), take(1), take(C, parts=1)
            got = [take(2, G, C) for _ in range(2)]
            gidx = [take(2, G, dt=I32) for _ in range(2)]
            kr = [take(G, P) for _ in range(2)]
            sel = [take(G, P) for _ in range(2)]
            fe = [take(G, C) for _ in range(2)]
            msg = [take(G, C) for _ in range(2)]
            h = take(G, C)
            ht = take(2, GC, parts=C)
            zb = take(2, GC)
            hid = take(G * P)
            xc, sq, st = take(G, C), take(G, C), take(2 * G)
            o = [take(G, C) for _ in range(2)]
            xt, sums, carry = bank[4], bank[5], bank[6][0:1, 0:C]
            gb, bb = (t[:].unsqueeze(1).to_broadcast([P, G, C]) for t in (gamma_b, beta_b))
            fview = d_rec.rearrange("(g k p) f -> g p k f", k=G, p=P)
            oview = xd.rearrange("(g k p) f -> g p k f", k=G, p=P)

            def pair(eng, body):
                def turn(i):
                    for b in range(2):
                        body(i, b, i * 2 + b)
                turns(eng, NG // 2, turn)

            with nc.Block() as block:
                @block.sync
                def _(sp):
                    ph.clear_previous(sp)
                    sp.dma_start(w1, w1n).then_inc(s_w, 16)
                    sp.dma_start(w2, w2n).then_inc(s_w, 16)
                    sp.dma_start(b1, b1n.unsqueeze(1)).then_inc(s_w, 16)
                    sp.dma_start(b2, b2n.unsqueeze(0)).then_inc(s_w, 16)

                    def load(i, b, g):
                        if later(i):
                            sp.wait_ge(s_sel, g - 1)
                            sp.wait_ge(s_msg, g - 1)
                        load_keys(sp, 1, g, kr[b], s_kr[b])
                        sp.dma_start(fe[b], fview[g][:, :, 8:DW]).then_inc(s_fe[b], 16)
                    pair(sp, load)

                @block.gpsimd
                def _(pool):
                    def gather(i, b, g):
                        wait_apart(pool, ph.sem("passed_pool"), (s_stage, g + 1), *([(s_out, g - 1)] if later(i) else []))
                        for r in range(2):
                            for k in range(G):
                                nc.gpsimd.indirect_dma_start(
                                    got[b][:, r, k, :], None, x1,
                                    bass.IndirectOffsetOnAxis(ap=gidx[b][:, r, k:k + 1], axis=0)
                                ).then_inc(got_in[b].sem, 16)
                    pair(pool, gather)

                @block.tensor
                def _(pe):
                    pe.wait_ge(s_w, 64)

                    def products(i, b, g):
                        wait_apart(pe, ph.sem("passed_pe"), (s_h, g + 1), *([(s_ht, g)] if reused(i, b, 1) else []))
                        for k in range(G):
                            for_bank = bank[k // 4][0:C, (k % 4) * P:(k % 4 + 1) * P]
                            mm = nc.tensor.transpose(for_bank, h[:, k, :], ident[:])
                        mm.then_inc(s_turn, 1)
                        pe.wait_ge(s_ht, g + 1)
                        if reused(i, b, 1):
                            pe.wait_ge(s_zb, g)
                        for r in range(2):
                            mm = nc.tensor.matmul(bank[2 + r][:, 0:GC], w1, ht[:, r, :], start=True, stop=True)
                        mm.then_inc(s_z, 1)
                        pe.wait_ge(s_hid, g + 1)
                        if reused(i, b, 1):
                            pe.wait_ge(s_msg, g)
                        for k in range(G):
                            t = xt[:, k * C:(k + 1) * C]
                            nc.tensor.matmul(t, hid[:, k * P:(k + 1) * P], w2, start=True, stop=False)
                            mm = nc.tensor.matmul(t, ones_row[:], b2, start=False, stop=True)
                        mm.then_inc(s_xt, 1)
                        pe.wait_ge(s_sel, g + 1)
                        if reused(i, b, 1):
                            pe.wait_ge(s_out, g)
                        for k in range(G):
                            pe.wait_ge(s_row0, g * G + k + 1)
                            nc.tensor.matmul(carry, sel[b][:, k, P - 1:P], msg[b][:, k, :], start=True, stop=True
                                             ).then_inc(s_carry, 1)
                            mm = nc.tensor.matmul(sums[:, k * C:(k + 1) * C], sel[b][:, k, :], msg[b][:, k, :],
                                                  start=True, stop=True)
                        mm.then_inc(s_sum, 1)
                    pair(pe, products)

                @block.scalar
                def _(act):
                    act.wait_ge(s_w, 64)

                    def copies(i, b, g):
                        root(act, st, G, roots, g * 3 - 2 if reused(i, b, 1) else 0)
                        act.wait_ge(s_turn, g + 1)
                        if reused(i, b, 1):
                            act.wait_ge(s_z, g)
                        flat = ht.rearrange("p r e -> p (r e)")
                        nc.scalar.activation(flat[:, 0:4 * P], bank[0][0:C, :], ACT.Copy)
                        nc.scalar.activation(flat[:, 4 * P:G * P], bank[1][0:C, 0:3 * P], ACT.Copy).then_inc(s_ht, 1)
                        if reused(i, b, 1):
                            root(act, st, G, roots, g * 3 - 1)
                        act.wait_ge(s_z, g + 1)
                        if reused(i, b, 1):
                            act.wait_ge(s_hid, g)
                        for r in range(2):
                            ins = nc.scalar.activation(zb[:, r, :], bank[2 + r][:, 0:GC], ACT.Identity, bias=b1)
                        ins.then_inc(s_zb, 1)
                        if reused(i, b, 1):
                            root(act, st, G, roots, g * 3)
                            act.wait_ge(s_out, g)
                            act.dma_start(oview[g - 1], o[(b - 1) % 2]).then_inc(s_st[(b - 1) % 2], 16)
                    pair(act, copies)
                    for r in range(2):
                        root(act, st, G, roots, 3 * NG - 2 + r)
                    act.wait_ge(s_out, NG)
                    act.dma_start(oview[NG - 1], o[1]).then_inc(s_st[1], 16)
                    for b in range(2):
                        act.wait_ge(s_st[b], 16 * (NG // 2))

                @block.vector
                def _(dve):
                    dve.wait_ge(s_w, 64)

                    def stage(g, b):
                        cols = bass.ds(g * G, G)
                        nc.vector.tensor_scalar(gidx[b][:, 0, :], src_idx[:, cols], 1.0, None, ALU.mult).then_inc(s_zero, 1)
                        nc.vector.tensor_scalar(gidx[b][:, 1, :], dst_idx[:, cols], 1.0, None, ALU.mult).then_inc(s_stage, 1)

                    def front(i, b, g, n0):
                        k = g * 3 - 2 if reused(i, b, 1) else 0
                        c = Chain(dve, s_dve, n0)
                        dve.wait_ge(s_kr[b], i * 16 + 16)
                        if later(i):
                            dve.wait_ge(s_sum, g - 1)
                        select(c, 1, g, kr[b], sel[b], s_sel)
                        dve.wait_ge(got_in[b].sem, i * (32 * G) + 32 * G)
                        if reused(i, b, 1):
                            dve.wait_ge(s_turn, g)
                        layernorm(c, got[b][:, 0], xc, sq, st, G, roots, k, dst_=h)
                        dve.sem_inc(s_h, 1)
                        return c.n

                    def back(i, b, g, n0, last):
                        c = Chain(dve, s_dve, n0)
                        k = g * 3 + (1 if last else 2)
                        ps = sums[:, 0:GC].rearrange("p (k d) -> p k d", k=G)
                        if reused(i, b, 2):
                            dve.wait_ge(s_st[b], i * 16)
                        layernorm(c, got[b][:, 1], xc, sq, st, G, roots, k, dst_=o[b])
                        dve.wait_ge(s_sum, g + 1)
                        c.do(nc.vector.scalar_tensor_tensor(o[b], ps, res_col[:], o[b], ALU.mult, ALU.add))
                        c.wait()
                        layernorm(c, o[b], xc, sq, st, G, roots, k + 1, relu=False, dst_=o[b])
                        c.do(nc.vector.tensor_tensor(o[b], o[b], gb, ALU.mult))
                        c.wait()
                        c.do(nc.vector.tensor_tensor(o[b], o[b], bb, ALU.add))
                        c.wait()
                        if not last:
                            stage(g + 2, b)
                        nc.vector.tensor_tensor(o[b], o[b], got[b][:, 1], ALU.add).then_inc(s_out, 1)
                        return c.n

                    def middle(i, b, g):
                        dve.wait_ge(s_zb, g + 1)
                        if reused(i, b, 1):
                            dve.wait_ge(s_xt, g)
                        zf = zb.rearrange("p r e -> p (r e)")
                        nc.vector.scalar_tensor_tensor(hid, zf, SLOPE, zf, ALU.mult, ALU.max).then_inc(s_hid, 1)
                        dve.wait_ge(s_xt, g + 1)
                        dve.wait_ge(s_fe[b], i * 16 + 16)
                        nc.vector.tensor_tensor(msg[b], xt[:, 0:GC].rearrange("p (k d) -> p k d", k=G), fe[b], ALU.mult
                                                ).then_inc(s_msg, 1)
                        dve.wait_ge(s_msg, g + 1)
                        for k in range(G):
                            t = g * G + k
                            if reused(i, b, 1) or k:
                                dve.wait_ge(s_carry, t)
                            nc.vector.scalar_tensor_tensor(
                                msg[b][0:1, k, :], carry, first_same[0:1, 1, bass.ds(t, 1)], msg[b][0:1, k, :],
                                ALU.mult, ALU.add).then_inc(s_row0, 1)

                    nc.vector.memset(carry, 0.0).then_inc(s_zero, 1)
                    dve.wait_ge(s_zero, 1)
                    stage(0, 0)
                    stage(1, 1)
                    F, B = 1 + 7, 7 + 1 + 7 + 2
                    assert front(0, 0, 0, 0) == F
                    middle(0, 0, 0)
                    assert front(0, 1, 1, F) == F
                    assert back(0, 0, 0, 2 * F, False) == B
                    middle(0, 1, 1)
                    with dve.Fori(1, NG // 2) as i:
                        n = i * (2 * (F + B)) - B
                        front(i, 0, i * 2, n)
                        back(i - 1, 1, i * 2 - 1, n + F, False)
                        middle(i, 0, i * 2)
                        front(i, 1, i * 2 + 1, n + F + B)
                        back(i, 0, i * 2, n + 2 * F + B, False)
                        middle(i, 1, i * 2 + 1)
                    i = NG // 2
                    back(i - 1, 1, NG - 1, i * (2 * (F + B)) - B, True)
                    dve.wait_ge(s_out, NG)

        DG = 2 * G
        ND = T // DG

        def between(update, final):
            ph.next()
            s_in = [ph.sem(f"b_in{b}") for b in range(2)]
            s_dve, s_cols, s_done, s_tab = (ph.sem("b_" + n) for n in ("dve", "cols", "done", "tab"))
            cursor[0] = 0
            cur = [take(DG, C) for _ in range(2)]
            y = [take(DG, C) for _ in range(2)]
            h, xc, sq, st = take(DG, C), take(DG, C), take(DG, C), take(2 * DG)
            isq, sqd, qsq = take(T), take(T), take(T)
            sidx = [take(DG, dt=I32) for _ in range(2)]
            vx = xd.rearrange("(g k p) d -> g p k d", k=DG, p=P)
            vt = table[0][0:E, :].rearrange("(g k p) d -> g p k d", k=DG, p=P)
            roots = (ph.sem("b_var"), ph.sem("b_root"))
            per = (2 if update else 0) + (0 if final else 9)
            stores = 16 * DG if final else 32 if update else 16
            s_st = [ph.landed(f"b_put{b}", stores * (ND // 2)).sem if final else ph.sem(f"b_st{b}") for b in range(2)]

            def pair(eng, body):
                def turn(i):
                    for b in range(2):
                        body(i, b, i * 2 + b)
                turns(eng, ND // 2, turn)

            with nc.Block() as block:
                @block.sync
                def _(sp):
                    ph.clear_previous(sp)

                    def load(i, b, g):
                        if later(i):
                            sp.wait_ge(s_st[b], i * stores)
                            sp.wait_ge(s_done, g - 1)
                        sp.dma_start(cur[b], vx[g]).then_inc(s_in[b], 16)
                    pair(sp, load)

                @block.vector
                def _(dve):
                    dve.wait_ge(s_cols, 1)
                    nc.vector.reciprocal(sqd, isq).then_inc(s_cols, 1)
                    nc.vector.tensor_scalar(qsq, isq, 0.25, None, ALU.mult).then_inc(s_cols, 1)
                    dve.wait_ge(s_cols, 3)

                    def group(i, b, g):
                        c = Chain(dve, s_dve, g * per)
                        cols = bass.ds(g * DG, DG)
                        dve.wait_ge(s_in[b], i * 16 + 16)
                        if later(i):
                            dve.wait_ge(s_st[b], i * stores)
                        if final and reused(i, b, 1):
                            dve.wait_ge(s_done, g)
                        if update:
                            c.do(nc.vector.tensor_tensor(h, acc[:, cols, :], bcast(qsq[:, cols], C), ALU.mult))
                            if final:
                                c.do(nc.vector.tensor_scalar(sidx[b], scat_idx[:, 1, cols], 1.0, None, ALU.mult))
                                c.wait()
                                nc.vector.tensor_tensor(cur[b], cur[b], h, ALU.add).then_inc(s_done, 1)
                                assert c.n == per
                                return
                            c.wait()
                            c.do(nc.vector.tensor_tensor(cur[b], cur[b], h, ALU.add))
                            c.wait()
                        layernorm(c, cur[b], xc, sq, st, DG, roots, g, dst_=h)
                        c.do(nc.vector.tensor_tensor(acc[:, cols, :], h, bcast(sqd[:, cols], C), ALU.mult))
                        c.do(nc.vector.tensor_tensor(y[b], h, bcast(isq[:, cols], C), ALU.mult))
                        c.wait()
                        dve.sem_inc(s_done, 1)
                        assert c.n == per, c.n
                    pair(dve, group)

                if final:
                    @block.scalar
                    def _(act):
                        nc.scalar.activation(isq, rdeg[:, 1, :], ACT.Sqrt).then_inc(s_cols, 1)

                    @block.gpsimd
                    def _(pool):
                        def scatter(i, b, g):
                            wait_apart(pool, ph.sem("passed_pool"), (s_done, g + 1))
                            for k in range(DG):
                                nc.gpsimd.indirect_dma_start(
                                    out, bass.IndirectOffsetOnAxis(ap=sidx[b][:, k:k + 1], axis=0),
                                    cur[b][:, k, :], None, bounds_check=NP - 1, oob_is_err=False).then_inc(s_st[b], 16)
                        pair(pool, scatter)
                        for b in range(2):
                            pool.wait_ge(s_st[b], stores * (ND // 2))
                else:
                    @block.scalar
                    def _(act):
                        nc.scalar.activation(isq, rdeg[:, 1, :], ACT.Sqrt).then_inc(s_cols, 1)

                        def store(i, b, g):
                            root(act, st, DG, roots, g)
                            act.wait_ge(s_done, g + 1)
                            act.dma_start(vt[g], y[b]).then_inc(s_st[b], 16)
                            if update:
                                act.dma_start(vx[g], cur[b]).then_inc(s_st[b], 16)
                        pair(act, store)
                        for b in range(2):
                            act.wait_ge(s_st[b], stores * (ND // 2))

        keys()
        ranks()
        edge_mlp()
        offsets()
        records()
        columns()
        hop(0, x, hop1_idx, norm=True, fresh=True, to_table=table[0])
        hop(0, table[0], end_idx[:, 0, :], to_table=table[1])
        hop(0, table[1], end_idx[:, 0, :], to_nodes=z0)
        nodes_after_first()
        nodes_alone()
        mlp_layer()
        for layer in (2, 3):
            between(layer == 3, False)
            hop(1, table[0], end_idx[:, 1, :], to_table=table[1])
            hop(1, table[1], end_idx[:, 1, :], to_table=table[0])
            hop(1, table[0], end_idx[:, 1, :])
        between(True, True)


def kernel(x, src, dst, edge_attr_32, L1_gnn_W1n, L1_gnn_b1n, L1_gnn_W2n, L1_gnn_b2n, L1_gnn_W1e, L1_gnn_b1e,
           L1_gnn_W2e, L1_gnn_b2e, L1_gnn_res_w, L1_gnn_dp_scale, L1_gnn_gamma, L1_gnn_beta):
    import numpy as np
    import concourse.bacc as bacc
    from concourse.bass_utils import run_bass_kernel_spmd

    def padded(a, n, fill):
        more = np.full((n - a.shape[0],) + a.shape[1:], fill, a.dtype)
        return np.concatenate([np.asarray(a), more], axis=0)

    arrays = {
        "x": padded(x, NP, 0),
        "src": padded(src, E, PADKEY),
        "dst": padded(dst, E, PADKEY),
        "attr_t": np.ascontiguousarray(padded(edge_attr_32, E, 0).T),
        "w1n": L1_gnn_W1n, "b1n": L1_gnn_b1n, "w2n": L1_gnn_W2n, "b2n": L1_gnn_b2n,
        "w1e": L1_gnn_W1e, "b1e": L1_gnn_b1e, "w2e": L1_gnn_W2e, "b2e": L1_gnn_b2e,
        "res_w": L1_gnn_res_w, "dp_scale": L1_gnn_dp_scale, "gamma": L1_gnn_gamma, "beta": L1_gnn_beta,
    }
    arrays = {f"in_{n}": np.ascontiguousarray(a) for n, a in arrays.items()}
    nc = bacc.Bacc("TRN2", target_bir_lowering=False, num_devices=1)
    args = [nc.dram_tensor(n, a.shape, mybir.dt.from_np(a.dtype), kind="ExternalInput").ap() for n, a in arrays.items()]
    args.append(nc.dram_tensor("nodes_out", (NP, C), F32, kind="ExternalOutput").ap())
    program(nc, *args)
    r = run_bass_kernel_spmd(nc, [arrays], core_ids=[0])
    return r.results[0]["nodes_out"][:N]
```

```python
from contextlib import ExitStack

import concourse.bass as bass
from concourse import mybir

F32 = mybir.dt.float32
I32 = mybir.dt.int32
ALU = mybir.AluOpType
ACT = mybir.ActivationFunctionType
AX_X = mybir.AxisListType.X

P = 128
C = 64
CE = 32
N = 100000
E0 = 50000
T = 392
E = T * P
NC = 784
NP = NC * P
PADKEY = NP - 1
G = 7
NG = T // G
GC = G * C
HALF = T // 2
ZROW = E
TROWS = E + P
SKIP = float(1 << 20)
EPS = 1e-5
SLOPE = 0.1
TB = 98
NTB = T // TB
DCH = 28
NDC = NC // DCH
DW = 8 + C
assert NG % 2 == 0 and NDC % 2 == 0 and NDC * DCH == NC and NTB * TB == T and NDC * DCH == NC


class Phase:

    def __init__(self, nc, ctx):
        self.nc, self.ctx, self.sets, self.n, self.kept = nc, ctx, ([], []), -1, {}
        self.names, self.previous = {}, 0

    def next(self):
        self.n += 1
        self.previous = len(self.names)
        self.names = {}

    def sem(self, name):
        if name not in self.names:
            pool, k = self.sets[self.n % 2], len(self.names)
            if k == len(pool):
                pool.append(self.ctx.enter_context(self.nc.semaphore(f"phase{self.n % 2}_{k}")))
            self.names[name] = pool[k]
        return self.names[name]

    def landed(self, name, total):
        if name not in self.kept:
            self.kept[name] = Landed(self.ctx.enter_context(self.nc.semaphore(name)))
        return self.kept[name].next(total)

    def clear_previous(self, sp):
        for s in self.sets[1 - self.n % 2][:self.previous]:
            sp.sem_clear(s)


class Landed:

    def __init__(self, sem):
        self.sem, self.at, self.end = sem, 0, 0

    def next(self, total):
        self.at, self.end = self.end, self.end + total
        return self


def wait_apart(eng, passed, *waits):
    for sem, value in waits:
        eng.wait_ge(sem, value)
    eng.sem_inc(passed, 1)


class Chain:

    def __init__(self, eng, sem, base=0):
        self.eng, self.sem, self.base, self.n = eng, sem, base, 0

    def do(self, ins):
        ins.then_inc(self.sem, 1)
        self.n += 1

    def wait(self):
        self.eng.wait_ge(self.sem, self.base + self.n)


def turns(eng, n, body):
    body(0)
    with eng.Fori(1, n) as i:
        body(i)


def later(i):
    return not isinstance(i, int) or i > 0


def reused(i, b, n):
    return later(i) or b >= n


def bcast(ap, n):
    return ap.unsqueeze(2).to_broadcast([ap.shape[0], ap.shape[1], n])


def program(nc, x, src, dst, attr_t, w1n, b1n, w2n, b2n, w1e, b1e, w2e, b2e, res_w, dp_scale, gamma, beta, out):
    with ExitStack() as ctx:
        def sb(name, shape, dt=F32):
            return ctx.enter_context(nc.sbuf_tensor(name, shape, dt))

        def psum(name, shape):
            return ctx.enter_context(nc.psum_tensor(name, shape, F32))

        def dram(name, shape):
            return nc.dram_tensor(name, shape, F32).ap()

        ph = Phase(nc, ctx)

        keyrow = [dram(f"keyrow{a}", [E]) for a in range(2)]
        count = [dram(f"count{j}", [NP, 1]) for j in range(4)]
        node_tab = dram("node_tab", [NP, 8])
        e_feat = dram("e_feat", [E, C])
        s_rec = dram("s_rec", [E, 8])
        d_rec = dram("d_rec", [E, DW])
        skey = [dram(f"skey{a}", [E]) for a in range(2)]
        joins = [dram(f"joins{a}", [E]) for a in range(2)]
        table = [dram(f"table{a}", [TROWS, C]) for a in range(2)]
        z0 = dram("z0", [NP, C])
        x1 = dram("x1", [NP, C])
        xd = dram("xd", [E, C])

        ident = sb("ident", [P, P])
        strict = sb("strict", [P, P])
        lower = sb("lower", [P, P])
        upper = sb("upper", [P, P])
        ones_row = sb("ones_row", [1, P])
        zeros = sb("zeros", [P, NC])
        res_col = sb("res_col", [P, 1])
        dp_col = sb("dp_col", [P, 1])
        gamma_b = sb("gamma_b", [P, C])
        beta_b = sb("beta_b", [P, C])

        key = sb("key", [P, 2, T])
        rank = sb("rank", [P, 2, T])
        after = sb("after", [P, 2, T])
        skey_col = sb("skey_col", [P, 2, T])
        rdeg = sb("rdeg", [P, 2, T])
        TS = T + 2 * G
        hop1_idx = sb("hop1_idx", [P, TS], I32)
        src_idx = sb("src_idx", [P, TS], I32)
        dst_idx = sb("dst_idx", [P, TS], I32)
        end_idx = sb("end_idx", [P, 2, TS], I32)
        scat_idx = sb("scat_idx", [P, 2, TS], I32)

        acc = sb("acc", [P, T, C])
        WORK = 14600
        work = sb("work", [P, WORK])
        cursor = [0]

        def take(*shape, dt=F32, parts=P, first=0):
            n = 1
            for s in shape:
                n *= s
            a = work[first:parts, cursor[0]:cursor[0] + n]
            cursor[0] += n
            assert cursor[0] <= WORK, cursor[0]
            if dt != F32:
                a = a.bitcast(dt)
            if len(shape) == 2:
                a = a.rearrange("p (a b) -> p a b", a=shape[0])
            if len(shape) == 3:
                a = a.rearrange("p (a b c) -> p a b c", a=shape[0], b=shape[1])
            return a

        bank = [psum(f"bank{k}", [P, 512]) for k in range(8)]

        class Norm:

            def __init__(self, name, n):
                self.n = n
                self.s_var, self.s_root, self.s_shift, self.s_out = (
                    ph.sem(f"{name}_{what}") for what in ("var", "root", "shift", "out"))
                self.bs, self.m, self.d, self.r, self.b = take(n, 6), take(n), take(n), take(n), take(n)

            def stats(self, c, rows, k):
                if not isinstance(k, int) or k:
                    c.eng.wait_ge(self.s_out, k)
                for j in range(self.n):
                    ins = nc.vector.bn_stats(self.bs[:, j, :], rows[:, j, :])
                c.do(ins)
                c.wait()
                bs = self.bs
                c.do(nc.vector.tensor_tensor(self.m, bs[:, :, 1], bs[:, :, 4], ALU.add))
                c.do(nc.vector.tensor_tensor(self.d, bs[:, :, 1], bs[:, :, 4], ALU.subtract))
                c.do(nc.vector.tensor_tensor(self.r, bs[:, :, 2], bs[:, :, 5], ALU.add))
                c.wait()
                c.do(nc.vector.scalar_tensor_tensor(self.d, self.d, 0.25, self.d, ALU.mult, ALU.mult))
                c.do(nc.vector.tensor_scalar(self.r, self.r, 1.0 / C, EPS, ALU.mult, ALU.add))
                c.wait()
                c.do(nc.vector.tensor_tensor(self.r, self.r, self.d, ALU.add))
                c.wait()
                nc.vector.reciprocal(self.r, self.r).then_inc(self.s_var, 1)

            STEPS = 7

            def root(self, act, k):
                act.wait_ge(self.s_var, k + 1)
                nc.scalar.activation(self.r, self.r, ACT.Sqrt).then_inc(self.s_root, 1)

            def shift(self, dve, k):
                dve.wait_ge(self.s_root, k + 1)
                nc.vector.scalar_tensor_tensor(self.b, self.m, -0.5, self.r, ALU.mult, ALU.mult
                                               ).then_inc(self.s_shift, 1)

            def apply(self, act, rows, to, func, k, cols=None):
                cols = range(self.n) if cols is None else cols
                if cols[0] == 0:
                    act.wait_ge(self.s_shift, k + 1)
                for j in cols:
                    ins = nc.scalar.activation(to[:, j, :], rows[:, j, :], func, scale=self.r[:, j:j + 1],
                                               bias=self.b[:, j:j + 1])
                if cols[-1] == self.n - 1:
                    ins.then_inc(self.s_out, 1)
                return ins

            def done(self, eng, k):
                eng.wait_ge(self.s_out, k + 1)

        def keys():
            ph.next()
            s_in, s_conv, s_turn, s_col, s_row = (ph.sem(n) for n in ("k_in", "k_conv", "k_turn", "k_col", "k_row"))
            s_zero, s_clear, s_const, s_par = (ph.sem(n) for n in ("k_zero", "k_clear", "k_const", "k_par"))
            cursor[0] = 0
            raw = take(2, NTB * P, dt=I32, parts=TB)
            rowf = take(2, NTB * P, parts=TB)
            with nc.Block() as block:
                @block.sync
                def _(sp):
                    ph.clear_previous(sp)
                    for a, arr in enumerate((src, dst)):
                        sp.dma_start(raw[:, a, :].rearrange("p (b e) -> p b e", b=NTB),
                                     arr.rearrange("(b p e) -> p b e", b=NTB, p=TB)).then_inc(s_in, 16)
                    sp.dma_start(res_col[:], res_w.unsqueeze(0).to_broadcast([P, 1])).then_inc(s_par, 16)
                    sp.dma_start(dp_col[:], dp_scale.unsqueeze(0).to_broadcast([P, 1])).then_inc(s_par, 16)
                    sp.dma_start(gamma_b[:], gamma.unsqueeze(0).to_broadcast([P, C])).then_inc(s_par, 16)
                    sp.dma_start(beta_b[:], beta.unsqueeze(0).to_broadcast([P, C])).then_inc(s_par, 16)
                    sp.wait_ge(s_zero, 1)
                    for t in count:
                        sp.dma_start(t.rearrange("(p c) o -> p (c o)", p=P), zeros[:]).then_inc(s_clear, 16)
                    for t in table:
                        sp.dma_start(t[ZROW:ZROW + P, :], zeros[:, 0:C]).then_inc(s_clear, 16)
                    sp.wait_ge(s_conv, 2)
                    for a in range(2):
                        sp.dma_start(keyrow[a].rearrange("(b p e) -> p b e", b=NTB, p=TB),
                                     rowf[:, a, :].rearrange("p (b e) -> p b e", b=NTB)).then_inc(s_row, 16)
                    sp.wait_ge(s_row, 32)
                    sp.wait_ge(s_clear, 96)
                    sp.wait_ge(s_par, 64)

                @block.gpsimd
                def _(pool):
                    nc.gpsimd.memset(zeros[:], 0.0).then_inc(s_zero, 1)
                    nc.gpsimd.memset(ident[:], 0.0).then_inc(s_const, 1)
                    for m in (strict, lower, upper, ones_row):
                        nc.gpsimd.memset(m[:], 1.0).then_inc(s_const, 1)
                    pool.wait_ge(s_const, 5)
                    for m, op, fill in ((ident, ALU.not_equal, 1.0), (strict, ALU.is_gt, 0.0)):
                        nc.gpsimd.affine_select(out=m[:], in_=m[:], compare_op=op, fill=fill, base=0,
                                                pattern=[[1, P]], channel_multiplier=-1).then_inc(s_const, 1)
                    nc.gpsimd.affine_select(out=upper[:], in_=upper[:], compare_op=ALU.is_gt, fill=0.0, base=0,
                                            pattern=[[1, P]], channel_multiplier=-1).then_inc(s_const, 1)
                    nc.gpsimd.affine_select(out=lower[:], in_=lower[:], compare_op=ALU.is_gt, fill=0.0, base=0,
                                            pattern=[[-1, P]], channel_multiplier=1).then_inc(s_const, 1)
                    pool.wait_ge(s_const, 9)

                @block.vector
                def _(dve):
                    dve.wait_ge(s_in, 32)
                    for a in range(2):
                        nc.vector.tensor_copy(rowf[:, a, :], raw[:, a, :]).then_inc(s_conv, 1)
                    for a in range(2):
                        dve.wait_ge(s_turn, NTB * (a + 1))
                        nc.vector.tensor_copy(key[:, a, :], bank[a][:, 0:T]).then_inc(s_col, 1)
                    dve.wait_ge(s_col, 2)

                @block.tensor
                def _(pe):
                    pe.wait_ge(s_conv, 2)
                    pe.wait_ge(s_const, 9)
                    for a in range(2):
                        for b in range(NTB):
                            nc.tensor.transpose(bank[a][:, b * TB:(b + 1) * TB], rowf[:, a, b * P:(b + 1) * P],
                                                ident[0:TB, 0:TB]).then_inc(s_turn, 1)

        def ranks():
            ph.next()
            s_row = [ph.sem(f"r_row{b}") for b in range(2)]
            s_pair, s_gidx, s_last, s_sidx, s_rank, s_clear = (
                ph.sem(n) for n in ("r_pair", "r_gidx", "r_last", "r_sidx", "r_rank", "r_clear"))
            got_in = [ph.landed(f"r_got{j}", 16 * HALF) for j in range(4)]
            s_new = [ph.sem(f"r_new{j}") for j in range(4)]
            put_out = [ph.landed(f"r_put{j}", 16 * HALF) for j in range(4)]
            cursor[0] = 0
            kr = take(2, 4, P)
            junk = take(8, P)
            gidx = take(2, 4, dt=I32)
            sidx = take(2, 4, dt=I32)
            last = take(2, 4)
            got = take(2, 4)
            val = take(2, 4)
            keyc, rankc, afterc = (t.rearrange("p a (h s) -> p a h s", h=2) for t in (key, rank, after))

            def four(t):
                return t.rearrange("p (a h o) -> p a h o", a=2, h=2)

            with nc.Block() as block:
                @block.sync
                def _(sp):
                    ph.clear_previous(sp)

                    def load(i, b):
                        if later(i):
                            sp.wait_ge(s_pair, i * 16 + 8 * b - 8)
                        for a in range(2):
                            for h in range(2):
                                sp.dma_start(kr[:, b, 2 * a + h, :],
                                             keyrow[a].rearrange("(h s e) -> h s e", h=2, e=P)
                                             [h, bass.ds(i * 2 + b, 1), :].to_broadcast([P, P])
                                             ).then_inc(s_row[b], 16)

                    def both(i):
                        load(i, 0)
                        load(i, 1)
                    turns(sp, HALF // 2, both)

                @block.scalar
                def _(act):
                    z = z0.rearrange("(p c) d -> p (c d)", p=P)
                    for k in range(C):
                        act.dma_start(z[:, k * NC:(k + 1) * NC], zeros[:]).then_inc(s_clear, 16)
                    act.wait_ge(s_clear, 16 * C)

                @block.gpsimd
                def _(pool):
                    passed = ph.sem("passed_pool")

                    def step(i, b):
                        s = i * 2 + b
                        wait_apart(pool, passed, (s_gidx, s + 1))
                        for j in range(4):
                            if reused(i, b, 1):
                                wait_apart(pool, passed, (put_out[j].sem, s * 16))
                            nc.gpsimd.indirect_dma_start(
                                got[:, b, j:j + 1], None, count[j],
                                bass.IndirectOffsetOnAxis(ap=gidx[:, b, j:j + 1], axis=0)).then_inc(got_in[j].sem, 16)
                        for j in range(4):
                            wait_apart(pool, passed, (s_new[j], s + 1), (s_sidx, s + 1))
                            nc.gpsimd.indirect_dma_start(
                                count[j], bass.IndirectOffsetOnAxis(ap=sidx[:, b, j:j + 1], axis=0),
                                val[:, b, j:j + 1], None, bounds_check=NP - 1, oob_is_err=False
                            ).then_inc(put_out[j].sem, 16)

                    def both(i):
                        step(i, 0)
                        step(i, 1)
                    turns(pool, HALF // 2, both)
                    for j in range(4):
                        pool.wait_ge(put_out[j].sem, 16 * HALF)

                @block.vector
                def _(dve):
                    def pairs(s, uses, b, first):
                        dve.wait_ge(s_row[b], uses * 64)
                        col = bass.ds(s, 1)
                        for j in range(4):
                            a, h = j // 2, j % 2
                            for m, to, k in ((lower, rankc, 0), (upper, afterc, 1)):
                                nc.vector.scalar_tensor_tensor(
                                    junk[:, 2 * j + k, :], kr[:, b, j, :], keyc[:, a, h, col], m[:], ALU.is_equal, ALU.mult,
                                    accum_out=to[:, a, h, col]).then_inc(s_pair, 1)
                        dve.wait_ge(s_pair, s * 8 + 8)
                        if not first:
                            for j in range(4):
                                dve.wait_ge(put_out[j].sem, s * 16 - 16)
                        nc.vector.tensor_scalar(four(gidx[:, b, :]), keyc[:, :, :, col], 1.0, None, ALU.mult).then_inc(s_gidx, 1)
                        nc.vector.tensor_scalar(four(last[:, b, :]), afterc[:, :, :, col], 1.0, SKIP, ALU.min,
                                                ALU.mult).then_inc(s_last, 1)
                        dve.wait_ge(s_last, s + 1)
                        nc.vector.tensor_tensor(four(sidx[:, b, :]), four(last[:, b, :]), keyc[:, :, :, col],
                                                ALU.add).then_inc(s_sidx, 1)

                    def update(s, b):
                        col = bass.ds(s, 1)
                        for j in range(4):
                            dve.wait_ge(got_in[j].sem, s * 16 + 16)
                            nc.vector.scalar_tensor_tensor(
                                val[:, b, j:j + 1], got[:, b, j:j + 1], 1.0, rankc[:, j // 2, j % 2, col],
                                ALU.add, ALU.add).then_inc(s_new[j], 1)
                        dve.wait_ge(s_new[3], s + 1)
                        nc.vector.tensor_tensor(rankc[:, :, :, col], rankc[:, :, :, col], four(got[:, b, :]),
                                                ALU.add).then_inc(s_rank, 1)

                    pairs(0, 1, 0, True)
                    pairs(1, 1, 1, True)
                    update(0, 0)
                    with dve.Fori(1, HALF // 2) as i:
                        pairs(i * 2, i + 1, 0, False)
                        update(i * 2 - 1, 1)
                        pairs(i * 2 + 1, i + 1, 1, False)
                        update(i * 2, 0)
                    update(HALF - 1, 1)
                    dve.wait_ge(s_rank, HALF)

        def edge_mlp():
            ph.next()
            s_w, s_hid, s_z, s_act, s_mm, s_out = (ph.sem(n) for n in ("e_w", "e_hid", "e_z", "e_act", "e_mm", "e_out"))
            s_in = [ph.sem(f"e_in{b}") for b in range(2)]
            stored = [ph.landed(f"e_st{b}", 16 * (NG // 2)) for b in range(2)]
            cursor[0] = 0
            w1 = take(C, parts=CE)
            w2 = take(C, parts=C)
            b1 = take(1, parts=C)
            b2 = take(C, parts=1)
            at = [take(G * P, parts=CE) for _ in range(2)]
            z = [take(2, GC, parts=C) for _ in range(2)]
            hid = [take(G * P, parts=C) for _ in range(2)]
            ft = [take(G, C) for _ in range(2)]
            e_view = e_feat.rearrange("(g k p) d -> g p k d", k=G, p=P)
            with nc.Block() as block:
                @block.sync
                def _(sp):
                    ph.clear_previous(sp)
                    sp.dma_start(w1, w1e).then_inc(s_w, 16)
                    sp.dma_start(w2, w2e).then_inc(s_w, 16)
                    sp.dma_start(b1, b1e.unsqueeze(1)).then_inc(s_w, 16)
                    sp.dma_start(b2, b2e.unsqueeze(0)).then_inc(s_w, 16)

                    def load(i):
                        for b in range(2):
                            g = i * 2 + b
                            if later(i):
                                sp.wait_ge(s_z, g - 1)
                            sp.dma_start(at[b], attr_t[:, bass.ds(g * (G * P), G * P)]).then_inc(s_in[b], 16)
                    turns(sp, NG // 2, load)

                @block.tensor
                def _(pe):
                    pe.wait_ge(s_w, 64)

                    def products(i):
                        for b in range(2):
                            pe.wait_ge(s_in[b], i * 16 + 16)
                            if later(i):
                                pe.wait_ge(s_act, i * 2 + b - 1)
                            for h in range(2):
                                mm = nc.tensor.matmul(bank[2 * b + h][0:C, 0:GC], w1, at[b][:, h * GC:(h + 1) * GC],
                                                      start=True, stop=True)
                            mm.then_inc(s_z, 1)
                        for b in range(2):
                            pe.wait_ge(s_hid, i * 2 + b + 1)
                            if later(i):
                                pe.wait_ge(s_out, i * 2 + b - 1)
                            for k in range(G):
                                o = bank[4 + b][:, k * C:(k + 1) * C]
                                nc.tensor.matmul(o, hid[b][:, k * P:(k + 1) * P], w2, start=True, stop=False)
                                mm = nc.tensor.matmul(o, ones_row[:], b2, start=False, stop=True)
                            mm.then_inc(s_mm, 1)
                    turns(pe, NG // 2, products)

                @block.scalar
                def _(act):
                    act.wait_ge(s_w, 64)

                    def bias(i):
                        for b in range(2):
                            act.wait_ge(s_z, i * 2 + b + 1)
                            if later(i):
                                act.wait_ge(s_hid, i * 2 + b - 1)
                            for h in range(2):
                                ins = nc.scalar.activation(z[b][:, h, :], bank[2 * b + h][0:C, 0:GC], ACT.Identity,
                                                           bias=b1)
                            ins.then_inc(s_act, 1)
                    turns(act, NG // 2, bias)

                @block.vector
                def _(dve):
                    def both(i):
                        for b in range(2):
                            dve.wait_ge(s_act, i * 2 + b + 1)
                            if later(i):
                                dve.wait_ge(s_mm, i * 2 + b - 1)
                            zf = z[b].rearrange("p h e -> p (h e)")
                            nc.vector.scalar_tensor_tensor(hid[b], zf, SLOPE, zf, ALU.mult, ALU.max).then_inc(s_hid, 1)
                        for b in range(2):
                            dve.wait_ge(s_mm, i * 2 + b + 1)
                            if later(i):
                                dve.wait_ge(stored[b].sem, i * 16)
                            nc.vector.tensor_scalar(ft[b].rearrange("p k d -> p (k d)"), bank[4 + b][:, 0:GC],
                                                    dp_col[:], None, ALU.mult).then_inc(s_out, 1)
                    turns(dve, NG // 2, both)

                @block.gpsimd
                def _(pool):
                    with pool.Fori(0, NG // 2) as i:
                        for b in range(2):
                            pool.wait_ge(s_out, i * 2 + b + 1)
                            pool.dma_start(e_view[i * 2 + b], ft[b]).then_inc(stored[b].sem, 16)
                    for b in range(2):
                        pool.wait_ge(stored[b].sem, 16 * (NG // 2))

        def offsets():
            ph.next()
            s_in, s_dve, s_pe, s_out = (ph.sem(n) for n in ("o_in", "o_dve", "o_pe", "o_out"))
            cursor[0] = 0
            cnt = take(4, NC)
            tab = take(NC, 8)
            scan = [acc[:].rearrange("p t d -> p (t d)")[:, k * 2 * NC:(k + 1) * 2 * NC]
                    .rearrange("p (a c) -> p a c", a=2) for k in range(3)]
            with nc.Block() as block:
                @block.sync
                def _(sp):
                    ph.clear_previous(sp)
                    for j in range(4):
                        sp.dma_start(cnt[:, j, :], count[j].rearrange("(p c) o -> p (c o)", p=P)).then_inc(s_in, 16)
                    sp.wait_ge(s_dve, 18)
                    sp.dma_start(node_tab.rearrange("(p c) f -> p c f", p=P), tab).then_inc(s_out, 16)
                    sp.wait_ge(s_out, 16)

                @block.tensor
                def _(pe):
                    pe.wait_ge(s_dve, 12)
                    nc.tensor.matmul(bank[0][:, 0:2], strict[:], scan[1][:, :, NC - 1], start=True, stop=True
                                     ).then_inc(s_pe, 1)

                @block.vector
                def _(dve):
                    c = Chain(dve, s_dve)
                    dve.wait_ge(s_in, 64)
                    halves = cnt.rearrange("p (a h) c -> p a h c", a=2)
                    deg, cur, nxt = scan[0], scan[1], scan[2]
                    c.do(nc.vector.tensor_tensor(deg, halves[:, :, 0, :], halves[:, :, 1, :], ALU.add))
                    c.wait()
                    src_, k = deg, 1
                    steps = []
                    while k < NC:
                        steps.append(k)
                        k *= 2
                    assert len(steps) == 10
                    dst_ = nxt
                    for k in steps:
                        nc.vector.tensor_copy(dst_[:, :, 0:k], src_[:, :, 0:k])
                        c.do(nc.vector.tensor_tensor(dst_[:, :, k:NC], src_[:, :, k:NC], src_[:, :, 0:NC - k], ALU.add))
                        c.wait()
                        src_, dst_ = dst_, (cur if dst_ is nxt else nxt)
                    assert src_ is cur
                    c.do(nc.vector.memset(tab[:, :, 6:8], 0.0))
                    t2 = tab.rearrange("p c f -> p f c")
                    dve.wait_ge(s_pe, 1)
                    for a in range(2):
                        c.do(nc.vector.scalar_tensor_tensor(t2[:, 3 * a, :], cur[:, a, :], bank[0][:, a:a + 1],
                                                            deg[:, a, :], ALU.add, ALU.subtract))
                        c.do(nc.vector.tensor_copy(t2[:, 3 * a + 1, :], cnt[:, 2 * a, :]))
                        c.do(nc.vector.tensor_copy(t2[:, 3 * a + 2, :], deg[:, a, :]))
                    assert c.n == 18, c.n

        def records():
            ph.next()
            s_dve, s_stage, s_ready, s_fill = (ph.sem(n) for n in ("d_dve", "d_stage", "d_ready", "d_fill"))
            s_feat = [ph.sem(f"d_feat{b}") for b in range(2)]
            got_in = [ph.landed(f"d_got{b}", 16 * G * NG) for b in range(2)]
            put_out = [ph.landed(f"d_put{b}", 16 * G * NG) for b in range(2)]
            cursor[0] = 0
            gidx = [take(2, G, dt=I32) for _ in range(2)]
            pidx = [take(2, G, dt=I32) for _ in range(2)]
            got = [take(2, G, 8) for _ in range(2)]
            srec = [take(G, 8) for _ in range(2)]
            drec = [take(G, DW) for _ in range(2)]
            pos = take(G)
            lastp = take(G)
            e_view = e_feat.rearrange("(g k p) d -> g p k d", k=G, p=P)
            with nc.Block() as block:
                @block.sync
                def _(sp):
                    ph.clear_previous(sp)

                    def load(i):
                        for b in range(2):
                            if later(i):
                                sp.wait_ge(put_out[b].sem, i * (16 * 2 * G))
                            sp.dma_start(drec[b][:, :, 8:DW], e_view[i * 2 + b]).then_inc(s_feat[b], 16)
                    turns(sp, NG // 2, load)

                @block.gpsimd
                def _(pool):
                    def both(i):
                        for b in range(2):
                            wait_apart(pool, ph.sem("passed_pool"), (s_stage, i * 2 + b + 1),
                                       *([(s_ready, i * 2 + b - 1)] if later(i) else []))
                            for a in range(2):
                                for k in range(G):
                                    nc.gpsimd.indirect_dma_start(
                                        got[b][:, a, k, :], None, node_tab,
                                        bass.IndirectOffsetOnAxis(ap=gidx[b][:, a, k:k + 1], axis=0)
                                    ).then_inc(got_in[b].sem, 16)
                        for b in range(2):
                            wait_apart(pool, ph.sem("passed_pool"), (s_feat[b], i * 16 + 16), (s_ready, i * 2 + b + 1))
                            for k in range(G):
                                nc.gpsimd.indirect_dma_start(
                                    s_rec, bass.IndirectOffsetOnAxis(ap=pidx[b][:, 0, k:k + 1], axis=0),
                                    srec[b][:, k, :], None).then_inc(put_out[b].sem, 16)
                                nc.gpsimd.indirect_dma_start(
                                    d_rec, bass.IndirectOffsetOnAxis(ap=pidx[b][:, 1, k:k + 1], axis=0),
                                    drec[b][:, k, :], None).then_inc(put_out[b].sem, 16)
                    turns(pool, NG // 2, both)
                    for b in range(2):
                        pool.wait_ge(put_out[b].sem, 16 * 2 * G * (NG // 2))

                @block.vector
                def _(dve):
                    def stage(g, b):
                        nc.vector.tensor_scalar(gidx[b], key[:, :, bass.ds(g * G, G)], 1.0, None, ALU.mult).then_inc(s_stage, 1)

                    def group(i, b, half, n0, again):
                        c = Chain(dve, s_dve, n0)
                        g = i * 2 + b
                        cols = bass.ds(g * G, G)
                        dve.wait_ge(got_in[b].sem, i * (16 * 2 * G) + 16 * 2 * G)
                        if again:
                            stage(g + 2, b)
                        if later(i):
                            dve.wait_ge(put_out[b].sem, i * (16 * 2 * G))
                        for a, rec in ((0, srec[b]), (1, drec[b])):
                            own = got[b][:, a, :, 3 * a:3 * a + 3]
                            oth = got[b][:, 1 - a, :, 3 * a:3 * a + 3]
                            f = rec[:, :, 0:8]
                            c.do(nc.vector.tensor_scalar(f[:, :, 0], key[:, a, cols], 1.0, None, ALU.mult))
                            c.do(nc.vector.tensor_copy(f[:, :, 1], own[:, :, 2]))
                            c.do(nc.vector.tensor_copy(f[:, :, 2], key[:, 1 - a, cols]))
                            c.do(nc.vector.tensor_tensor(pos, own[:, :, 0], rank[:, a, cols], ALU.add))
                            c.wait()
                            if half:
                                c.do(nc.vector.tensor_tensor(pos, pos, own[:, :, 1], ALU.add))
                                c.wait()
                            c.do(nc.vector.tensor_copy(pidx[b][:, a, :], pos))
                            c.do(nc.vector.scalar_tensor_tensor(lastp, own[:, :, 0], -1.0, own[:, :, 2], ALU.add,
                                                                ALU.add))
                            c.wait()
                            c.do(nc.vector.tensor_tensor(lastp, lastp, pos, ALU.not_equal))
                            c.wait()
                            c.do(nc.vector.scalar_tensor_tensor(f[:, :, 4], lastp, SKIP, key[:, a, cols], ALU.mult,
                                                                ALU.add))
                            c.do(nc.vector.scalar_tensor_tensor(f[:, :, 3], oth[:, :, 0], -1.0 - ZROW, oth[:, :, 2],
                                                                ALU.add, ALU.add))
                            c.do(nc.vector.tensor_scalar(f[:, :, 5], oth[:, :, 2], 1.0, None, ALU.min))
                            c.wait()
                            c.do(nc.vector.tensor_tensor(f[:, :, 3], f[:, :, 3], f[:, :, 5], ALU.mult))
                            c.wait()
                            row = nc.vector.tensor_scalar(f[:, :, 3], f[:, :, 3], float(ZROW), None, ALU.add)
                            if a == 0:
                                c.do(row)
                                c.wait()
                            else:
                                row.then_inc(s_ready, 1)
                        return c.n

                    for b in range(2):
                        nc.vector.memset(srec[b][:, :, 6:8], 0.0).then_inc(s_fill, 1)
                        nc.vector.memset(drec[b][:, :, 6:8], 0.0).then_inc(s_fill, 1)
                    dve.wait_ge(s_fill, 4)
                    stage(0, 0)
                    stage(1, 1)
                    per = [23, 25]
                    mid = NG // 4

                    def both(half, i0):
                        def body(i):
                            for b in range(2):
                                n0 = (i - i0) * (2 * per[half]) + (mid * 2 * per[0] if half else 0) + b * per[half]
                                n = group(i, b, half, n0, True)
                                assert n == per[half], n
                        return body
                    both(0, 0)(0)
                    with dve.Fori(1, mid) as i:
                        both(0, 0)(i)
                    with dve.Fori(mid, NG // 2 - 1) as i:
                        both(1, mid)(i)
                    for b in range(2):
                        i = NG // 2 - 1
                        n = group(i, b, 1, (i - mid) * 2 * per[1] + mid * 2 * per[0] + b * per[1], False)
                        assert n == per[1], n

        def columns():
            ph.next()
            s_in, s_dve, s_turn, s_rows, s_put, s_ft, s_z, s_same = (
                ph.sem(n) for n in ("c_in", "c_dve", "c_turn", "c_rows", "c_put", "c_ft", "c_z", "c_same"))
            cursor[0] = 0
            flat = acc[:].rearrange("p t d -> p (t d)")
            meta = [flat[:, a * T * 8:(a + 1) * T * 8].rearrange("p (t f) -> p t f", f=8) for a in range(2)]
            rows = take(2, NTB * P, parts=TB)
            ends = take(2, NTB, parts=TB)
            same = take(2, NTB * P, parts=TB)
            with nc.Block() as block:
                @block.sync
                def _(sp):
                    ph.clear_previous(sp)
                    for m, r in zip(meta, (s_rec, d_rec)):
                        sp.dma_start(m[:, :, 0:5], r[:, 0:5].rearrange("(t p) f -> p t f", p=P)).then_inc(s_in, 16)
                    sp.wait_ge(s_rows, 2 * NTB)
                    for a in range(2):
                        sp.dma_start(skey[a].rearrange("(b p e) -> p b e", b=NTB, p=TB),
                                     rows[:, a, :].rearrange("p (b e) -> p b e", b=NTB)).then_inc(s_put, 16)
                    sp.wait_ge(s_put, 32)
                    sp.wait_ge(s_z, 1)
                    for a in range(2):
                        v = skey[a].rearrange("(t e) -> t e", e=P)
                        for b in range(NTB):
                            lo = 1 if b == 0 else 0
                            sp.dma_start(ends[lo:TB, a, b:b + 1], v[b * TB + lo - 1:(b + 1) * TB - 1, P - 1:P],
                                         allow_slow_non_contiguous=True).then_inc(s_ft, 16)
                    sp.wait_ge(s_same, 2)
                    for a in range(2):
                        sp.dma_start(joins[a].rearrange("(b p e) -> p b e", b=NTB, p=TB),
                                     same[:, a, :].rearrange("p (b e) -> p b e", b=NTB)).then_inc(s_put, 16)
                    sp.wait_ge(s_put, 64)

                @block.tensor
                def _(pe):
                    pe.wait_ge(s_dve, 2)
                    for a in range(2):
                        for b in range(NTB):
                            nc.tensor.transpose(bank[4 * a + b][0:TB, 0:P], skey_col[:, a, b * TB:(b + 1) * TB],
                                                ident[:]).then_inc(s_turn, 1)

                @block.vector
                def _(dve):
                    c = Chain(dve, s_dve)
                    dve.wait_ge(s_in, 32)
                    for a in range(2):
                        c.do(nc.vector.tensor_copy(skey_col[:, a, :], meta[a][:, :, 0]))
                    nc.vector.memset(ends, -1.0).then_inc(s_z, 1)
                    for a in range(2):
                        c.do(nc.vector.reciprocal(rdeg[:, a, :], meta[a][:, :, 1]))
                        c.do(nc.vector.tensor_copy((hop1_idx, src_idx)[a][:, 0:T], meta[a][:, :, 2]))
                        c.do(nc.vector.tensor_copy(end_idx[:, a, 0:T], meta[a][:, :, 3]))
                        c.do(nc.vector.tensor_copy(scat_idx[:, a, 0:T], meta[a][:, :, 4]))
                        for t in (end_idx[:, a, :], scat_idx[:, a, :], (hop1_idx, src_idx)[a][:, :]):
                            c.do(nc.vector.memset(t[:, T:TS], 0))
                    c.do(nc.vector.tensor_copy(dst_idx[:, 0:T], meta[1][:, :, 0]))
                    c.do(nc.vector.memset(dst_idx[:, T:TS], 0))
                    for a in range(2):
                        for b in range(NTB):
                            dve.wait_ge(s_turn, a * NTB + b + 1)
                            nc.vector.tensor_copy(rows[:, a, b * P:(b + 1) * P], bank[4 * a + b][0:TB, 0:P]
                                                  ).then_inc(s_rows, 1)
                    dve.wait_ge(s_ft, 16 * 2 * NTB)
                    for a in range(2):
                        nc.vector.tensor_tensor(
                            *(t[:, a, :].rearrange("p (b e) -> p b e", b=NTB) for t in (same, rows)),
                            bcast(ends[:, a, :], P), ALU.is_equal).then_inc(s_same, 1)
                    c.wait()

        def select(a, g, kr, sel, s_sel):
            nc.vector.tensor_tensor(sel, kr, bcast(skey_col[:, a, bass.ds(g * G, G)], P), ALU.is_equal
                                    ).then_inc(s_sel, 1)

        def load_keys(sp, a, g, keys_all, sem):
            sp.dma_start(keys_all.rearrange("p k e -> p (k e)"),
                         skey[a].unsqueeze(0)[:, bass.ds(g * (G * P), G * P)].to_broadcast([P, G * P])
                         ).then_inc(sem, 16)

        class Sums:

            TOP = P - 32

            def __init__(self, name, a, pairs):
                self.a, self.pairs = a, pairs
                self.s_tile, self.s_in, self.s_zero = (ph.sem(f"{name}_{what}") for what in ("tile", "handed", "zero"))
                self.s_join = [ph.sem(f"{name}_join{b}") for b in range(2)]
                self.inn = [take(C, parts=P, first=self.TOP) for _ in range(2)]
                start = cursor[0]
                self.join = [take(G, P, parts=P, first=self.TOP) for _ in range(2)]
                self.join_row = [work[P - 1:P, start + b * G * P:start + (b + 1) * G * P] for b in range(2)]

            def start(self, dve):
                for t in self.join:
                    nc.vector.memset(t, 0.0).then_inc(self.s_zero, 1)

            def load(self, sp, i, b, g):
                if reused(i, b, 2):
                    sp.wait_ge(*self.summed(g - 1))
                elif b == 0:
                    sp.wait_ge(self.s_zero, 2)
                sp.dma_start(self.join_row[b % 2], joins[self.a].unsqueeze(0)[:, bass.ds(g * (G * P), G * P)]
                             ).then_inc(self.s_join[b % 2], 16)

            def out(self, b, k):
                two = self.pairs[b % len(self.pairs)]
                return bank[two[k % 2]][:, (k // 2) * C:(k // 2 + 1) * C]

            def halves(self, b, g, *arrays):
                for c in range(2):
                    n = (G + 1 - c) // 2
                    ps = bank[self.pairs[b % len(self.pairs)][c]][:, 0:n * C].rearrange("p (k d) -> p k d", k=n)
                    yield (ps, *arrays_of(arrays, g, c, n))

            def add_up(self, pe, i, b, g, sel, rows):
                pe.wait_ge(self.s_join[b % 2], i * (TURN // 2 * 16) + (b // 2 * 16 + 16))
                for k in range(G):
                    t, o = g * G + k, self.out(b, k)
                    before = reused(i, b, 1) or k > 0
                    if before and k == 0 and len(self.pairs) == 1:
                        wait_apart(pe, ph.sem("passed_pe"), (self.s_in, t))
                    ins = nc.tensor.matmul(o, sel[:, k, :], rows[:, k, :], start=True, stop=not before)
                    if before:
                        pe.wait_ge(self.s_in, t)
                        ins = nc.tensor.matmul(o, self.join[b % 2][:, k, :], self.inn[(b + k + 1) % 2], start=False,
                                               stop=True)
                    ins.then_inc(self.s_tile, 1)

            def hand_on(self, act, i, b, g, k):
                if reused(i, b, 1) or k:
                    act.wait_ge(self.s_tile, g * G + k)
                    o = self.out(b, k - 1) if k else self.out(b - 1, G - 1)
                    nc.scalar.activation(self.inn[(b + k + 1) % 2], o[self.TOP:P, :], ACT.Copy).then_inc(self.s_in, 1)

            def summed(self, n):
                return self.s_in, n * G

        def arrays_of(arrays, g, c, n):
            for t in arrays:
                if g is None:
                    yield t[:, c:G:2, ...]
                else:
                    yield t[:, bass.ds(g * G + c, n, 2), ...]

        NB = 4
        TURN = 8
        NT = NG // TURN
        assert NT * TURN == NG and NDC == 4 * NT and DCH % G == 0

        def hop(a, source, idx, norm=False, fresh=False, to_table=None, to_nodes=None, dense=None):
            ph.next()
            s_kr = [ph.sem(f"h_kr{b}") for b in range(2)]
            got_in = [ph.landed(f"got{b}", 16 * G * (NG // NB)) for b in range(NB)]
            s_st = [ph.sem(f"h_st{b}") for b in range(2)]
            put_out = [ph.landed(f"put{b}", 16 * G * (NG // 2) if to_nodes is not None else 0) for b in range(2)]
            s_dve, s_stage, s_sel, s_tab, s_acc, s_scat, s_sidx = (
                ph.sem(n) for n in ("h_dve", "h_stage", "h_sel", "h_tab", "h_acc", "h_scat", "h_sidx"))
            s_nin, s_nfree, s_ndone, s_nout, s_ndve = (
                ph.sem(n) for n in ("n_in", "n_free", "n_done", "n_out", "n_dve"))
            cursor[0] = 0
            got = [take(G, C) for _ in range(NB)]
            gidx = [take(G, dt=I32) for _ in range(NB)]
            kr = [take(G, P) for _ in range(2)]
            sel = [take(G, P) for _ in range(2)]
            tb = [take(G, C) for _ in range(2)]
            sidx = [take(G, dt=I32) for _ in range(2)]
            sums = Sums("h", a, [(2 * b, 2 * b + 1) for b in range(NB)])
            ln = Norm("h", G) if norm else None
            if dense is not None:
                cur, h, res = take(DCH, C), take(DCH, C), take(DCH, C)
                nln = Norm("nl", DCH)
                gb, bb = (t[:].unsqueeze(1).to_broadcast([P, DCH, C]) for t in (gamma_b, beta_b))
                _, _, v1, vo = node_chunks()

            def groups(eng, body):
                def turn(i):
                    for b in range(TURN):
                        body(i, b, i * TURN + b)
                turns(eng, NT, turn)

            def uses(i, b, n):
                return i * (TURN // n) + b // n

            with nc.Block() as block:
                @block.sync
                def _(sp):
                    ph.clear_previous(sp)

                    def load(i, b, g):
                        if reused(i, b, 2):
                            sp.wait_ge(s_sel, g - 1)
                        load_keys(sp, a, g, kr[b % 2], s_kr[b % 2])
                        sums.load(sp, i, b, g)
                        if dense is not None and b == 0:
                            if later(i):
                                sp.wait_ge(s_nfree, i)
                            sp.dma_start(cur, v1[i + dense * NT]).then_inc(s_nin, 16)
                        if dense is not None and b == 2 and later(i):
                            sp.wait_ge(s_ndone, i)
                            sp.dma_start(vo[i + (dense * NT - 1)], res).then_inc(s_nout, 16)
                    groups(sp, load)
                    if dense is not None:
                        sp.wait_ge(s_ndone, NT)
                        sp.dma_start(vo[dense * NT + NT - 1], res).then_inc(s_nout, 16)
                        sp.wait_ge(s_nout, 16 * NT)

                @block.scalar
                def _(act):
                    if to_table is not None:
                        view = to_table[0:E, :].rearrange("(g k p) d -> g p k d", k=G, p=P)

                    def store(i, b, g):
                        if to_table is not None:
                            act.wait_ge(s_tab, g * 2)
                            act.dma_start(view[g - 1], tb[(b - 1) % 2]).then_inc(s_st[(b - 1) % 2], 16)

                    def group(i, b, g):
                        if norm:
                            ln.root(act, g)
                            ln.apply(act, got[b % NB], got[b % NB], ACT.Relu, g)
                        for k in range(G):
                            sums.hand_on(act, i, b, g, k)
                            if dense is not None and b % 2:
                                s = b // 2
                                rows, to, func = ((cur, h, ACT.Relu), (h, h, ACT.Identity), (res, h, ACT.Relu),
                                                  (res, h, ACT.Relu))[s]
                                nln.apply(act, rows, to, func, i * 4 + s,
                                          range(k * (DCH // G), (k + 1) * (DCH // G)))
                            if k == 3 and reused(i, b, 1):
                                store(i, b, g)
                        if dense is not None and b % 2 == 0:
                            nln.root(act, i * 4 + b // 2)
                    groups(act, group)
                    sums.hand_on(act, NT, 0, NG, 0)
                    store(NT, 0, NG)
                    if to_table is not None:
                        for b in range(2):
                            act.wait_ge(s_st[b], 16 * (NG // 2))

                @block.gpsimd
                def _(pool):
                    passed = ph.sem("passed_pool")

                    def scatter(g, b):
                        wait_apart(pool, passed, (s_scat, g + 1))
                        for k in range(G):
                            nc.gpsimd.indirect_dma_start(
                                to_nodes, bass.IndirectOffsetOnAxis(ap=sidx[b][:, k:k + 1], axis=0),
                                tb[b][:, k, :], None, bounds_check=NP - 1, oob_is_err=False
                            ).then_inc(put_out[b].sem, 16)

                    def gather(i, b, g):
                        wait_apart(pool, passed, (s_stage, g + 1),
                                   *([sums.summed(g - (NB - 1))] if reused(i, b, NB) else []))
                        for k in range(G):
                            nc.gpsimd.indirect_dma_start(
                                got[b % NB][:, k, :], None, source,
                                bass.IndirectOffsetOnAxis(ap=gidx[b % NB][:, k:k + 1], axis=0)
                            ).then_inc(got_in[b % NB].sem, 16)
                        if to_nodes is not None and reused(i, b, 2):
                            scatter(g - 2, b % 2)
                    groups(pool, gather)
                    if to_nodes is not None:
                        for b in range(2):
                            scatter(NG - 2 + b, b)
                        for b in range(2):
                            pool.wait_ge(put_out[b].sem, put_out[b].end)

                @block.tensor
                def _(pe):
                    def sum_group(i, b, g):
                        pe.wait_ge(s_sel, g + 1)
                        if reused(i, b, NB):
                            pe.wait_ge(s_acc, g * 2 - 2 * (NB - 1))
                        if norm:
                            ln.done(pe, g)
                        else:
                            pe.wait_ge(got_in[b % NB].sem, uses(i, b, NB) * (16 * G) + (got_in[b % NB].at + 16 * G))
                        sums.add_up(pe, i, b, g, sel[b % 2], got[b % NB])
                    groups(pe, sum_group)

                @block.vector
                def _(dve):
                    def stage(g, b):
                        nc.vector.tensor_scalar(gidx[b % NB], idx[:, bass.ds(g * G, G)], 1.0, None, ALU.mult
                                                ).then_inc(s_stage, 1)

                    def post(i, b, g):
                        b2, cols = b % 2, bass.ds(g * G, G)
                        dve.wait_ge(*sums.summed(g + 1))
                        if to_table is not None:
                            if reused(i, b, 2):
                                dve.wait_ge(s_st[b2], uses(i, b, 2) * 16)
                            for c, (ps, rd) in enumerate(sums.halves(b, g, rdeg[:, a, :])):
                                nc.vector.tensor_tensor(tb[b2][:, c:G:2, :], ps, bcast(rd, C), ALU.mult
                                                        ).then_inc(s_tab, 1)
                        for ps, ac in sums.halves(b, g, acc):
                            if fresh:
                                nc.vector.tensor_scalar(ac, ps, 1.0, None, ALU.mult).then_inc(s_acc, 1)
                            else:
                                nc.vector.tensor_tensor(ac, ac, ps, ALU.add).then_inc(s_acc, 1)
                        if to_nodes is not None:
                            if reused(i, b, 2):
                                dve.wait_ge(put_out[b2].sem, uses(i, b, 2) * (16 * G) + put_out[b2].at)
                            dve.wait_ge(s_acc, g * 2 + 2)
                            nc.vector.tensor_scalar(sidx[b2], scat_idx[:, a, cols], 1.0, None, ALU.mult
                                                    ).then_inc(s_sidx, 1)
                            nc.vector.tensor_tensor(tb[b2], acc[:, cols, :], bcast(rdeg[:, a, cols], C), ALU.mult
                                                    ).then_inc(s_scat, 1)

                    def finish_chunk(i):
                        nln.done(dve, i * 4 + 3)
                        nc.vector.scalar_tensor_tensor(res, h, 0.25, res, ALU.mult, ALU.add).then_inc(s_ndone, 1)

                    def stage_of_chunk(i, s, c):
                        if s == 0:
                            if later(i):
                                finish_chunk(i - 1)
                            dve.wait_ge(s_nin, i * 16 + 16)
                            nln.stats(c, cur, i * 4)
                            return
                        nln.done(dve, i * 4 + s - 1)
                        if s == 1:
                            nln.stats(c, h, i * 4 + 1)
                            return
                        if s == 2:
                            c.do(nc.vector.tensor_tensor(h, h, gb, ALU.mult))
                            c.wait()
                            c.do(nc.vector.tensor_tensor(h, h, bb, ALU.add))
                            c.wait()
                            if later(i):
                                dve.wait_ge(s_nout, i * 16)
                            c.do(nc.vector.tensor_tensor(res, cur, h, ALU.add))
                            c.wait()
                            dve.sem_inc(s_nfree, 1)
                        else:
                            c.do(nc.vector.scalar_tensor_tensor(res, h, 0.25, res, ALU.mult, ALU.add))
                            c.wait()
                        nln.stats(c, res, i * 4 + s)

                    def turn(i):
                        nd = Chain(dve, s_ndve, i * (4 + 4 * Norm.STEPS))
                        for b in range(TURN):
                            g = i * TURN + b
                            dve.wait_ge(s_kr[b % 2], uses(i, b, 2) * 16 + 16)
                            if reused(i, b, 2):
                                dve.wait_ge(*sums.summed(g - 1))
                            select(a, g, kr[b % 2], sel[b % 2], s_sel)
                            dve.wait_ge(got_in[b % NB].sem, uses(i, b, NB) * (16 * G) + (got_in[b % NB].at + 16 * G))
                            stage(g + 2, b + 2)
                            if norm:
                                c = Chain(dve, s_dve, g * Norm.STEPS)
                                ln.stats(c, got[b % NB], g)
                                ln.shift(dve, g)
                            if dense is not None:
                                if b % 2 == 0:
                                    stage_of_chunk(i, b // 2, nd)
                                else:
                                    nln.shift(dve, i * 4 + b // 2)
                            if b:
                                post(i, b - 1, g - 1)
                            elif later(i):
                                post(i - 1, TURN - 1, g - 1)
                        if dense is not None:
                            assert nd.n == 4 + 4 * Norm.STEPS

                    sums.start(dve)
                    stage(0, 0)
                    stage(1, 1)
                    turns(dve, NT, turn)
                    post(NT - 1, TURN - 1, NG - 1)
                    if dense is not None:
                        finish_chunk(NT - 1)
                        dve.wait_ge(s_ndone, NT)
                    dve.wait_ge(s_acc, 2 * NG)

        def node_chunks():
            return [t.rearrange("(p j c) d -> j p c d", p=P, c=DCH) for t in (x, z0, x1, out)]

        def nodes_after_first():
            ph.next()
            s_in = [ph.sem(f"n_in{b}") for b in range(2)]
            s_out = [ph.sem(f"n_out{b}") for b in range(2)]
            s_dve, s_done, s_add = (ph.sem(n) for n in ("n_dve", "n_done", "n_add"))
            cursor[0] = 0
            cur = [take(DCH, C) for _ in range(2)]
            zz = [take(DCH, C) for _ in range(2)]
            h = [take(DCH, C) for _ in range(2)]
            ln = [Norm(f"n{b}", DCH) for b in range(2)]
            vx, vz, v1, _ = node_chunks()
            with nc.Block() as block:
                @block.sync
                def _(sp):
                    ph.clear_previous(sp)

                    def load(i):
                        for b in range(2):
                            if later(i):
                                sp.wait_ge(s_out[b], i * 16)
                            sp.dma_start(cur[b], vx[i * 2 + b]).then_inc(s_in[b], 16)
                            sp.dma_start(zz[b], vz[i * 2 + b]).then_inc(s_in[b], 16)
                    turns(sp, NDC // 2, load)

                @block.vector
                def _(dve):
                    def front(i, b):
                        c = Chain(dve, s_dve, i * (2 * Norm.STEPS) + b * Norm.STEPS)
                        dve.wait_ge(s_in[b], i * 32 + 32)
                        ln[b].stats(c, cur[b], i)
                        ln[b].shift(dve, i)

                    def back(i, b):
                        ln[b].done(dve, i)
                        nc.vector.tensor_tensor(h[b], h[b], zz[b], ALU.add).then_inc(s_add, 1)
                        dve.wait_ge(s_add, i * 2 + b + 1)
                        nc.vector.scalar_tensor_tensor(cur[b], h[b], 0.25, cur[b], ALU.mult, ALU.add
                                                       ).then_inc(s_done, 1)

                    def turn(i):
                        front(i, 0)
                        if later(i):
                            back(i - 1, 1)
                        front(i, 1)
                        back(i, 0)
                    turns(dve, NDC // 2, turn)
                    back(NDC // 2 - 1, 1)

                @block.scalar
                def _(act):
                    def work_on(i, b):
                        ln[b].root(act, i)
                        if later(i):
                            act.wait_ge(s_done, i * 2 + b - 1)
                        ln[b].apply(act, cur[b], h[b], ACT.Relu, i)

                    def store(i, b):
                        act.wait_ge(s_done, i * 2 + b + 1)
                        act.dma_start(v1[i * 2 + b], cur[b]).then_inc(s_out[b], 16)

                    def turn(i):
                        work_on(i, 0)
                        if later(i):
                            store(i - 1, 1)
                        work_on(i, 1)
                        store(i, 0)
                    turns(act, NDC // 2, turn)
                    store(NDC // 2 - 1, 1)
                    for b in range(2):
                        act.wait_ge(s_out[b], 16 * (NDC // 2))

        def mlp_layer():
            ph.next()
            s_kr = [ph.sem(f"m_kr{b}") for b in range(2)]
            s_fe = [ph.sem(f"m_fe{b}") for b in range(2)]
            s_st = [ph.sem(f"m_st{b}") for b in range(2)]
            got_in = [ph.landed(f"got{b}", 16 * 2 * G * NT) for b in range(TURN)]
            (s_w, s_dve, s_dve_out, s_fin, s_stage, s_sel, s_h, s_turn, s_ht, s_z, s_zb, s_hid, s_xt, s_msg, s_o, s_out,
             s_zero) = (ph.sem("m_" + n) for n in (
                 "w", "dve", "dve_out", "fin", "stage", "sel", "h", "turn", "ht", "z", "zb", "hid", "xt", "msg", "o",
                 "out", "zero"))
            cursor[0] = 0
            w1, w2, b1, b2 = take(P, parts=C), take(C), take(1), take(C, parts=1)
            gidx = [take(2, G, dt=I32) for _ in range(4)]
            kr = [take(G, P) for _ in range(2)]
            fe = [take(G, C) for _ in range(2)]
            msg = [take(G, C) for _ in range(2)]
            ht = take(2, GC, parts=C)
            zb = take(2, GC)
            hid = take(G * P)
            o = [take(G, C) for _ in range(2)]
            flat = acc[:].rearrange("p t d -> p (t d)")

            def room(k, width):
                return flat[:, k * 2 * GC:(k + 1) * 2 * GC].rearrange("p (r d) -> p r d", d=width)
            got = [room(k, C) for k in range(TURN)]
            h = [room(TURN + k, C) for k in range(4)]
            sel = [room(TURN + 4 + k, P) for k in range(4)]
            sums = Sums("m", 1, [(5, 6)])
            ln_in, ln_out = Norm("mi", 2 * G), Norm("mo", G)
            xt = bank[4]
            gb, bb = (t[:].unsqueeze(1).to_broadcast([P, G, C]) for t in (gamma_b, beta_b))
            fview = d_rec.rearrange("(g k p) f -> g p k f", k=G, p=P)
            oview = xd.rearrange("(g k p) f -> g p k f", k=G, p=P)

            def slots(eng, body):
                def turn(i):
                    for b in range(TURN):
                        body(i, b, i * TURN + b)
                turns(eng, NT, turn)
                for b in range(3):
                    body(NT, b, NG + b)

            def age(i, b, n):
                return reused(i, b, n) if not isinstance(i, int) or i < NT else n > b

            with nc.Block() as block:
                @block.sync
                def _(sp):
                    ph.clear_previous(sp)
                    sp.dma_start(w1, w1n).then_inc(s_w, 16)
                    sp.dma_start(w2, w2n).then_inc(s_w, 16)
                    sp.dma_start(b1, b1n.unsqueeze(1)).then_inc(s_w, 16)
                    sp.dma_start(b2, b2n.unsqueeze(0)).then_inc(s_w, 16)

                    def load(i, b, g):
                        if reused(i, b, 2):
                            sp.wait_ge(s_sel, g - 1)
                        load_keys(sp, 1, g, kr[b % 2], s_kr[b % 2])
                        sums.load(sp, i, b, g)
                        if reused(i, b, 2):
                            sp.wait_ge(s_msg, g - 1)
                        sp.dma_start(fe[b % 2], fview[g][:, :, 8:DW]).then_inc(s_fe[b % 2], 16)

                    def turn(i):
                        for b in range(TURN):
                            load(i, b, i * TURN + b)
                    turns(sp, NT, turn)

                @block.gpsimd
                def _(pool):
                    def gather(i, b, g):
                        wait_apart(pool, ph.sem("passed_pool"), (s_stage, g + 1),
                                   *([(s_out, g - (TURN - 1))] if later(i) else []))
                        for r in range(2):
                            for k in range(G):
                                nc.gpsimd.indirect_dma_start(
                                    got[b][:, r * G + k, :], None, x1,
                                    bass.IndirectOffsetOnAxis(ap=gidx[b % 4][:, r, k:k + 1], axis=0)
                                ).then_inc(got_in[b].sem, 16)

                    def turn(i):
                        for b in range(TURN):
                            gather(i, b, i * TURN + b)
                    turns(pool, NT, turn)

                @block.tensor
                def _(pe):
                    pe.wait_ge(s_w, 64)

                    def first(i, b, g):
                        wait_apart(pe, ph.sem("passed_pe"), (s_h, g + 1), *([(s_ht, g)] if reused(i, b, 1) else []))
                        for k in range(G):
                            half = bank[k // 4][0:C, (k % 4) * P:(k % 4 + 1) * P]
                            mm = nc.tensor.transpose(half, h[b % 4][:, k, :], ident[:])
                        mm.then_inc(s_turn, 1)
                        pe.wait_ge(s_ht, g + 1)
                        if reused(i, b, 1):
                            pe.wait_ge(s_zb, g)
                        for r in range(2):
                            mm = nc.tensor.matmul(bank[2 + r][:, 0:GC], w1, ht[:, r, :], start=True, stop=True)
                        mm.then_inc(s_z, 1)

                    def second(i, b, g):
                        pe.wait_ge(s_hid, g + 1)
                        if reused(i, b, 1):
                            pe.wait_ge(s_msg, g)
                        for k in range(G):
                            t = xt[:, k * C:(k + 1) * C]
                            nc.tensor.matmul(t, hid[:, k * P:(k + 1) * P], w2, start=True, stop=False)
                            mm = nc.tensor.matmul(t, ones_row[:], b2, start=False, stop=True)
                        mm.then_inc(s_xt, 1)

                    def add_up(i, b, g):
                        pe.wait_ge(s_msg, g + 1)
                        if reused(i, b, 1):
                            pe.wait_ge(s_o, g * 2)
                        sums.add_up(pe, i, b, g, sel[b % 4], msg[b % 2])

                    def slot(i, b, g):
                        if age(i, b, 1):
                            second(i, b - 1, g - 1)
                        if age(i, b, 0):
                            first(i, b, g)
                        if age(i, b, 1):
                            add_up(i, b - 1, g - 1)
                    slots(pe, slot)

                @block.scalar
                def _(act):
                    act.wait_ge(s_w, 64)

                    def first(i, b, g):
                        ln_in.root(act, g)
                        if reused(i, b, 4):
                            act.wait_ge(s_o, g * 2 - 6)
                        ln_in.apply(act, got[b % TURN], h[b % 4], ACT.Relu, g, range(G)).then_inc(s_h, 1)
                        ln_in.apply(act, got[b % TURN], h[b % 4], ACT.Relu, g, range(G, 2 * G))
                        act.wait_ge(s_turn, g + 1)
                        if reused(i, b, 1):
                            act.wait_ge(s_z, g)
                        fl = ht.rearrange("p r e -> p (r e)")
                        nc.scalar.activation(fl[:, 0:4 * P], bank[0][0:C, :], ACT.Copy)
                        nc.scalar.activation(fl[:, 4 * P:G * P], bank[1][0:C, 0:3 * P], ACT.Copy).then_inc(s_ht, 1)
                        act.wait_ge(s_z, g + 1)
                        if reused(i, b, 1):
                            act.wait_ge(s_hid, g)
                        for r in range(2):
                            ins = nc.scalar.activation(zb[:, r, :], bank[2 + r][:, 0:GC], ACT.Identity, bias=b1)
                        ins.then_inc(s_zb, 1)

                    def slot(i, b, g):
                        if age(i, b, 0):
                            first(i, b, g)
                        for k in range(G):
                            if age(i, b, 1) and k:
                                sums.hand_on(act, i, b - 1, g - 1, k)
                            if k == 2 and age(i, b, 2):
                                ln_out.root(act, g - 2)
                            if k == G - 1 and age(i, b, 1):
                                sums.hand_on(act, i, b - 1, g - 1, G)
                            if k >= 3 and age(i, b, 2):
                                ln_out.apply(act, o[b % 2], o[b % 2], ACT.Identity, g - 2,
                                             range(2 * (k - 3), min(2 * (k - 2), G)))
                        if age(i, b, 3):
                            act.wait_ge(s_out, g - 2)
                            act.dma_start(oview[g - 3], o[(b - 3) % 2]).then_inc(s_st[(b - 3) % 2], 16)
                    slots(act, slot)
                    for b in range(2):
                        act.wait_ge(s_st[b], 16 * (NG // 2))

                @block.vector
                def _(dve):
                    def stage(g, b):
                        cols = bass.ds(g * G, G)
                        nc.vector.tensor_scalar(gidx[b % 4][:, 0, :], src_idx[:, cols], 1.0, None, ALU.mult
                                                ).then_inc(s_zero, 1)
                        nc.vector.tensor_scalar(gidx[b % 4][:, 1, :], dst_idx[:, cols], 1.0, None, ALU.mult
                                                ).then_inc(s_stage, 1)

                    def first(i, b, g):
                        dve.wait_ge(s_kr[b % 2], i * (16 * TURN // 2) + (b // 2 * 16 + 16))
                        if reused(i, b, 4):
                            dve.wait_ge(*sums.summed(g - 3))
                        select(1, g, kr[b % 2], sel[b % 4], s_sel)
                        dve.wait_ge(got_in[b].sem, i * (32 * G) + (got_in[b].at + 32 * G))
                        ln_in.stats(Chain(dve, s_dve, g * Norm.STEPS), got[b], g)
                        stage(g + 2, b + 2)

                    def second(i, b, g):
                        dve.wait_ge(s_zb, g + 1)
                        if reused(i, b, 1):
                            dve.wait_ge(s_xt, g)
                        zf = zb.rearrange("p r e -> p (r e)")
                        nc.vector.scalar_tensor_tensor(hid, zf, SLOPE, zf, ALU.mult, ALU.max).then_inc(s_hid, 1)

                    def messages(i, b, g):
                        dve.wait_ge(s_xt, g + 1)
                        dve.wait_ge(s_fe[b % 2], i * (16 * TURN // 2) + (b // 2 * 16 + 16))
                        nc.vector.tensor_tensor(msg[b % 2], xt[:, 0:GC].rearrange("p (k d) -> p k d", k=G), fe[b % 2],
                                                ALU.mult).then_inc(s_msg, 1)

                    def third(i, b, g):
                        if reused(i, b, 2):
                            dve.wait_ge(s_st[b % 2], i * (16 * TURN // 2) + b // 2 * 16)
                        dve.wait_ge(*sums.summed(g + 1))
                        for ps, to, own in sums.halves(b, None, o[b % 2], h[b % 4][:, G:2 * G, :]):
                            nc.vector.scalar_tensor_tensor(to, ps, res_col[:], own, ALU.mult, ALU.add).then_inc(s_o, 1)
                        dve.wait_ge(s_o, g * 2 + 2)
                        ln_out.stats(Chain(dve, s_dve_out, g * Norm.STEPS), o[b % 2], g)

                    def finish(i, b, g):
                        ln_out.done(dve, g)
                        c = Chain(dve, s_fin, g * 2)
                        c.do(nc.vector.tensor_tensor(o[b % 2], o[b % 2], gb, ALU.mult))
                        c.wait()
                        c.do(nc.vector.tensor_tensor(o[b % 2], o[b % 2], bb, ALU.add))
                        c.wait()
                        nc.vector.tensor_tensor(o[b % 2], o[b % 2], got[b % TURN][:, G:2 * G, :], ALU.add
                                                ).then_inc(s_out, 1)

                    def slot(i, b, g):
                        if age(i, b, 0):
                            first(i, b, g)
                        if age(i, b, 1):
                            second(i, b - 1, g - 1)
                        if age(i, b, 0):
                            ln_in.shift(dve, g)
                        if age(i, b, 3):
                            finish(i, b - 3, g - 3)
                        if age(i, b, 2):
                            third(i, b - 2, g - 2)
                        if age(i, b, 1):
                            messages(i, b - 1, g - 1)
                        if age(i, b, 2):
                            ln_out.shift(dve, g - 2)

                    sums.start(dve)
                    stage(0, 0)
                    stage(1, 1)
                    slots(dve, slot)
                    dve.wait_ge(s_out, NG)

        DG = 2 * G
        ND = T // DG

        def between(update, final):
            ph.next()
            s_in = [ph.sem(f"b_in{b}") for b in range(2)]
            s_dve, s_cols, s_h, s_done = (ph.sem("b_" + n) for n in ("dve", "cols", "h", "done"))
            cursor[0] = 0
            cur = [take(DG, C) for _ in range(2)]
            y = [take(DG, C) for _ in range(2)]
            h = [take(DG, C) for _ in range(2)]
            isq, sqd, qsq = take(T), take(T), take(T)
            sidx = [take(DG, dt=I32) for _ in range(2)]
            ln = Norm("b", DG)
            vx = xd.rearrange("(g k p) d -> g p k d", k=DG, p=P)
            vt = table[0][0:E, :].rearrange("(g k p) d -> g p k d", k=DG, p=P)
            per = (2 if update else 0) + (0 if final else Norm.STEPS)
            stores = 16 * DG if final else 32 if update else 16
            put_out = [ph.landed(f"put{b}", stores * (ND // 2) if final else 0) for b in range(2)]
            s_st = [p.sem if final else ph.sem(f"b_st{b}") for b, p in enumerate(put_out)]
            at = [p.at if final else 0 for p in put_out]

            def pair(eng, body):
                def turn(i):
                    for b in range(2):
                        body(i, b, i * 2 + b)
                turns(eng, ND // 2, turn)

            with nc.Block() as block:
                @block.sync
                def _(sp):
                    ph.clear_previous(sp)

                    def load(i, b, g):
                        if later(i):
                            sp.wait_ge(s_st[b], i * stores + at[b])
                            sp.wait_ge(s_done, g - 1)
                        sp.dma_start(cur[b], vx[g]).then_inc(s_in[b], 16)
                    pair(sp, load)

                @block.vector
                def _(dve):
                    dve.wait_ge(s_cols, 1)
                    nc.vector.reciprocal(sqd, isq).then_inc(s_cols, 1)
                    nc.vector.tensor_scalar(qsq, isq, 0.25, None, ALU.mult).then_inc(s_cols, 1)
                    dve.wait_ge(s_cols, 3)

                    def front(i, b, g):
                        c = Chain(dve, s_dve, g * per)
                        cols = bass.ds(g * DG, DG)
                        dve.wait_ge(s_in[b], i * 16 + 16)
                        if update:
                            if later(i):
                                dve.wait_ge(s_done, g - 1)
                            if final and later(i):
                                dve.wait_ge(s_st[b], i * stores + at[b])
                            c.do(nc.vector.tensor_tensor(h[b], acc[:, cols, :], bcast(qsq[:, cols], C), ALU.mult))
                            if final:
                                c.do(nc.vector.tensor_scalar(sidx[b], scat_idx[:, 1, cols], 1.0, None, ALU.mult))
                                c.wait()
                                nc.vector.tensor_tensor(cur[b], cur[b], h[b], ALU.add).then_inc(s_done, 1)
                                return
                            c.wait()
                            c.do(nc.vector.tensor_tensor(cur[b], cur[b], h[b], ALU.add))
                            c.wait()
                        ln.stats(c, cur[b], g)
                        ln.shift(dve, g)

                    def back(i, b, g):
                        cols = bass.ds(g * DG, DG)
                        ln.done(dve, g)
                        if reused(i, b, 2):
                            dve.wait_ge(s_st[b % 2], i * stores + b // 2 * stores)
                        nc.vector.tensor_tensor(acc[:, cols, :], h[b % 2], bcast(sqd[:, cols], C), ALU.mult
                                                ).then_inc(s_h, 1)
                        nc.vector.tensor_tensor(y[b % 2], h[b % 2], bcast(isq[:, cols], C), ALU.mult
                                                ).then_inc(s_done, 1)

                    def group(i, b, g):
                        front(i, b, g)
                        if not final and reused(i, b, 1):
                            back(i, b - 1, g - 1)
                    pair(dve, group)
                    if not final:
                        back(ND // 2, -1, ND - 1)
                    dve.wait_ge(s_done, ND)

                @block.scalar
                def _(act):
                    nc.scalar.activation(isq, rdeg[:, 1, :], ACT.Sqrt).then_inc(s_cols, 1)

                    def store(b, g):
                        act.wait_ge(s_done, g + 1)
                        act.dma_start(vt[g], y[b]).then_inc(s_st[b], 16)
                        if update:
                            act.dma_start(vx[g], cur[b]).then_inc(s_st[b], 16)

                    def group(i, b, g):
                        ln.root(act, g)
                        if later(i):
                            act.wait_ge(s_done, g - 1)
                        ln.apply(act, cur[b], h[b], ACT.Relu, g)
                        if reused(i, b, 1):
                            store(1 - b, g - 1)
                    if not final:
                        pair(act, group)
                        store(1, ND - 1)
                        for b in range(2):
                            act.wait_ge(s_st[b], stores * (ND // 2))

                if final:
                    @block.gpsimd
                    def _(pool):
                        def scatter(i, b, g):
                            wait_apart(pool, ph.sem("passed_pool"), (s_done, g + 1))
                            for k in range(DG):
                                nc.gpsimd.indirect_dma_start(
                                    out, bass.IndirectOffsetOnAxis(ap=sidx[b][:, k:k + 1], axis=0),
                                    cur[b][:, k, :], None, bounds_check=NP - 1, oob_is_err=False).then_inc(s_st[b], 16)
                        pair(pool, scatter)
                        for b in range(2):
                            pool.wait_ge(s_st[b], put_out[b].end)

        keys()
        ranks()
        edge_mlp()
        offsets()
        records()
        columns()
        hop(0, x, hop1_idx, norm=True, fresh=True, to_table=table[0])
        hop(0, table[0], end_idx[:, 0, :], to_table=table[1])
        hop(0, table[1], end_idx[:, 0, :], to_nodes=z0)
        nodes_after_first()
        mlp_layer()
        for layer in (2, 3):
            between(layer == 3, False)
            hop(1, table[0], end_idx[:, 1, :], to_table=table[1], dense=0 if layer == 2 else 3)
            hop(1, table[1], end_idx[:, 1, :], to_table=table[0], dense=1 if layer == 2 else None)
            hop(1, table[0], end_idx[:, 1, :], dense=2 if layer == 2 else None)
        between(True, True)


def kernel(x, src, dst, edge_attr_32, L1_gnn_W1n, L1_gnn_b1n, L1_gnn_W2n, L1_gnn_b2n, L1_gnn_W1e, L1_gnn_b1e,
           L1_gnn_W2e, L1_gnn_b2e, L1_gnn_res_w, L1_gnn_dp_scale, L1_gnn_gamma, L1_gnn_beta):
    import numpy as np
    import concourse.bacc as bacc
    from concourse.bass_utils import run_bass_kernel_spmd

    def padded(a, n, fill):
        more = np.full((n - a.shape[0],) + a.shape[1:], fill, a.dtype)
        return np.concatenate([np.asarray(a), more], axis=0)

    arrays = {
        "x": padded(x, NP, 0),
        "src": padded(src, E, PADKEY),
        "dst": padded(dst, E, PADKEY),
        "attr_t": np.ascontiguousarray(padded(edge_attr_32, E, 0).T),
        "w1n": L1_gnn_W1n, "b1n": L1_gnn_b1n, "w2n": L1_gnn_W2n, "b2n": L1_gnn_b2n,
        "w1e": L1_gnn_W1e, "b1e": L1_gnn_b1e, "w2e": L1_gnn_W2e, "b2e": L1_gnn_b2e,
        "res_w": L1_gnn_res_w, "dp_scale": L1_gnn_dp_scale, "gamma": L1_gnn_gamma, "beta": L1_gnn_beta,
    }
    arrays = {f"in_{n}": np.ascontiguousarray(a) for n, a in arrays.items()}
    nc = bacc.Bacc("TRN2", target_bir_lowering=False, num_devices=1)
    args = [nc.dram_tensor(n, a.shape, mybir.dt.from_np(a.dtype), kind="ExternalInput").ap() for n, a in arrays.items()]
    args.append(nc.dram_tensor("nodes_out", (NP, C), F32, kind="ExternalOutput").ap())
    program(nc, *args)
    r = run_bass_kernel_spmd(nc, [arrays], core_ids=[0])
    return r.results[0]["nodes_out"][:N]
```

```python
from contextlib import ExitStack

import concourse.bass as bass
from concourse import mybir

F32 = mybir.dt.float32
I32 = mybir.dt.int32
ALU = mybir.AluOpType
ACT = mybir.ActivationFunctionType
AX_X = mybir.AxisListType.X

P = 128
C = 64
CE = 32
N = 100000
E0 = 50000
T = 392
E = T * P
NC = 784
NP = NC * P
PADKEY = NP - 1
G = 7
NG = T // G
GC = G * C
HALF = T // 2
ZROW = E
TROWS = E + P
SKIP = float(1 << 20)
EPS = 1e-5
SLOPE = 0.1
TB = 98
NTB = T // TB
DCH = 28
NDC = NC // DCH
DW = 8 + C
assert NG % 2 == 0 and NDC * DCH == NC and NTB * TB == T


class Phase:

    def __init__(self, nc, ctx):
        self.nc, self.ctx, self.sets, self.n, self.kept = nc, ctx, ([], []), -1, {}
        self.names, self.previous = {}, 0

    def next(self):
        self.n += 1
        self.previous = len(self.names)
        self.names = {}

    def sem(self, name):
        if name not in self.names:
            pool, k = self.sets[self.n % 2], len(self.names)
            if k == len(pool):
                pool.append(self.ctx.enter_context(self.nc.semaphore(f"phase{self.n % 2}_{k}")))
            self.names[name] = pool[k]
        return self.names[name]

    def landed(self, name, total):
        if name not in self.kept:
            self.kept[name] = Landed(self.ctx.enter_context(self.nc.semaphore(name)))
        return self.kept[name].next(total)

    def clear_previous(self, sp):
        for s in self.sets[1 - self.n % 2][:self.previous]:
            sp.sem_clear(s)


class Landed:

    def __init__(self, sem):
        self.sem, self.at, self.end = sem, 0, 0

    def next(self, total):
        self.at, self.end = self.end, self.end + total
        return self


def wait_apart(eng, passed, *waits):
    for sem, value in waits:
        eng.wait_ge(sem, value)
    eng.sem_inc(passed, 1)


class Chain:

    def __init__(self, eng, sem, base=0):
        self.eng, self.sem, self.base, self.n = eng, sem, base, 0

    def do(self, ins):
        ins.then_inc(self.sem, 1)
        self.n += 1

    def wait(self):
        self.eng.wait_ge(self.sem, self.base + self.n)


def turns(eng, n, body, last_apart=False):
    body(0)
    with eng.Fori(1, n - last_apart) as i:
        body(i)
    if last_apart:
        body(n - 1)


def later(i):
    return not isinstance(i, int) or i > 0


def reused(i, b, n):
    return later(i) or b >= n


def bcast(ap, n):
    return ap.unsqueeze(2).to_broadcast([ap.shape[0], ap.shape[1], n])


def program(nc, x, src, dst, attr_t, w1n, b1n, w2n, b2n, w1e, b1e, w2e, b2e, res_w, dp_scale, gamma, beta, out):
    with ExitStack() as ctx:
        def sb(name, shape, dt=F32):
            return ctx.enter_context(nc.sbuf_tensor(name, shape, dt))

        def psum(name, shape):
            return ctx.enter_context(nc.psum_tensor(name, shape, F32))

        def dram(name, shape):
            return nc.dram_tensor(name, shape, F32).ap()

        ph = Phase(nc, ctx)

        keyrow = [dram(f"keyrow{a}", [E]) for a in range(2)]
        count = [dram(f"count{j}", [NP, 1]) for j in range(4)]
        node_tab = dram("node_tab", [NP, 8])
        e_feat = dram("e_feat", [E, C])
        s_rec = dram("s_rec", [E, 8])
        d_rec = dram("d_rec", [E, DW])
        skey = [dram(f"skey{a}", [E]) for a in range(2)]
        joins = [dram(f"joins{a}", [E]) for a in range(2)]
        table = [dram(f"table{a}", [TROWS, C]) for a in range(2)]
        z0 = dram("z0", [NP, C])
        x1 = dram("x1", [NP, C])
        xd = dram("xd", [E, C])

        ident = sb("ident", [P, P])
        strict = sb("strict", [P, P])
        lower = sb("lower", [P, P])
        upper = sb("upper", [P, P])
        ones_row = sb("ones_row", [1, P])
        zeros = sb("zeros", [P, NC])
        res_col = sb("res_col", [P, 1])
        dp_col = sb("dp_col", [P, 1])
        gamma_b = sb("gamma_b", [P, C])
        beta_b = sb("beta_b", [P, C])

        key = sb("key", [P, 2, T])
        rank = sb("rank", [P, 2, T])
        after = sb("after", [P, 2, T])
        skey_col = sb("skey_col", [P, 2, T])
        rdeg = sb("rdeg", [P, 2, T])
        TS = T + 2 * G
        hop1_idx = sb("hop1_idx", [P, TS], I32)
        src_idx = sb("src_idx", [P, TS], I32)
        dst_idx = sb("dst_idx", [P, TS], I32)
        end_idx = sb("end_idx", [P, 2, TS], I32)
        scat_idx = sb("scat_idx", [P, 2, TS], I32)

        acc = sb("acc", [P, T, C])
        WORK = 14600
        work = sb("work", [P, WORK])
        cursor = [0]

        def take(*shape, dt=F32, parts=P, first=0):
            n = 1
            for s in shape:
                n *= s
            a = work[first:parts, cursor[0]:cursor[0] + n]
            cursor[0] += n
            assert cursor[0] <= WORK, cursor[0]
            if dt != F32:
                a = a.bitcast(dt)
            if len(shape) == 2:
                a = a.rearrange("p (a b) -> p a b", a=shape[0])
            if len(shape) == 3:
                a = a.rearrange("p (a b c) -> p a b c", a=shape[0], b=shape[1])
            return a

        bank = [psum(f"bank{k}", [P, 512]) for k in range(8)]

        class Norm:

            def __init__(self, name, n):
                self.n = n
                self.s_var, self.s_root, self.s_shift, self.s_out = (
                    ph.sem(f"{name}_{what}") for what in ("var", "root", "shift", "out"))
                self.bs, self.m, self.d, self.r, self.b = take(n, 6), take(n), take(n), take(n), take(n)

            def stats(self, c, rows, k):
                if not isinstance(k, int) or k:
                    c.eng.wait_ge(self.s_out, k)
                for j in range(self.n):
                    ins = nc.vector.bn_stats(self.bs[:, j, :], rows[:, j, :])
                c.do(ins)
                c.wait()
                bs = self.bs
                c.do(nc.vector.tensor_tensor(self.m, bs[:, :, 1], bs[:, :, 4], ALU.add))
                c.do(nc.vector.tensor_tensor(self.d, bs[:, :, 1], bs[:, :, 4], ALU.subtract))
                c.do(nc.vector.tensor_tensor(self.r, bs[:, :, 2], bs[:, :, 5], ALU.add))
                c.wait()
                c.do(nc.vector.scalar_tensor_tensor(self.d, self.d, 0.25, self.d, ALU.mult, ALU.mult))
                c.do(nc.vector.tensor_scalar(self.r, self.r, 1.0 / C, EPS, ALU.mult, ALU.add))
                c.wait()
                c.do(nc.vector.tensor_tensor(self.r, self.r, self.d, ALU.add))
                c.wait()
                nc.vector.reciprocal(self.r, self.r).then_inc(self.s_var, 1)

            STEPS = 7

            def root(self, act, k):
                act.wait_ge(self.s_var, k + 1)
                nc.scalar.activation(self.r, self.r, ACT.Sqrt).then_inc(self.s_root, 1)

            def shift(self, dve, k):
                dve.wait_ge(self.s_root, k + 1)
                nc.vector.scalar_tensor_tensor(self.b, self.m, -0.5, self.r, ALU.mult, ALU.mult
                                               ).then_inc(self.s_shift, 1)

            def apply(self, act, rows, to, func, k, cols=None):
                cols = range(self.n) if cols is None else cols
                if cols[0] == 0:
                    act.wait_ge(self.s_shift, k + 1)
                for j in cols:
                    ins = nc.scalar.activation(to[:, j, :], rows[:, j, :], func, scale=self.r[:, j:j + 1],
                                               bias=self.b[:, j:j + 1])
                if cols[-1] == self.n - 1:
                    ins.then_inc(self.s_out, 1)
                return ins

            def done(self, eng, k):
                eng.wait_ge(self.s_out, k + 1)

        def keys():
            ph.next()
            s_in, s_conv, s_turn, s_col, s_row = (ph.sem(n) for n in ("k_in", "k_conv", "k_turn", "k_col", "k_row"))
            s_zero, s_clear, s_const, s_par = (ph.sem(n) for n in ("k_zero", "k_clear", "k_const", "k_par"))
            cursor[0] = 0
            raw = take(2, NTB * P, dt=I32, parts=TB)
            rowf = take(2, NTB * P, parts=TB)
            with nc.Block() as block:
                @block.sync
                def _(sp):
                    ph.clear_previous(sp)
                    for a, arr in enumerate((src, dst)):
                        sp.dma_start(raw[:, a, :].rearrange("p (b e) -> p b e", b=NTB),
                                     arr.rearrange("(b p e) -> p b e", b=NTB, p=TB)).then_inc(s_in, 16)
                    sp.dma_start(res_col[:], res_w.unsqueeze(0).to_broadcast([P, 1])).then_inc(s_par, 16)
                    sp.dma_start(dp_col[:], dp_scale.unsqueeze(0).to_broadcast([P, 1])).then_inc(s_par, 16)
                    sp.dma_start(gamma_b[:], gamma.unsqueeze(0).to_broadcast([P, C])).then_inc(s_par, 16)
                    sp.dma_start(beta_b[:], beta.unsqueeze(0).to_broadcast([P, C])).then_inc(s_par, 16)
                    sp.wait_ge(s_zero, 1)
                    for t in count:
                        sp.dma_start(t.rearrange("(p c) o -> p (c o)", p=P), zeros[:]).then_inc(s_clear, 16)
                    for t in table:
                        sp.dma_start(t[ZROW:ZROW + P, :], zeros[:, 0:C]).then_inc(s_clear, 16)
                    sp.wait_ge(s_conv, 2)
                    for a in range(2):
                        sp.dma_start(keyrow[a].rearrange("(b p e) -> p b e", b=NTB, p=TB),
                                     rowf[:, a, :].rearrange("p (b e) -> p b e", b=NTB)).then_inc(s_row, 16)
                    sp.wait_ge(s_row, 32)
                    sp.wait_ge(s_clear, 96)
                    sp.wait_ge(s_par, 64)

                @block.gpsimd
                def _(pool):
                    nc.gpsimd.memset(zeros[:], 0.0).then_inc(s_zero, 1)
                    nc.gpsimd.memset(ident[:], 0.0).then_inc(s_const, 1)
                    for m in (strict, lower, upper, ones_row):
                        nc.gpsimd.memset(m[:], 1.0).then_inc(s_const, 1)
                    pool.wait_ge(s_const, 5)
                    for m, op, fill in ((ident, ALU.not_equal, 1.0), (strict, ALU.is_gt, 0.0)):
                        nc.gpsimd.affine_select(out=m[:], in_=m[:], compare_op=op, fill=fill, base=0,
                                                pattern=[[1, P]], channel_multiplier=-1).then_inc(s_const, 1)
                    nc.gpsimd.affine_select(out=upper[:], in_=upper[:], compare_op=ALU.is_gt, fill=0.0, base=0,
                                            pattern=[[1, P]], channel_multiplier=-1).then_inc(s_const, 1)
                    nc.gpsimd.affine_select(out=lower[:], in_=lower[:], compare_op=ALU.is_gt, fill=0.0, base=0,
                                            pattern=[[-1, P]], channel_multiplier=1).then_inc(s_const, 1)
                    pool.wait_ge(s_const, 9)

                @block.vector
                def _(dve):
                    dve.wait_ge(s_in, 32)
                    for a in range(2):
                        nc.vector.tensor_copy(rowf[:, a, :], raw[:, a, :]).then_inc(s_conv, 1)
                    for a in range(2):
                        dve.wait_ge(s_turn, NTB * (a + 1))
                        nc.vector.tensor_copy(key[:, a, :], bank[a][:, 0:T]).then_inc(s_col, 1)
                    dve.wait_ge(s_col, 2)

                @block.tensor
                def _(pe):
                    pe.wait_ge(s_conv, 2)
                    pe.wait_ge(s_const, 9)
                    for a in range(2):
                        for b in range(NTB):
                            nc.tensor.transpose(bank[a][:, b * TB:(b + 1) * TB], rowf[:, a, b * P:(b + 1) * P],
                                                ident[0:TB, 0:TB]).then_inc(s_turn, 1)

        def ranks():
            ph.next()
            s_row = [ph.sem(f"r_row{b}") for b in range(2)]
            s_pair, s_gidx, s_last, s_sidx, s_rank, s_clear = (
                ph.sem(n) for n in ("r_pair", "r_gidx", "r_last", "r_sidx", "r_rank", "r_clear"))
            s_w, s_at, s_hid, s_z, s_zb, s_mm, s_ft, s_est = (
                ph.sem(n) for n in ("e_w", "e_at", "e_hid", "e_z", "e_zb", "e_mm", "e_ft", "e_stored"))
            got_in = [ph.landed(f"r_got{j}", 16 * HALF) for j in range(4)]
            s_new = [ph.sem(f"r_new{j}") for j in range(4)]
            put_out = [ph.landed(f"r_put{j}", 16 * HALF) for j in range(4)]
            cursor[0] = 0
            kr = take(2, 4, P)
            junk = take(8, P)
            gidx = take(2, 4, dt=I32)
            sidx = take(2, 4, dt=I32)
            last = take(2, 4)
            got = take(2, 4)
            val = take(2, 4)
            RT = HALF // 2
            EG = T // RT
            assert EG * RT == T and EG * P <= 512
            w1, w2, b1, b2 = take(C, parts=CE), take(C, parts=C), take(1, parts=C), take(C, parts=1)
            at = take(EG * P, parts=CE)
            zb = take(EG * P, parts=C)
            hid = take(EG * P, parts=C)
            ft = take(EG, C)
            e_view = e_feat.rearrange("(g k p) d -> g p k d", k=EG, p=P)
            keyc, rankc, afterc = (t.rearrange("p a (h s) -> p a h s", h=2) for t in (key, rank, after))

            def four(t):
                return t.rearrange("p (a h o) -> p a h o", a=2, h=2)

            with nc.Block() as block:
                @block.sync
                def _(sp):
                    ph.clear_previous(sp)

                    def load(i, b):
                        if later(i):
                            sp.wait_ge(s_pair, i * 16 + 8 * b - 8)
                        for a in range(2):
                            for h in range(2):
                                sp.dma_start(kr[:, b, 2 * a + h, :],
                                             keyrow[a].rearrange("(h s e) -> h s e", h=2, e=P)
                                             [h, bass.ds(i * 2 + b, 1), :].to_broadcast([P, P])
                                             ).then_inc(s_row[b], 16)

                    sp.dma_start(w1, w1e).then_inc(s_w, 16)
                    sp.dma_start(w2, w2e).then_inc(s_w, 16)
                    sp.dma_start(b1, b1e.unsqueeze(1)).then_inc(s_w, 16)
                    sp.dma_start(b2, b2e.unsqueeze(0)).then_inc(s_w, 16)

                    def both(i):
                        load(i, 0)
                        if later(i):
                            sp.wait_ge(s_z, i)
                        sp.dma_start(at, attr_t[:, bass.ds(i * (EG * P), EG * P)]).then_inc(s_at, 16)
                        load(i, 1)
                    turns(sp, RT, both)

                @block.tensor
                def _(pe):
                    pe.wait_ge(s_w, 64)

                    def products(i):
                        pe.wait_ge(s_at, i * 16 + 16)
                        if later(i):
                            pe.wait_ge(s_zb, i)
                        nc.tensor.matmul(bank[0][0:C, 0:EG * P], w1, at, start=True, stop=True).then_inc(s_z, 1)
                        pe.wait_ge(s_hid, i + 1)
                        if later(i):
                            pe.wait_ge(s_ft, i)
                        for k in range(EG):
                            o = bank[1][:, k * C:(k + 1) * C]
                            nc.tensor.matmul(o, hid[:, k * P:(k + 1) * P], w2, start=True, stop=False)
                            mm = nc.tensor.matmul(o, ones_row[:], b2, start=False, stop=True)
                        mm.then_inc(s_mm, 1)
                    turns(pe, RT, products)

                @block.scalar
                def _(act):
                    z = z0.rearrange("(p c) d -> p (c d)", p=P)
                    for k in range(C):
                        act.dma_start(z[:, k * NC:(k + 1) * NC], zeros[:]).then_inc(s_clear, 16)
                    act.wait_ge(s_w, 64)

                    def features(i):
                        act.wait_ge(s_z, i + 1)
                        if later(i):
                            act.wait_ge(s_hid, i)
                        nc.scalar.activation(zb, bank[0][0:C, 0:EG * P], ACT.Identity, bias=b1).then_inc(s_zb, 1)
                        act.wait_ge(s_mm, i + 1)
                        if later(i):
                            act.wait_ge(s_est, i * 16)
                        nc.scalar.activation(ft.rearrange("p k d -> p (k d)"), bank[1][:, 0:EG * C], ACT.Copy,
                                             scale=dp_col[:]).then_inc(s_ft, 1)
                        act.wait_ge(s_ft, i + 1)
                        act.dma_start(e_view[i], ft).then_inc(s_est, 16)
                    turns(act, RT, features)
                    act.wait_ge(s_est, 16 * RT)
                    act.wait_ge(s_clear, 16 * C)

                @block.gpsimd
                def _(pool):
                    passed = ph.sem("passed_pool")

                    def step(i, b):
                        s = i * 2 + b
                        wait_apart(pool, passed, (s_gidx, s + 1))
                        for j in range(4):
                            if reused(i, b, 1):
                                wait_apart(pool, passed, (put_out[j].sem, s * 16))
                            nc.gpsimd.indirect_dma_start(
                                got[:, b, j:j + 1], None, count[j],
                                bass.IndirectOffsetOnAxis(ap=gidx[:, b, j:j + 1], axis=0)).then_inc(got_in[j].sem, 16)
                        for j in range(4):
                            wait_apart(pool, passed, (s_new[j], s + 1), (s_sidx, s + 1))
                            nc.gpsimd.indirect_dma_start(
                                count[j], bass.IndirectOffsetOnAxis(ap=sidx[:, b, j:j + 1], axis=0),
                                val[:, b, j:j + 1], None, bounds_check=NP - 1, oob_is_err=False
                            ).then_inc(put_out[j].sem, 16)

                    def both(i):
                        step(i, 0)
                        step(i, 1)
                    turns(pool, HALF // 2, both)
                    for j in range(4):
                        pool.wait_ge(put_out[j].sem, 16 * HALF)

                @block.vector
                def _(dve):
                    def pairs(s, uses, b, first):
                        dve.wait_ge(s_row[b], uses * 64)
                        col = bass.ds(s, 1)
                        for j in range(4):
                            a, h = j // 2, j % 2
                            for m, to, k in ((lower, rankc, 0), (upper, afterc, 1)):
                                nc.vector.scalar_tensor_tensor(
                                    junk[:, 2 * j + k, :], kr[:, b, j, :], keyc[:, a, h, col], m[:], ALU.is_equal,
                                    ALU.mult, accum_out=to[:, a, h, col]).then_inc(s_pair, 1)
                        dve.wait_ge(s_pair, s * 8 + 8)
                        if not first:
                            for j in range(4):
                                dve.wait_ge(put_out[j].sem, s * 16 - 16)
                        nc.vector.tensor_scalar(four(gidx[:, b, :]), keyc[:, :, :, col], 1.0, None, ALU.mult
                                                ).then_inc(s_gidx, 1)
                        nc.vector.tensor_scalar(four(last[:, b, :]), afterc[:, :, :, col], 1.0, SKIP, ALU.min,
                                                ALU.mult).then_inc(s_last, 1)
                        dve.wait_ge(s_last, s + 1)
                        nc.vector.tensor_tensor(four(sidx[:, b, :]), four(last[:, b, :]), keyc[:, :, :, col],
                                                ALU.add).then_inc(s_sidx, 1)

                    def update(s, b):
                        col = bass.ds(s, 1)
                        for j in range(4):
                            dve.wait_ge(got_in[j].sem, s * 16 + 16)
                            nc.vector.scalar_tensor_tensor(
                                val[:, b, j:j + 1], got[:, b, j:j + 1], 1.0, rankc[:, j // 2, j % 2, col],
                                ALU.add, ALU.add).then_inc(s_new[j], 1)
                        dve.wait_ge(s_new[3], s + 1)
                        nc.vector.tensor_tensor(rankc[:, :, :, col], rankc[:, :, :, col], four(got[:, b, :]),
                                                ALU.add).then_inc(s_rank, 1)

                    def leaky(i):
                        dve.wait_ge(s_zb, i + 1)
                        if later(i):
                            dve.wait_ge(s_mm, i)
                        nc.vector.scalar_tensor_tensor(hid, zb, SLOPE, zb, ALU.mult, ALU.max).then_inc(s_hid, 1)

                    pairs(0, 1, 0, True)
                    pairs(1, 1, 1, True)
                    leaky(0)
                    update(0, 0)
                    with dve.Fori(1, RT) as i:
                        pairs(i * 2, i + 1, 0, False)
                        update(i * 2 - 1, 1)
                        pairs(i * 2 + 1, i + 1, 1, False)
                        leaky(i)
                        update(i * 2, 0)
                    update(HALF - 1, 1)
                    dve.wait_ge(s_rank, HALF)

        def offsets():
            ph.next()
            s_in, s_dve, s_pe, s_out = (ph.sem(n) for n in ("o_in", "o_dve", "o_pe", "o_out"))
            cursor[0] = 0
            cnt = take(4, NC)
            tab = take(NC, 8)
            scan = [acc[:].rearrange("p t d -> p (t d)")[:, k * 2 * NC:(k + 1) * 2 * NC]
                    .rearrange("p (a c) -> p a c", a=2) for k in range(3)]
            with nc.Block() as block:
                @block.sync
                def _(sp):
                    ph.clear_previous(sp)
                    for j in range(4):
                        sp.dma_start(cnt[:, j, :], count[j].rearrange("(p c) o -> p (c o)", p=P)).then_inc(s_in, 16)
                    sp.wait_ge(s_dve, 18)
                    sp.dma_start(node_tab.rearrange("(p c) f -> p c f", p=P), tab).then_inc(s_out, 16)
                    sp.wait_ge(s_out, 16)

                @block.tensor
                def _(pe):
                    pe.wait_ge(s_dve, 12)
                    nc.tensor.matmul(bank[0][:, 0:2], strict[:], scan[1][:, :, NC - 1], start=True, stop=True
                                     ).then_inc(s_pe, 1)

                @block.vector
                def _(dve):
                    c = Chain(dve, s_dve)
                    dve.wait_ge(s_in, 64)
                    halves = cnt.rearrange("p (a h) c -> p a h c", a=2)
                    deg, cur, nxt = scan[0], scan[1], scan[2]
                    c.do(nc.vector.tensor_tensor(deg, halves[:, :, 0, :], halves[:, :, 1, :], ALU.add))
                    c.wait()
                    src_, k = deg, 1
                    steps = []
                    while k < NC:
                        steps.append(k)
                        k *= 2
                    assert len(steps) == 10
                    dst_ = nxt
                    for k in steps:
                        nc.vector.tensor_copy(dst_[:, :, 0:k], src_[:, :, 0:k])
                        c.do(nc.vector.tensor_tensor(dst_[:, :, k:NC], src_[:, :, k:NC], src_[:, :, 0:NC - k], ALU.add))
                        c.wait()
                        src_, dst_ = dst_, (cur if dst_ is nxt else nxt)
                    assert src_ is cur
                    c.do(nc.vector.memset(tab[:, :, 6:8], 0.0))
                    t2 = tab.rearrange("p c f -> p f c")
                    dve.wait_ge(s_pe, 1)
                    for a in range(2):
                        c.do(nc.vector.scalar_tensor_tensor(t2[:, 3 * a, :], cur[:, a, :], bank[0][:, a:a + 1],
                                                            deg[:, a, :], ALU.add, ALU.subtract))
                        c.do(nc.vector.tensor_copy(t2[:, 3 * a + 1, :], cnt[:, 2 * a, :]))
                        c.do(nc.vector.tensor_copy(t2[:, 3 * a + 2, :], deg[:, a, :]))
                    assert c.n == 18, c.n

        def records():
            ph.next()
            s_dve, s_stage, s_ready, s_fill = (ph.sem(n) for n in ("d_dve", "d_stage", "d_ready", "d_fill"))
            s_feat = [ph.sem(f"d_feat{b}") for b in range(2)]
            got_in = [ph.landed(f"d_got{b}", 16 * G * NG) for b in range(2)]
            put_out = [ph.landed(f"d_put{b}", 16 * G * NG) for b in range(2)]
            cursor[0] = 0
            gidx = [take(2, G, dt=I32) for _ in range(2)]
            pidx = [take(2, G, dt=I32) for _ in range(2)]
            got = [take(2, G, 8) for _ in range(2)]
            srec = [take(G, 8) for _ in range(2)]
            drec = [take(G, DW) for _ in range(2)]
            pos = take(G)
            lastp = take(G)
            e_view = e_feat.rearrange("(g k p) d -> g p k d", k=G, p=P)
            with nc.Block() as block:
                @block.sync
                def _(sp):
                    ph.clear_previous(sp)

                    def load(i):
                        for b in range(2):
                            if later(i):
                                sp.wait_ge(put_out[b].sem, i * (16 * 2 * G))
                            sp.dma_start(drec[b][:, :, 8:DW], e_view[i * 2 + b]).then_inc(s_feat[b], 16)
                    turns(sp, NG // 2, load)

                @block.gpsimd
                def _(pool):
                    def both(i):
                        for b in range(2):
                            wait_apart(pool, ph.sem("passed_pool"), (s_stage, i * 2 + b + 1),
                                       *([(s_ready, i * 2 + b - 1)] if later(i) else []))
                            for a in range(2):
                                for k in range(G):
                                    nc.gpsimd.indirect_dma_start(
                                        got[b][:, a, k, :], None, node_tab,
                                        bass.IndirectOffsetOnAxis(ap=gidx[b][:, a, k:k + 1], axis=0)
                                    ).then_inc(got_in[b].sem, 16)
                        for b in range(2):
                            wait_apart(pool, ph.sem("passed_pool"), (s_feat[b], i * 16 + 16), (s_ready, i * 2 + b + 1))
                            for k in range(G):
                                nc.gpsimd.indirect_dma_start(
                                    s_rec, bass.IndirectOffsetOnAxis(ap=pidx[b][:, 0, k:k + 1], axis=0),
                                    srec[b][:, k, :], None).then_inc(put_out[b].sem, 16)
                                nc.gpsimd.indirect_dma_start(
                                    d_rec, bass.IndirectOffsetOnAxis(ap=pidx[b][:, 1, k:k + 1], axis=0),
                                    drec[b][:, k, :], None).then_inc(put_out[b].sem, 16)
                    turns(pool, NG // 2, both)
                    for b in range(2):
                        pool.wait_ge(put_out[b].sem, 16 * 2 * G * (NG // 2))

                @block.vector
                def _(dve):
                    def stage(g, b):
                        nc.vector.tensor_scalar(gidx[b], key[:, :, bass.ds(g * G, G)], 1.0, None, ALU.mult
                                                ).then_inc(s_stage, 1)

                    def group(i, b, half, n0, again):
                        c = Chain(dve, s_dve, n0)
                        g = i * 2 + b
                        cols = bass.ds(g * G, G)
                        dve.wait_ge(got_in[b].sem, i * (16 * 2 * G) + 16 * 2 * G)
                        if again:
                            stage(g + 2, b)
                        if later(i):
                            dve.wait_ge(put_out[b].sem, i * (16 * 2 * G))
                        for a, rec in ((0, srec[b]), (1, drec[b])):
                            own = got[b][:, a, :, 3 * a:3 * a + 3]
                            oth = got[b][:, 1 - a, :, 3 * a:3 * a + 3]
                            f = rec[:, :, 0:8]
                            c.do(nc.vector.tensor_scalar(f[:, :, 0], key[:, a, cols], 1.0, None, ALU.mult))
                            c.do(nc.vector.tensor_copy(f[:, :, 1], own[:, :, 2]))
                            c.do(nc.vector.tensor_copy(f[:, :, 2], key[:, 1 - a, cols]))
                            c.do(nc.vector.tensor_tensor(pos, own[:, :, 0], rank[:, a, cols], ALU.add))
                            c.wait()
                            if half:
                                c.do(nc.vector.tensor_tensor(pos, pos, own[:, :, 1], ALU.add))
                                c.wait()
                            c.do(nc.vector.tensor_copy(pidx[b][:, a, :], pos))
                            c.do(nc.vector.scalar_tensor_tensor(lastp, own[:, :, 0], -1.0, own[:, :, 2], ALU.add,
                                                                ALU.add))
                            c.wait()
                            c.do(nc.vector.tensor_tensor(lastp, lastp, pos, ALU.not_equal))
                            c.wait()
                            c.do(nc.vector.scalar_tensor_tensor(f[:, :, 4], lastp, SKIP, key[:, a, cols], ALU.mult,
                                                                ALU.add))
                            c.do(nc.vector.scalar_tensor_tensor(f[:, :, 3], oth[:, :, 0], -1.0 - ZROW, oth[:, :, 2],
                                                                ALU.add, ALU.add))
                            c.do(nc.vector.tensor_scalar(f[:, :, 5], oth[:, :, 2], 1.0, None, ALU.min))
                            c.wait()
                            c.do(nc.vector.tensor_tensor(f[:, :, 3], f[:, :, 3], f[:, :, 5], ALU.mult))
                            c.wait()
                            row = nc.vector.tensor_scalar(f[:, :, 3], f[:, :, 3], float(ZROW), None, ALU.add)
                            if a == 0:
                                c.do(row)
                                c.wait()
                            else:
                                row.then_inc(s_ready, 1)
                        return c.n

                    for b in range(2):
                        nc.vector.memset(srec[b][:, :, 6:8], 0.0).then_inc(s_fill, 1)
                        nc.vector.memset(drec[b][:, :, 6:8], 0.0).then_inc(s_fill, 1)
                    dve.wait_ge(s_fill, 4)
                    stage(0, 0)
                    stage(1, 1)
                    per = [23, 25]
                    mid = NG // 4

                    def both(half, i0):
                        def body(i):
                            for b in range(2):
                                n0 = (i - i0) * (2 * per[half]) + (mid * 2 * per[0] if half else 0) + b * per[half]
                                n = group(i, b, half, n0, True)
                                assert n == per[half], n
                        return body
                    both(0, 0)(0)
                    with dve.Fori(1, mid) as i:
                        both(0, 0)(i)
                    with dve.Fori(mid, NG // 2 - 1) as i:
                        both(1, mid)(i)
                    for b in range(2):
                        i = NG // 2 - 1
                        n = group(i, b, 1, (i - mid) * 2 * per[1] + mid * 2 * per[0] + b * per[1], False)
                        assert n == per[1], n

        def columns():
            ph.next()
            s_in, s_dve, s_turn, s_rows, s_put, s_ft, s_z, s_same = (
                ph.sem(n) for n in ("c_in", "c_dve", "c_turn", "c_rows", "c_put", "c_ft", "c_z", "c_same"))
            cursor[0] = 0
            flat = acc[:].rearrange("p t d -> p (t d)")
            meta = [flat[:, a * T * 8:(a + 1) * T * 8].rearrange("p (t f) -> p t f", f=8) for a in range(2)]
            rows = take(2, NTB * P, parts=TB)
            ends = take(2, NTB, parts=TB)
            same = take(2, NTB * P, parts=TB)
            with nc.Block() as block:
                @block.sync
                def _(sp):
                    ph.clear_previous(sp)
                    for m, r in zip(meta, (s_rec, d_rec)):
                        sp.dma_start(m[:, :, 0:5], r[:, 0:5].rearrange("(t p) f -> p t f", p=P)).then_inc(s_in, 16)
                    sp.wait_ge(s_rows, 2 * NTB)
                    for a in range(2):
                        sp.dma_start(skey[a].rearrange("(b p e) -> p b e", b=NTB, p=TB),
                                     rows[:, a, :].rearrange("p (b e) -> p b e", b=NTB)).then_inc(s_put, 16)
                    sp.wait_ge(s_put, 32)
                    sp.wait_ge(s_z, 1)
                    for a in range(2):
                        v = skey[a].rearrange("(t e) -> t e", e=P)
                        for b in range(NTB):
                            lo = 1 if b == 0 else 0
                            sp.dma_start(ends[lo:TB, a, b:b + 1], v[b * TB + lo - 1:(b + 1) * TB - 1, P - 1:P],
                                         allow_slow_non_contiguous=True).then_inc(s_ft, 16)
                    sp.wait_ge(s_same, 2)
                    for a in range(2):
                        sp.dma_start(joins[a].rearrange("(b p e) -> p b e", b=NTB, p=TB),
                                     same[:, a, :].rearrange("p (b e) -> p b e", b=NTB)).then_inc(s_put, 16)
                    sp.wait_ge(s_put, 64)

                @block.tensor
                def _(pe):
                    pe.wait_ge(s_dve, 2)
                    for a in range(2):
                        for b in range(NTB):
                            nc.tensor.transpose(bank[4 * a + b][0:TB, 0:P], skey_col[:, a, b * TB:(b + 1) * TB],
                                                ident[:]).then_inc(s_turn, 1)

                @block.vector
                def _(dve):
                    c = Chain(dve, s_dve)
                    dve.wait_ge(s_in, 32)
                    for a in range(2):
                        c.do(nc.vector.tensor_copy(skey_col[:, a, :], meta[a][:, :, 0]))
                    nc.vector.memset(ends, -1.0).then_inc(s_z, 1)
                    for a in range(2):
                        c.do(nc.vector.reciprocal(rdeg[:, a, :], meta[a][:, :, 1]))
                        c.do(nc.vector.tensor_copy((hop1_idx, src_idx)[a][:, 0:T], meta[a][:, :, 2]))
                        c.do(nc.vector.tensor_copy(end_idx[:, a, 0:T], meta[a][:, :, 3]))
                        c.do(nc.vector.tensor_copy(scat_idx[:, a, 0:T], meta[a][:, :, 4]))
                        for t in (end_idx[:, a, :], scat_idx[:, a, :], (hop1_idx, src_idx)[a][:, :]):
                            c.do(nc.vector.memset(t[:, T:TS], 0))
                    c.do(nc.vector.tensor_copy(dst_idx[:, 0:T], meta[1][:, :, 0]))
                    c.do(nc.vector.memset(dst_idx[:, T:TS], 0))
                    for a in range(2):
                        for b in range(NTB):
                            dve.wait_ge(s_turn, a * NTB + b + 1)
                            nc.vector.tensor_copy(rows[:, a, b * P:(b + 1) * P], bank[4 * a + b][0:TB, 0:P]
                                                  ).then_inc(s_rows, 1)
                    dve.wait_ge(s_ft, 16 * 2 * NTB)
                    for a in range(2):
                        nc.vector.tensor_tensor(
                            *(t[:, a, :].rearrange("p (b e) -> p b e", b=NTB) for t in (same, rows)),
                            bcast(ends[:, a, :], P), ALU.is_equal).then_inc(s_same, 1)
                    c.wait()

        def select(a, g, kr, sel, s_sel):
            nc.vector.tensor_tensor(sel, kr, bcast(skey_col[:, a, bass.ds(g * G, G)], P), ALU.is_equal
                                    ).then_inc(s_sel, 1)

        def load_keys(sp, a, g, keys_all, sem):
            sp.dma_start(keys_all.rearrange("p k e -> p (k e)"),
                         skey[a].unsqueeze(0)[:, bass.ds(g * (G * P), G * P)].to_broadcast([P, G * P])
                         ).then_inc(sem, 16)

        class Sums:

            TOP = P - 32

            def __init__(self, name, a, pairs):
                self.a, self.pairs = a, pairs
                self.s_tile, self.s_in, self.s_zero = (ph.sem(f"{name}_{what}") for what in ("tile", "handed", "zero"))
                self.s_join = [ph.sem(f"{name}_join{b}") for b in range(2)]
                self.inn = [take(C, parts=P, first=self.TOP) for _ in range(2)]
                start = cursor[0]
                self.join = [take(G, P, parts=P, first=self.TOP) for _ in range(2)]
                self.join_row = [work[P - 1:P, start + b * G * P:start + (b + 1) * G * P] for b in range(2)]

            def start(self, dve):
                for t in self.join:
                    nc.vector.memset(t, 0.0).then_inc(self.s_zero, 1)

            def load(self, sp, i, b, g):
                if reused(i, b, 2):
                    sp.wait_ge(*self.summed(g - 1))
                elif b == 0:
                    sp.wait_ge(self.s_zero, 2)
                sp.dma_start(self.join_row[b % 2], joins[self.a].unsqueeze(0)[:, bass.ds(g * (G * P), G * P)]
                             ).then_inc(self.s_join[b % 2], 16)

            def out(self, b, k):
                two = self.pairs[b % len(self.pairs)]
                return bank[two[k % 2]][:, (k // 2) * C:(k // 2 + 1) * C]

            def halves(self, b, g, *arrays):
                for c in range(2):
                    n = (G + 1 - c) // 2
                    ps = bank[self.pairs[b % len(self.pairs)][c]][:, 0:n * C].rearrange("p (k d) -> p k d", k=n)
                    yield (ps, *arrays_of(arrays, g, c, n))

            def add_up(self, pe, i, b, g, sel, rows):
                pe.wait_ge(self.s_join[b % 2], i * (TURN // 2 * 16) + (b // 2 * 16 + 16))
                for k in range(G):
                    t, o = g * G + k, self.out(b, k)
                    before = reused(i, b, 1) or k > 0
                    if before and k == 0 and len(self.pairs) == 1:
                        wait_apart(pe, ph.sem("passed_pe"), (self.s_in, t))
                    ins = nc.tensor.matmul(o, sel[:, k, :], rows[:, k, :], start=True, stop=not before)
                    if before:
                        pe.wait_ge(self.s_in, t)
                        ins = nc.tensor.matmul(o, self.join[b % 2][:, k, :], self.inn[(b + k + 1) % 2], start=False,
                                               stop=True)
                    ins.then_inc(self.s_tile, 1)

            def hand_on(self, act, i, b, g, k):
                if reused(i, b, 1) or k:
                    act.wait_ge(self.s_tile, g * G + k)
                    o = self.out(b, k - 1) if k else self.out(b - 1, G - 1)
                    nc.scalar.activation(self.inn[(b + k + 1) % 2], o[self.TOP:P, :], ACT.Copy).then_inc(self.s_in, 1)

            def summed(self, n):
                return self.s_in, n * G

        def arrays_of(arrays, g, c, n):
            for t in arrays:
                if g is None:
                    yield t[:, c:G:2, ...]
                else:
                    yield t[:, bass.ds(g * G + c, n, 2), ...]

        NB = 4
        TURN = 8
        NT = NG // TURN
        DH = DCH // 2
        assert NT * TURN == NG and NDC == 4 * NT and DH == 2 * G

        def hop(a, source, idx, norm=False, fresh=False, to_table=None, to_nodes=None, dense=None):
            ph.next()
            s_kr = [ph.sem(f"h_kr{b}") for b in range(2)]
            got_in = [ph.landed(f"got{b}", 16 * G * (NG // NB)) for b in range(NB)]
            s_st = [ph.sem(f"h_st{b}") for b in range(2)]
            put_out = [ph.landed(f"put{b}", 16 * G * (NG // 2) if to_nodes is not None else 0) for b in range(2)]
            s_dve, s_stage, s_sel, s_tab, s_acc, s_scat, s_sidx = (
                ph.sem(n) for n in ("h_dve", "h_stage", "h_sel", "h_tab", "h_acc", "h_scat", "h_sidx"))
            s_nin, s_nfree, s_ndone, s_nout, s_ndve = (
                [ph.sem(f"{n}{f}") for f in range(2)] for n in ("n_in", "n_free", "n_done", "n_stored", "n_dve"))
            cursor[0] = 0
            got = [take(G, C) for _ in range(NB)]
            gidx = [take(G, dt=I32) for _ in range(NB)]
            kr = [take(G, P) for _ in range(2)]
            sel = [take(G, P) for _ in range(2)]
            tb = [take(G, C) for _ in range(2)]
            sidx = [take(G, dt=I32) for _ in range(2)]
            sums = Sums("h", a, [(2 * b, 2 * b + 1) for b in range(NB)])
            ln = Norm("h", G) if norm else None
            if dense is not None:
                cur, h, res = ([take(DH, C) for _ in range(2)] for _ in range(3))
                nln = [Norm(f"nl{f}", DH) for f in range(2)]
                gb, bb = (t[:].unsqueeze(1).to_broadcast([P, DH, C]) for t in (gamma_b, beta_b))
                v1, vo = ([t[:, :, f * DH:(f + 1) * DH, :] for f in range(2)] for t in node_chunks()[2:])

            def groups(eng, body):
                def turn(i):
                    for b in range(TURN):
                        body(i, b, i * TURN + b)
                turns(eng, NT, turn, norm)

            def ahead(i, b):
                return not isinstance(i, int) or i < NT - 1 or b < TURN - 1

            def uses(i, b, n):
                return i * (TURN // n) + b // n

            with nc.Block() as block:
                @block.sync
                def _(sp):
                    ph.clear_previous(sp)

                    def load(i, b, g):
                        if reused(i, b, 2):
                            sp.wait_ge(s_sel, g - 1)
                        load_keys(sp, a, g, kr[b % 2], s_kr[b % 2])
                        sums.load(sp, i, b, g)
                        f = b % 2
                        if dense is not None and b < 2:
                            if later(i):
                                sp.wait_ge(s_nfree[f], i)
                            sp.dma_start(cur[f], v1[f][i + dense * NT]).then_inc(s_nin[f], 16)
                        if dense is not None and 2 <= b < 4 and later(i):
                            sp.wait_ge(s_ndone[f], i)
                            sp.dma_start(vo[f][i + (dense * NT - 1)], res[f]).then_inc(s_nout[f], 16)
                    groups(sp, load)
                    if dense is not None:
                        for f in range(2):
                            sp.wait_ge(s_ndone[f], NT)
                            sp.dma_start(vo[f][dense * NT + NT - 1], res[f]).then_inc(s_nout[f], 16)
                        for f in range(2):
                            sp.wait_ge(s_nout[f], 16 * NT)

                @block.scalar
                def _(act):
                    if to_table is not None:
                        view = to_table[0:E, :].rearrange("(g k p) d -> g p k d", k=G, p=P)

                    def store(i, b, g):
                        if to_table is not None:
                            act.wait_ge(s_tab, g * 2)
                            act.dma_start(view[g - 1], tb[(b - 1) % 2]).then_inc(s_st[(b - 1) % 2], 16)

                    def apply_stage(i, b, rows):
                        f, s = b % 2, b // 2 % 4
                        of, func = ((cur, ACT.Relu), (h, ACT.Identity), (res, ACT.Relu), (res, ACT.Relu))[s]
                        nln[f].apply(act, of[f], h[f], func, i * 4 + b // 2, rows)

                    def group(i, b, g):
                        for k in range(G):
                            sums.hand_on(act, i, b, g, k)
                            if norm and ahead(i, b):
                                if k == 0:
                                    ln.root(act, g + 1)
                                rows = got[(b + 1) % NB]
                                ln.apply(act, rows, rows, ACT.Relu, g + 1, range(k, k + 1))
                            if dense is not None and (b or later(i)):
                                apply_stage(i, b - 1, range(2 * k, 2 * k + 2))
                            if dense is not None and k == G - 2:
                                nln[b % 2].root(act, i * 4 + b // 2)
                            if k == 3 and reused(i, b, 1):
                                store(i, b, g)
                    if norm:
                        ln.root(act, 0)
                        ln.apply(act, got[0], got[0], ACT.Relu, 0)
                    groups(act, group)
                    sums.hand_on(act, NT, 0, NG, 0)
                    if dense is not None:
                        apply_stage(NT, -1, range(DH))
                    store(NT, 0, NG)
                    if to_table is not None:
                        for b in range(2):
                            act.wait_ge(s_st[b], 16 * (NG // 2))

                @block.gpsimd
                def _(pool):
                    passed = ph.sem("passed_pool")

                    def scatter(g, b):
                        wait_apart(pool, passed, (s_scat, g + 1))
                        for k in range(G):
                            nc.gpsimd.indirect_dma_start(
                                to_nodes, bass.IndirectOffsetOnAxis(ap=sidx[b][:, k:k + 1], axis=0),
                                tb[b][:, k, :], None, bounds_check=NP - 1, oob_is_err=False
                            ).then_inc(put_out[b].sem, 16)

                    def gather(i, b, g):
                        wait_apart(pool, passed, (s_stage, g + 1),
                                   *([sums.summed(g - (NB - 1))] if reused(i, b, NB) else []))
                        for k in range(G):
                            nc.gpsimd.indirect_dma_start(
                                got[b % NB][:, k, :], None, source,
                                bass.IndirectOffsetOnAxis(ap=gidx[b % NB][:, k:k + 1], axis=0)
                            ).then_inc(got_in[b % NB].sem, 16)
                        if to_nodes is not None and reused(i, b, 2):
                            scatter(g - 2, b % 2)
                    groups(pool, gather)
                    if to_nodes is not None:
                        for b in range(2):
                            scatter(NG - 2 + b, b)
                        for b in range(2):
                            pool.wait_ge(put_out[b].sem, put_out[b].end)

                @block.tensor
                def _(pe):
                    def sum_group(i, b, g):
                        pe.wait_ge(s_sel, g + 1)
                        if reused(i, b, NB):
                            pe.wait_ge(s_acc, g * 2 - 2 * (NB - 1))
                        if norm:
                            ln.done(pe, g)
                        else:
                            pe.wait_ge(got_in[b % NB].sem, uses(i, b, NB) * (16 * G) + (got_in[b % NB].at + 16 * G))
                        sums.add_up(pe, i, b, g, sel[b % 2], got[b % NB])
                    groups(pe, sum_group)

                @block.vector
                def _(dve):
                    def stage(g, b):
                        nc.vector.tensor_scalar(gidx[b % NB], idx[:, bass.ds(g * G, G)], 1.0, None, ALU.mult
                                                ).then_inc(s_stage, 1)

                    def post(i, b, g):
                        b2, cols = b % 2, bass.ds(g * G, G)
                        dve.wait_ge(*sums.summed(g + 1))
                        if to_table is not None:
                            if reused(i, b, 2):
                                dve.wait_ge(s_st[b2], uses(i, b, 2) * 16)
                            for c, (ps, rd) in enumerate(sums.halves(b, g, rdeg[:, a, :])):
                                nc.vector.tensor_tensor(tb[b2][:, c:G:2, :], ps, bcast(rd, C), ALU.mult
                                                        ).then_inc(s_tab, 1)
                        for ps, ac in sums.halves(b, g, acc):
                            if fresh:
                                nc.vector.tensor_scalar(ac, ps, 1.0, None, ALU.mult).then_inc(s_acc, 1)
                            else:
                                nc.vector.tensor_tensor(ac, ac, ps, ALU.add).then_inc(s_acc, 1)
                        if to_nodes is not None:
                            if reused(i, b, 2):
                                dve.wait_ge(put_out[b2].sem, uses(i, b, 2) * (16 * G) + put_out[b2].at)
                            dve.wait_ge(s_acc, g * 2 + 2)
                            nc.vector.tensor_scalar(sidx[b2], scat_idx[:, a, cols], 1.0, None, ALU.mult
                                                    ).then_inc(s_sidx, 1)
                            nc.vector.tensor_tensor(tb[b2], acc[:, cols, :], bcast(rdeg[:, a, cols], C), ALU.mult
                                                    ).then_inc(s_scat, 1)

                    def finish_chunk(i, f):
                        nln[f].done(dve, i * 4 + 3)
                        nc.vector.scalar_tensor_tensor(res[f], h[f], 0.25, res[f], ALU.mult, ALU.add
                                                       ).then_inc(s_ndone[f], 1)

                    def stage_of_chunk(i, f, s, c):
                        k = i * 4 + s
                        if s == 0:
                            if later(i):
                                finish_chunk(i - 1, f)
                            dve.wait_ge(s_nin[f], i * 16 + 16)
                            nln[f].stats(c, cur[f], k)
                            return
                        nln[f].done(dve, k - 1)
                        if s == 1:
                            nln[f].stats(c, h[f], k)
                            return
                        if s == 2:
                            c.do(nc.vector.tensor_tensor(h[f], h[f], gb, ALU.mult))
                            c.wait()
                            c.do(nc.vector.tensor_tensor(h[f], h[f], bb, ALU.add))
                            c.wait()
                            if later(i):
                                dve.wait_ge(s_nout[f], i * 16)
                            c.do(nc.vector.tensor_tensor(res[f], cur[f], h[f], ALU.add))
                            c.wait()
                            dve.sem_inc(s_nfree[f], 1)
                        else:
                            c.do(nc.vector.scalar_tensor_tensor(res[f], h[f], 0.25, res[f], ALU.mult, ALU.add))
                            c.wait()
                        nln[f].stats(c, res[f], k)

                    def rows_in(i, b):
                        dve.wait_ge(got_in[b % NB].sem, uses(i, b, NB) * (16 * G) + (got_in[b % NB].at + 16 * G))

                    def statistics(i, b, g):
                        rows_in(i, b)
                        stage(g + 2, b + 2)
                        ln.stats(Chain(dve, s_dve, g * Norm.STEPS), got[b % NB], g)
                        ln.shift(dve, g)

                    def turn(i):
                        nd = [Chain(dve, s_ndve[f], i * (4 + 4 * Norm.STEPS)) for f in range(2)]
                        for b in range(TURN):
                            g = i * TURN + b
                            dve.wait_ge(s_kr[b % 2], uses(i, b, 2) * 16 + 16)
                            if reused(i, b, 2):
                                dve.wait_ge(*sums.summed(g - 1))
                            select(a, g, kr[b % 2], sel[b % 2], s_sel)
                            if dense is not None and (b or later(i)):
                                nln[(b - 1) % 2].shift(dve, i * 4 + (b - 1) // 2)
                            if not norm:
                                rows_in(i, b)
                                stage(g + 2, b + 2)
                            elif ahead(i, b):
                                statistics(i, b + 1, g + 1)
                            if dense is not None:
                                stage_of_chunk(i, b % 2, b // 2, nd[b % 2])
                            if b:
                                post(i, b - 1, g - 1)
                            elif later(i):
                                post(i - 1, TURN - 1, g - 1)
                        if dense is not None:
                            assert all(c.n == 4 + 4 * Norm.STEPS for c in nd)

                    sums.start(dve)
                    stage(0, 0)
                    stage(1, 1)
                    if norm:
                        statistics(0, 0, 0)
                    turns(dve, NT, turn, norm)
                    if dense is not None:
                        nln[1].shift(dve, NT * 4 - 1)
                    post(NT - 1, TURN - 1, NG - 1)
                    if dense is not None:
                        for f in range(2):
                            finish_chunk(NT - 1, f)
                    dve.wait_ge(s_acc, 2 * NG)

        def node_chunks():
            return [t.rearrange("(p j c) d -> j p c d", p=P, c=DCH) for t in (x, z0, x1, out)]

        def nodes_after_first():
            ph.next()
            s_in = [ph.sem(f"n_in{b}") for b in range(4)]
            s_out = [ph.sem(f"n_out{b}") for b in range(4)]
            s_dve, s_done, s_add = (ph.sem(n) for n in ("n_dve", "n_done", "n_add"))
            cursor[0] = 0
            flat = acc[:].rearrange("p t d -> p (t d)")
            room = [flat[:, k * DCH * C:(k + 1) * DCH * C].rearrange("p (r d) -> p r d", d=C) for k in range(10)]
            cur, zz, h = room[0:4], room[4:8], room[8:10]
            ln = Norm("n", DCH)
            vx, vz, v1, _ = node_chunks()

            def chunks(eng, body):
                def turn(i):
                    for b in range(4):
                        body(i, b, i * 4 + b)
                turns(eng, NDC // 4, turn)

            with nc.Block() as block:
                @block.sync
                def _(sp):
                    ph.clear_previous(sp)

                    def load(i, b, j):
                        if later(i):
                            sp.wait_ge(s_out[b], i * 16)
                        sp.dma_start(cur[b], vx[j]).then_inc(s_in[b], 16)
                        sp.dma_start(zz[b], vz[j]).then_inc(s_in[b], 16)
                    chunks(sp, load)

                @block.vector
                def _(dve):
                    def front(i, b, j):
                        dve.wait_ge(s_in[b], i * 32 + 32)
                        ln.stats(Chain(dve, s_dve, j * Norm.STEPS), cur[b], j)
                        ln.shift(dve, j)

                    def back(b, j):
                        ln.done(dve, j)
                        nc.vector.tensor_tensor(h[b % 2], h[b % 2], zz[b], ALU.add).then_inc(s_add, 1)
                        dve.wait_ge(s_add, j + 1)
                        nc.vector.scalar_tensor_tensor(cur[b], h[b % 2], 0.25, cur[b], ALU.mult, ALU.add
                                                       ).then_inc(s_done, 1)

                    def chunk(i, b, j):
                        front(i, b, j)
                        if reused(i, b, 1):
                            back((b - 1) % 4, j - 1)
                    chunks(dve, chunk)
                    back(3, NDC - 1)

                @block.scalar
                def _(act):
                    def store(b, j):
                        act.wait_ge(s_done, j + 1)
                        act.dma_start(v1[j], cur[b]).then_inc(s_out[b], 16)

                    def chunk(i, b, j):
                        ln.root(act, j)
                        if reused(i, b, 2):
                            act.wait_ge(s_done, j - 1)
                        ln.apply(act, cur[b], h[b % 2], ACT.Relu, j)
                        if reused(i, b, 1):
                            store((b - 1) % 4, j - 1)
                    chunks(act, chunk)
                    store(3, NDC - 1)
                    for b in range(4):
                        act.wait_ge(s_out[b], 16 * (NDC // 4))

        def mlp_layer():
            ph.next()
            s_kr = [ph.sem(f"m_kr{b}") for b in range(2)]
            s_fe = [ph.sem(f"m_fe{b}") for b in range(2)]
            s_st = [ph.sem(f"m_st{b}") for b in range(2)]
            got_in = [ph.landed(f"got{b}", 16 * 2 * G * NT) for b in range(TURN)]
            (s_w, s_dve, s_dve_out, s_fin, s_stage, s_sel, s_h, s_turn, s_ht, s_z, s_zb, s_hid, s_xt, s_msg, s_o, s_out,
             s_zero, s_b2) = (ph.sem("m_" + n) for n in (
                 "w", "dve", "dve_out", "fin", "stage", "sel", "h", "turn", "ht", "z", "zb", "hid", "xt", "msg", "o",
                 "out", "zero", "b2"))
            cursor[0] = 0
            w1, w2, b1, b2 = take(P, parts=C), take(C), take(1), take(C)
            gidx = [take(2, G, dt=I32) for _ in range(4)]
            kr = [take(G, P) for _ in range(2)]
            fe = [take(G, C) for _ in range(2)]
            msg = [take(G, C) for _ in range(2)]
            ht = take(2, GC, parts=C)
            zb = take(2, GC)
            hid = take(G * P)
            o = [take(G, C) for _ in range(2)]
            flat = acc[:].rearrange("p t d -> p (t d)")

            def room(k, width):
                return flat[:, k * 2 * GC:(k + 1) * 2 * GC].rearrange("p (r d) -> p r d", d=width)
            got = [room(k, C) for k in range(TURN)]
            h = [room(TURN + k, C) for k in range(4)]
            sel = [room(TURN + 4 + k, P) for k in range(4)]
            sums = Sums("m", 1, [(5, 6)])
            ln_in, ln_out = Norm("mi", 2 * G), Norm("mo", G)
            xt = bank[4]
            gb, bb = (t[:].unsqueeze(1).to_broadcast([P, G, C]) for t in (gamma_b, beta_b))
            fview = d_rec.rearrange("(g k p) f -> g p k f", k=G, p=P)
            oview = xd.rearrange("(g k p) f -> g p k f", k=G, p=P)

            def slots(eng, body):
                def turn(i):
                    for b in range(TURN):
                        body(i, b, i * TURN + b)
                turns(eng, NT, turn)
                for b in range(3):
                    body(NT, b, NG + b)

            def age(i, b, n):
                return reused(i, b, n) if not isinstance(i, int) or i < NT else n > b

            with nc.Block() as block:
                @block.sync
                def _(sp):
                    ph.clear_previous(sp)
                    sp.dma_start(w1, w1n).then_inc(s_w, 16)
                    sp.dma_start(w2, w2n).then_inc(s_w, 16)
                    sp.dma_start(b1, b1n.unsqueeze(1)).then_inc(s_w, 16)
                    sp.dma_start(b2, b2n.unsqueeze(0).to_broadcast([P, C])).then_inc(s_w, 16)

                    def load(i, b, g):
                        if reused(i, b, 2):
                            sp.wait_ge(s_sel, g - 1)
                        load_keys(sp, 1, g, kr[b % 2], s_kr[b % 2])
                        sums.load(sp, i, b, g)
                        if reused(i, b, 2):
                            sp.wait_ge(s_msg, g - 1)
                        sp.dma_start(fe[b % 2], fview[g][:, :, 8:DW]).then_inc(s_fe[b % 2], 16)

                    def turn(i):
                        for b in range(TURN):
                            load(i, b, i * TURN + b)
                    turns(sp, NT, turn)

                @block.gpsimd
                def _(pool):
                    def gather(i, b, g):
                        wait_apart(pool, ph.sem("passed_pool"), (s_stage, g + 1),
                                   *([(s_out, g - (TURN - 1))] if later(i) else []))
                        for r in range(2):
                            for k in range(G):
                                nc.gpsimd.indirect_dma_start(
                                    got[b][:, r * G + k, :], None, x1,
                                    bass.IndirectOffsetOnAxis(ap=gidx[b % 4][:, r, k:k + 1], axis=0)
                                ).then_inc(got_in[b].sem, 16)

                    def turn(i):
                        for b in range(TURN):
                            gather(i, b, i * TURN + b)
                    turns(pool, NT, turn)

                @block.tensor
                def _(pe):
                    pe.wait_ge(s_w, 64)

                    def first(i, b, g):
                        wait_apart(pe, ph.sem("passed_pe"), (s_h, g + 1), *([(s_ht, g)] if reused(i, b, 1) else []))
                        for k in range(G):
                            half = bank[k // 4][0:C, (k % 4) * P:(k % 4 + 1) * P]
                            mm = nc.tensor.transpose(half, h[b % 4][:, k, :], ident[:])
                        mm.then_inc(s_turn, 1)
                        pe.wait_ge(s_ht, g + 1)
                        if reused(i, b, 1):
                            pe.wait_ge(s_zb, g)
                        for r in range(2):
                            mm = nc.tensor.matmul(bank[2 + r][:, 0:GC], w1, ht[:, r, :], start=True, stop=True)
                        mm.then_inc(s_z, 1)

                    def second(i, b, g):
                        pe.wait_ge(s_hid, g + 1)
                        if reused(i, b, 1):
                            pe.wait_ge(s_msg, g)
                        for k in range(G):
                            mm = nc.tensor.matmul(xt[:, k * C:(k + 1) * C], hid[:, k * P:(k + 1) * P], w2,
                                                  start=True, stop=True)
                        mm.then_inc(s_xt, 1)

                    def add_up(i, b, g):
                        pe.wait_ge(s_msg, g + 1)
                        if reused(i, b, 1):
                            pe.wait_ge(s_o, g * 2)
                        sums.add_up(pe, i, b, g, sel[b % 4], msg[b % 2])

                    def slot(i, b, g):
                        if age(i, b, 1):
                            second(i, b - 1, g - 1)
                        if age(i, b, 0):
                            first(i, b, g)
                        if age(i, b, 1):
                            add_up(i, b - 1, g - 1)
                    slots(pe, slot)

                @block.scalar
                def _(act):
                    act.wait_ge(s_w, 64)

                    def first(i, b, g):
                        ln_in.root(act, g)
                        if reused(i, b, 4):
                            act.wait_ge(s_o, g * 2 - 6)
                        ln_in.apply(act, got[b % TURN], h[b % 4], ACT.Relu, g, range(G)).then_inc(s_h, 1)
                        ln_in.apply(act, got[b % TURN], h[b % 4], ACT.Relu, g, range(G, 2 * G))
                        act.wait_ge(s_turn, g + 1)
                        if reused(i, b, 1):
                            act.wait_ge(s_z, g)
                        fl = ht.rearrange("p r e -> p (r e)")
                        nc.scalar.activation(fl[:, 0:4 * P], bank[0][0:C, :], ACT.Copy)
                        nc.scalar.activation(fl[:, 4 * P:G * P], bank[1][0:C, 0:3 * P], ACT.Copy).then_inc(s_ht, 1)
                        act.wait_ge(s_z, g + 1)
                        if reused(i, b, 1):
                            act.wait_ge(s_hid, g)
                        for r in range(2):
                            ins = nc.scalar.activation(zb[:, r, :], bank[2 + r][:, 0:GC], ACT.Identity, bias=b1)
                        ins.then_inc(s_zb, 1)

                    def slot(i, b, g):
                        if age(i, b, 0):
                            first(i, b, g)
                        for k in range(G):
                            if age(i, b, 1) and k:
                                sums.hand_on(act, i, b - 1, g - 1, k)
                            if k == 2 and age(i, b, 2):
                                ln_out.root(act, g - 2)
                            if k == G - 1 and age(i, b, 1):
                                sums.hand_on(act, i, b - 1, g - 1, G)
                            if k >= 3 and age(i, b, 2):
                                ln_out.apply(act, o[b % 2], o[b % 2], ACT.Identity, g - 2,
                                             range(2 * (k - 3), min(2 * (k - 2), G)))
                        if age(i, b, 3):
                            act.wait_ge(s_out, g - 2)
                            act.dma_start(oview[g - 3], o[(b - 3) % 2]).then_inc(s_st[(b - 3) % 2], 16)
                    slots(act, slot)
                    for b in range(2):
                        act.wait_ge(s_st[b], 16 * (NG // 2))

                @block.vector
                def _(dve):
                    def stage(g, b):
                        cols = bass.ds(g * G, G)
                        nc.vector.tensor_scalar(gidx[b % 4][:, 0, :], src_idx[:, cols], 1.0, None, ALU.mult
                                                ).then_inc(s_zero, 1)
                        nc.vector.tensor_scalar(gidx[b % 4][:, 1, :], dst_idx[:, cols], 1.0, None, ALU.mult
                                                ).then_inc(s_stage, 1)

                    def first(i, b, g):
                        dve.wait_ge(s_kr[b % 2], i * (16 * TURN // 2) + (b // 2 * 16 + 16))
                        if reused(i, b, 4):
                            dve.wait_ge(*sums.summed(g - 3))
                        select(1, g, kr[b % 2], sel[b % 4], s_sel)
                        dve.wait_ge(got_in[b].sem, i * (32 * G) + (got_in[b].at + 32 * G))
                        ln_in.stats(Chain(dve, s_dve, g * Norm.STEPS), got[b], g)
                        stage(g + 2, b + 2)

                    def second(i, b, g):
                        dve.wait_ge(s_zb, g + 1)
                        if reused(i, b, 1):
                            dve.wait_ge(s_xt, g)
                        zf = zb.rearrange("p r e -> p (r e)")
                        nc.vector.scalar_tensor_tensor(hid, zf, SLOPE, zf, ALU.mult, ALU.max).then_inc(s_hid, 1)

                    def messages(i, b, g):
                        dve.wait_ge(s_xt, g + 1)
                        nc.vector.tensor_tensor(msg[b % 2], xt[:, 0:GC].rearrange("p (k d) -> p k d", k=G),
                                                b2.unsqueeze(1).to_broadcast([P, G, C]), ALU.add).then_inc(s_b2, 1)
                        dve.wait_ge(s_b2, g + 1)
                        dve.wait_ge(s_fe[b % 2], i * (16 * TURN // 2) + (b // 2 * 16 + 16))
                        nc.vector.tensor_tensor(msg[b % 2], msg[b % 2], fe[b % 2], ALU.mult).then_inc(s_msg, 1)

                    def third(i, b, g):
                        if reused(i, b, 2):
                            dve.wait_ge(s_st[b % 2], i * (16 * TURN // 2) + b // 2 * 16)
                        dve.wait_ge(*sums.summed(g + 1))
                        for ps, to, own in sums.halves(b, None, o[b % 2], h[b % 4][:, G:2 * G, :]):
                            nc.vector.scalar_tensor_tensor(to, ps, res_col[:], own, ALU.mult, ALU.add).then_inc(s_o, 1)
                        dve.wait_ge(s_o, g * 2 + 2)
                        ln_out.stats(Chain(dve, s_dve_out, g * Norm.STEPS), o[b % 2], g)

                    def finish(i, b, g):
                        ln_out.done(dve, g)
                        c = Chain(dve, s_fin, g * 2)
                        c.do(nc.vector.tensor_tensor(o[b % 2], o[b % 2], gb, ALU.mult))
                        c.wait()
                        c.do(nc.vector.tensor_tensor(o[b % 2], o[b % 2], bb, ALU.add))
                        c.wait()
                        nc.vector.tensor_tensor(o[b % 2], o[b % 2], got[b % TURN][:, G:2 * G, :], ALU.add
                                                ).then_inc(s_out, 1)

                    def slot(i, b, g):
                        if age(i, b, 0):
                            first(i, b, g)
                        if age(i, b, 1):
                            second(i, b - 1, g - 1)
                        if age(i, b, 0):
                            ln_in.shift(dve, g)
                        if age(i, b, 3):
                            finish(i, b - 3, g - 3)
                        if age(i, b, 2):
                            third(i, b - 2, g - 2)
                        if age(i, b, 1):
                            messages(i, b - 1, g - 1)
                        if age(i, b, 2):
                            ln_out.shift(dve, g - 2)

                    sums.start(dve)
                    dve.wait_ge(s_w, 64)
                    stage(0, 0)
                    stage(1, 1)
                    slots(dve, slot)
                    dve.wait_ge(s_out, NG)

        DG = 2 * G
        ND = T // DG

        def between(update, final):
            ph.next()
            s_in = [ph.sem(f"b_in{b}") for b in range(4)]
            s_dve, s_cols, s_h, s_done = (ph.sem("b_" + n) for n in ("dve", "cols", "h", "done"))
            cursor[0] = 0
            cur = [take(DG, C) for _ in range(4)]
            y = [take(DG, C) for _ in range(4)]
            h = [take(DG, C) for _ in range(2)]
            isq, sqd, qsq = take(T), take(T), take(T)
            sidx = [take(DG, dt=I32) for _ in range(4)]
            ln = Norm("b", DG)
            vx = xd.rearrange("(g k p) d -> g p k d", k=DG, p=P)
            vt = table[0][0:E, :].rearrange("(g k p) d -> g p k d", k=DG, p=P)
            per = (2 if update else 0) + (0 if final else Norm.STEPS)
            stores = 16 * DG if final else 32 if update else 16
            put_out = [ph.landed(f"put{b}", stores * (ND // 4) if final else 0) for b in range(4)]
            s_st = [p.sem if final else ph.sem(f"b_st{b}") for b, p in enumerate(put_out)]
            at = [p.at if final else 0 for p in put_out]

            def groups(eng, body):
                def turn(i):
                    for b in range(4):
                        body(i, b, i * 4 + b)
                turns(eng, ND // 4, turn)

            with nc.Block() as block:
                @block.sync
                def _(sp):
                    ph.clear_previous(sp)

                    def load(i, b, g):
                        if later(i):
                            sp.wait_ge(s_st[b], i * stores + at[b])
                        sp.dma_start(cur[b], vx[g]).then_inc(s_in[b], 16)
                    groups(sp, load)

                @block.vector
                def _(dve):
                    dve.wait_ge(s_cols, 1)
                    nc.vector.reciprocal(sqd, isq).then_inc(s_cols, 1)
                    nc.vector.tensor_scalar(qsq, isq, 0.25, None, ALU.mult).then_inc(s_cols, 1)
                    dve.wait_ge(s_cols, 3)

                    def front(i, b, g):
                        c = Chain(dve, s_dve, g * per)
                        cols = bass.ds(g * DG, DG)
                        dve.wait_ge(s_in[b], i * 16 + 16)
                        if update:
                            if reused(i, b, 2):
                                dve.wait_ge(s_done, g - 1)
                            if final and later(i):
                                dve.wait_ge(s_st[b], i * stores + at[b])
                            c.do(nc.vector.tensor_tensor(h[b % 2], acc[:, cols, :], bcast(qsq[:, cols], C), ALU.mult))
                            if final:
                                c.do(nc.vector.tensor_scalar(sidx[b], scat_idx[:, 1, cols], 1.0, None, ALU.mult))
                                c.wait()
                                nc.vector.tensor_tensor(cur[b], cur[b], h[b % 2], ALU.add).then_inc(s_done, 1)
                                return
                            c.wait()
                            c.do(nc.vector.tensor_tensor(cur[b], cur[b], h[b % 2], ALU.add))
                            c.wait()
                        ln.stats(c, cur[b], g)
                        ln.shift(dve, g)

                    def back(b, g):
                        cols = bass.ds(g * DG, DG)
                        ln.done(dve, g)
                        nc.vector.tensor_tensor(acc[:, cols, :], h[b % 2], bcast(sqd[:, cols], C), ALU.mult
                                                ).then_inc(s_h, 1)
                        nc.vector.tensor_tensor(y[b], h[b % 2], bcast(isq[:, cols], C), ALU.mult
                                                ).then_inc(s_done, 1)

                    def group(i, b, g):
                        front(i, b, g)
                        if not final and reused(i, b, 1):
                            back((b - 1) % 4, g - 1)
                    groups(dve, group)
                    if not final:
                        back(3, ND - 1)
                    dve.wait_ge(s_done, ND)

                @block.scalar
                def _(act):
                    nc.scalar.activation(isq, rdeg[:, 1, :], ACT.Sqrt).then_inc(s_cols, 1)

                    def store(b, g):
                        act.wait_ge(s_done, g + 1)
                        act.dma_start(vt[g], y[b]).then_inc(s_st[b], 16)
                        if update:
                            act.dma_start(vx[g], cur[b]).then_inc(s_st[b], 16)

                    def group(i, b, g):
                        ln.root(act, g)
                        if reused(i, b, 2):
                            act.wait_ge(s_done, g - 1)
                        ln.apply(act, cur[b], h[b % 2], ACT.Relu, g)
                        if reused(i, b, 1):
                            store((b - 1) % 4, g - 1)
                    if not final:
                        groups(act, group)
                        store(3, ND - 1)
                        for b in range(4):
                            act.wait_ge(s_st[b], stores * (ND // 4))

                if final:
                    @block.gpsimd
                    def _(pool):
                        def scatter(i, b, g):
                            wait_apart(pool, ph.sem("passed_pool"), (s_done, g + 1))
                            for k in range(DG):
                                nc.gpsimd.indirect_dma_start(
                                    out, bass.IndirectOffsetOnAxis(ap=sidx[b][:, k:k + 1], axis=0),
                                    cur[b][:, k, :], None, bounds_check=NP - 1, oob_is_err=False).then_inc(s_st[b], 16)
                        groups(pool, scatter)
                        for b in range(4):
                            pool.wait_ge(s_st[b], put_out[b].end)

        keys()
        ranks()
        offsets()
        records()
        columns()
        hop(0, x, hop1_idx, norm=True, fresh=True, to_table=table[0])
        hop(0, table[0], end_idx[:, 0, :], to_table=table[1])
        hop(0, table[1], end_idx[:, 0, :], to_nodes=z0)
        nodes_after_first()
        mlp_layer()
        for layer in (2, 3):
            between(layer == 3, False)
            hop(1, table[0], end_idx[:, 1, :], to_table=table[1], dense=0 if layer == 2 else 3)
            hop(1, table[1], end_idx[:, 1, :], to_table=table[0], dense=1 if layer == 2 else None)
            hop(1, table[0], end_idx[:, 1, :], dense=2 if layer == 2 else None)
        between(True, True)


def kernel(x, src, dst, edge_attr_32, L1_gnn_W1n, L1_gnn_b1n, L1_gnn_W2n, L1_gnn_b2n, L1_gnn_W1e, L1_gnn_b1e,
           L1_gnn_W2e, L1_gnn_b2e, L1_gnn_res_w, L1_gnn_dp_scale, L1_gnn_gamma, L1_gnn_beta):
    import numpy as np
    import concourse.bacc as bacc
    from concourse.bass_utils import run_bass_kernel_spmd

    def padded(a, n, fill):
        more = np.full((n - a.shape[0],) + a.shape[1:], fill, a.dtype)
        return np.concatenate([np.asarray(a), more], axis=0)

    arrays = {
        "x": padded(x, NP, 0),
        "src": padded(src, E, PADKEY),
        "dst": padded(dst, E, PADKEY),
        "attr_t": np.ascontiguousarray(padded(edge_attr_32, E, 0).T),
        "w1n": L1_gnn_W1n, "b1n": L1_gnn_b1n, "w2n": L1_gnn_W2n, "b2n": L1_gnn_b2n,
        "w1e": L1_gnn_W1e, "b1e": L1_gnn_b1e, "w2e": L1_gnn_W2e, "b2e": L1_gnn_b2e,
        "res_w": L1_gnn_res_w, "dp_scale": L1_gnn_dp_scale, "gamma": L1_gnn_gamma, "beta": L1_gnn_beta,
    }
    arrays = {f"in_{n}": np.ascontiguousarray(a) for n, a in arrays.items()}
    nc = bacc.Bacc("TRN2", target_bir_lowering=False, num_devices=1)
    args = [nc.dram_tensor(n, a.shape, mybir.dt.from_np(a.dtype), kind="ExternalInput").ap() for n, a in arrays.items()]
    args.append(nc.dram_tensor("nodes_out", (NP, C), F32, kind="ExternalOutput").ap())
    program(nc, *args)
    r = run_bass_kernel_spmd(nc, [arrays], core_ids=[0])
    return r.results[0]["nodes_out"][:N]
```
